# Optimizing a Trainium2 kernel written in Bass

```python
import numpy as np
import jax
import jax.numpy as jnp

def _softmax(x, axis=-1):
    return jax.nn.softmax(x, axis=axis)

def _gelu(x):
    return jax.nn.gelu(x, approximate=True)

def _silu(x):
    return jax.nn.silu(x)

def _sigmoid(x):
    return jax.nn.sigmoid(x)

def _layernorm(x, axis=-1, eps=1e-05):
    m = jnp.mean(x, axis=axis, keepdims=True)
    v = jnp.var(x, axis=axis, keepdims=True)
    return (x - m) / jnp.sqrt(v + eps)

def _scatter_add(tgt, idx, src, axis=0):
    return tgt.at[idx].add(src)

def _segment_sum(src, seg, n):
    return jax.ops.segment_sum(src, seg, n)
kernel_name = 'mk_gnn_resnorm_d2_gnn_r32_4327f5'

def setup_inputs(seed: int=0):
    np.random.seed(seed)
    _w = jnp.asarray

    def _rec_inputs():
        import jax
        import jax.numpy as jnp
        _gk = jax.random.key(seed)
        x = -0.000202 + 1 * jax.random.normal(jax.random.fold_in(_gk, 1), (50000, 128), jnp.float32)
        src = jax.random.randint(jax.random.fold_in(_gk, 2), (50000,), 0, 50000, jnp.int32)
        dst = jnp.minimum((50000 * jax.random.uniform(jax.random.fold_in(_gk, 3), (50000,)) ** 2.0).astype(jnp.int32), 49999)
        _o = jnp.argsort(dst, stable=True)
        src = src[_o]
        dst = dst[_o]
        return (x, src, dst)
    x, src, dst = _rec_inputs()

    def _L0_gnn_setup():
        import jax, jax.numpy as jnp
        import numpy as np
        N_NODES = 50000
        N_EDGES = 25000
        D = 128
        H = 128
        U = 256

        def _propagate(node_states, fi, ti, W1, b1, W2, b2):
            edge_inputs = jnp.concatenate([node_states[fi], node_states[ti]], axis=-1)
            h = jax.nn.relu(edge_inputs @ W1 + b1)
            messages = h @ W2 + b2
            return jax.ops.segment_sum(messages, ti, num_segments=node_states.shape[0])
        key = jax.random.key(seed)
        ks = jax.random.split(key, 16)
        s = 0.1
        inp = {'node_states': jax.random.normal(ks[0], (N_NODES, D), jnp.float32), 'from_idx': jax.random.randint(ks[1], (N_EDGES,), 0, N_NODES, jnp.int64), 'to_idx': jax.random.randint(ks[2], (N_EDGES,), 0, N_NODES, jnp.int64), 'msg_W1': jax.random.normal(ks[3], (2 * D, H), jnp.float32) * s / np.sqrt(2 * D), 'msg_b1': jnp.zeros((H,), jnp.float32), 'msg_W2': jax.random.normal(ks[4], (H, H), jnp.float32) * s / np.sqrt(H), 'msg_b2': jnp.zeros((H,), jnp.float32), 'rev_W1': jax.random.normal(ks[5], (2 * D, H), jnp.float32) * s / np.sqrt(2 * D), 'rev_b1': jnp.zeros((H,), jnp.float32), 'rev_W2': jax.random.normal(ks[6], (H, H), jnp.float32) * s / np.sqrt(H), 'rev_b2': jnp.zeros((H,), jnp.float32), 'upd_W1': jax.random.normal(ks[7], (D + H, U), jnp.float32) / np.sqrt(D + H), 'upd_b1': jnp.zeros((U,), jnp.float32), 'upd_W2': jax.random.normal(ks[8], (U, D), jnp.float32) * 0.02, 'upd_b2': jnp.zeros((D,), jnp.float32)}
        return inp
    _L0_gnn_all = _L0_gnn_setup()
    _L0_gnn_in = {k: v for k, v in _L0_gnn_all.items() if k in ('msg_W1', 'msg_b1', 'msg_W2', 'msg_b2', 'rev_W1', 'rev_b1', 'rev_W2', 'rev_b2', 'upd_W1', 'upd_b1', 'upd_W2', 'upd_b2')}
    del _L0_gnn_all

    def _L1_gnn_setup():
        import jax, jax.numpy as jnp
        import numpy as np
        N = 10000
        E = 10000
        D = 128
        H = 4
        L = 3
        NEG_SLOPE = 0.2

        def gat_conv(x, src, dst, W_l, a_src, a_dst, b_l):
            n = x.shape[0]
            h = (x @ W_l).reshape(n, H, -1)
            alpha_s = (h * a_src).sum(-1)
            alpha_d = (h * a_dst).sum(-1)
            e = jax.nn.leaky_relu(alpha_s[src] + alpha_d[dst], NEG_SLOPE)
            m = jax.ops.segment_max(e, dst, num_segments=n)
            ex = jnp.exp(e - m[dst])
            den = jax.ops.segment_sum(ex, dst, num_segments=n)
            alpha = ex / den[dst]
            msg = alpha[:, :, None] * h[src]
            out = jax.ops.segment_sum(msg, dst, num_segments=n)
            return out.mean(axis=1) + b_l
        key = jax.random.key(seed)
        ks = jax.random.split(key, 8)
        return {'x': jax.random.normal(ks[0], (N, D), dtype=jnp.float32), 'edge_index': jax.random.randint(ks[1], (2, E), 0, N, dtype=jnp.int64), 'W': jax.random.normal(ks[2], (L, D, H * D), dtype=jnp.float32) * 0.05, 'att_src': jax.random.normal(ks[3], (L, H, D), dtype=jnp.float32) * 0.05, 'att_dst': jax.random.normal(ks[4], (L, H, D), dtype=jnp.float32) * 0.05, 'bias': jax.random.normal(ks[5], (L, D), dtype=jnp.float32) * 0.05, 'skip_W': jax.random.normal(ks[6], (L, D, D), dtype=jnp.float32) * 0.05, 'skip_b': jax.random.normal(ks[7], (L, D), dtype=jnp.float32) * 0.05}
    _L1_gnn_all = _L1_gnn_setup()
    _L1_gnn_in = {k: v for k, v in _L1_gnn_all.items() if k in ('W', 'att_src', 'att_dst', 'bias', 'skip_W', 'skip_b')}
    del _L1_gnn_all
    return {'x': x, 'src': src, 'dst': dst, 'L0_gnn_msg_W1': _L0_gnn_in['msg_W1'], 'L0_gnn_msg_b1': _L0_gnn_in['msg_b1'], 'L0_gnn_msg_W2': _L0_gnn_in['msg_W2'], 'L0_gnn_msg_b2': _L0_gnn_in['msg_b2'], 'L0_gnn_rev_W1': _L0_gnn_in['rev_W1'], 'L0_gnn_rev_b1': _L0_gnn_in['rev_b1'], 'L0_gnn_rev_W2': _L0_gnn_in['rev_W2'], 'L0_gnn_rev_b2': _L0_gnn_in['rev_b2'], 'L0_gnn_upd_W1': _L0_gnn_in['upd_W1'], 'L0_gnn_upd_b1': _L0_gnn_in['upd_b1'], 'L0_gnn_upd_W2': _L0_gnn_in['upd_W2'], 'L0_gnn_upd_b2': _L0_gnn_in['upd_b2'], 'L1_gnn_W': _L1_gnn_in['W'], 'L1_gnn_att_src': _L1_gnn_in['att_src'], 'L1_gnn_att_dst': _L1_gnn_in['att_dst'], 'L1_gnn_bias': _L1_gnn_in['bias'], 'L1_gnn_skip_W': _L1_gnn_in['skip_W'], 'L1_gnn_skip_b': _L1_gnn_in['skip_b']}

def reference(x, src, dst, L0_gnn_msg_W1, L0_gnn_msg_b1, L0_gnn_msg_W2, L0_gnn_msg_b2, L0_gnn_rev_W1, L0_gnn_rev_b1, L0_gnn_rev_W2, L0_gnn_rev_b2, L0_gnn_upd_W1, L0_gnn_upd_b1, L0_gnn_upd_W2, L0_gnn_upd_b2, L1_gnn_W, L1_gnn_att_src, L1_gnn_att_dst, L1_gnn_bias, L1_gnn_skip_W, L1_gnn_skip_b):
    import jax
    import jax.numpy as jnp

    def _L0_gnn_ref(node_states, from_idx, to_idx, msg_W1, msg_b1, msg_W2, msg_b2, rev_W1, rev_b1, rev_W2, rev_b2, upd_W1, upd_b1, upd_W2, upd_b2):
        import jax, jax.numpy as jnp
        import numpy as np
        N_NODES = 50000
        N_EDGES = 25000
        D = 128
        H = 128
        U = 256

        def _propagate(node_states, fi, ti, W1, b1, W2, b2):
            edge_inputs = jnp.concatenate([node_states[fi], node_states[ti]], axis=-1)
            h = jax.nn.relu(edge_inputs @ W1 + b1)
            messages = h @ W2 + b2
            return jax.ops.segment_sum(messages, ti, num_segments=node_states.shape[0])
        agg = _propagate(node_states, from_idx, to_idx, msg_W1, msg_b1, msg_W2, msg_b2)
        agg = agg + _propagate(node_states, to_idx, from_idx, rev_W1, rev_b1, rev_W2, rev_b2)
        upd_in = jnp.concatenate([agg, node_states], axis=-1)
        h = jax.nn.relu(upd_in @ upd_W1 + upd_b1)
        mlp_out = h @ upd_W2 + upd_b2
        return node_states + mlp_out

    def _L1_gnn_ref(x, edge_index, W, att_src, att_dst, bias, skip_W, skip_b):
        import jax, jax.numpy as jnp
        import numpy as np
        N = 10000
        E = 10000
        D = 128
        H = 4
        L = 3
        NEG_SLOPE = 0.2

        def gat_conv(x, src, dst, W_l, a_src, a_dst, b_l):
            n = x.shape[0]
            h = (x @ W_l).reshape(n, H, -1)
            alpha_s = (h * a_src).sum(-1)
            alpha_d = (h * a_dst).sum(-1)
            e = jax.nn.leaky_relu(alpha_s[src] + alpha_d[dst], NEG_SLOPE)
            m = jax.ops.segment_max(e, dst, num_segments=n)
            ex = jnp.exp(e - m[dst])
            den = jax.ops.segment_sum(ex, dst, num_segments=n)
            alpha = ex / den[dst]
            msg = alpha[:, :, None] * h[src]
            out = jax.ops.segment_sum(msg, dst, num_segments=n)
            return out.mean(axis=1) + b_l
        n = x.shape[0]
        loops = jnp.arange(n, dtype=edge_index.dtype)
        src = jnp.concatenate([edge_index[0], loops])
        dst = jnp.concatenate([edge_index[1], loops])
        for i in range(L):
            y = gat_conv(x, src, dst, W[i], att_src[i], att_dst[i], bias[i])
            x = y + y @ skip_W[i] + skip_b[i]
            if i != L - 1:
                x = jax.nn.relu(x)
        return x
    edge_index = jnp.stack([src, dst])
    x = _layernorm(x + _L0_gnn_ref(x, src, dst, L0_gnn_msg_W1, L0_gnn_msg_b1, L0_gnn_msg_W2, L0_gnn_msg_b2, L0_gnn_rev_W1, L0_gnn_rev_b1, L0_gnn_rev_W2, L0_gnn_rev_b2, L0_gnn_upd_W1, L0_gnn_upd_b1, L0_gnn_upd_W2, L0_gnn_upd_b2), axis=-1)
    x = _layernorm(x + _L1_gnn_ref(x, edge_index, L1_gnn_W, L1_gnn_att_src, L1_gnn_att_dst, L1_gnn_bias, L1_gnn_skip_W, L1_gnn_skip_b), axis=-1)
    return x

_drawn_inputs = setup_inputs


def setup_inputs(seed=0):
    import zlib

    import numpy as np

    out = dict(_drawn_inputs(seed))
    spreads = {'L0_gnn_msg_b1': (0.0, 0.8),
     'L0_gnn_msg_b2': (0.0, 0.618),
     'L0_gnn_rev_b1': (0.0, 0.8),
     'L0_gnn_rev_b2': (0.0, 0.659),
     'L0_gnn_upd_b1': (0.0, 0.734),
     'L0_gnn_upd_b2': (0.0, 0.1)}
    factors = {'L0_gnn_msg_W1': 8.0,
     'L0_gnn_msg_W2': 8.0,
     'L0_gnn_rev_W1': 8.0,
     'L0_gnn_rev_W2': 8.0,
     'L1_gnn_att_src': 8.0,
     'L1_gnn_att_dst': 8.0}
    for name, (base, spread) in spreads.items():
        noise = np.random.default_rng([zlib.crc32(name.encode()), seed]).standard_normal(out[name].shape)
        drawn = base * np.exp(spread * noise) if base else spread * noise
        out[name] = jnp.asarray(drawn.astype(out[name].dtype))
    for name, factor in factors.items():
        out[name] = (out[name] * factor).astype(out[name].dtype)
    return out
```

```python
from collections import namedtuple
from contextlib import ExitStack, contextmanager

import concourse.bass as bass
from concourse import mybir

ALU = mybir.AluOpType
ACT = mybir.ActivationFunctionType
AX = mybir.AxisListType
F32 = mybir.dt.float32
BF16 = mybir.dt.bfloat16
I32 = mybir.dt.int32

P = 128
N = 50000
E = 50000
D = 128
U = 256
HEADS = 4
LAYERS = 3
T = -(-E // (P * 8)) * 8
SLOTS = P * T
HALVES = T // 4
ITERS = T // 8
W = 136
SIDE = SLOTS
ROWS = SLOTS + P
SKIP = float(1 << 20)
BLOCK = 512
NBLOCKS = -(-N // BLOCK)
BIG = 1.0e30
EPS = 1e-05
SLOPE = 0.2


@contextmanager
def phase(nc, name, *signals):
    sems = namedtuple("Signals", signals)(*[nc.alloc_semaphore(f"{name}_{s}") for s in signals])
    with nc.Block() as block:
        yield block, sems
    nc.clear_and_free_semaphores(list(sems))
    nc.all_engine_barrier()


class Buffers:
    pass


class Steps:

    def __init__(self, eng, sem, start=0):
        self.eng, self.sem, self.n = eng, sem, start

    def then(self, ins):
        ins.then_inc(self.sem, 1)
        self.n = self.n + 1

    def wait(self):
        self.eng.wait_ge(self.sem, self.n)


def hold(eng, passed):
    eng.sem_inc(passed, 1)


def row_of(v):
    return v.rearrange("(a d) -> a d", a=1)


def make_constants(nc, s):
    with phase(nc, "const", "filled", "made") as (block, q):
        @block.gpsimd
        def _(pool):
            nc.gpsimd.memset(s.ident[:, :], 0.0).then_inc(q.filled, 1)
            nc.gpsimd.memset(s.lower[:, :], 1.0).then_inc(q.filled, 1)
            nc.gpsimd.memset(s.upper[:, :], 1.0).then_inc(q.filled, 1)
            nc.gpsimd.memset(s.upper_in[:, :], 1.0).then_inc(q.filled, 1)
            nc.gpsimd.memset(s.lower_in[:, :], 1.0).then_inc(q.filled, 1)
            nc.gpsimd.memset(s.ones[:, :], 1.0).then_inc(q.filled, 1)
            nc.gpsimd.memset(s.eps[:, :], EPS)
            nc.gpsimd.iota(s.iota256[:, :], [[1, 256]], base=0, channel_multiplier=0,
                           allow_small_or_imprecise_dtypes=True).then_inc(q.filled, 1)
            nc.gpsimd.iota(s.dummy[:, :], [[0, 1]], base=SIDE, channel_multiplier=1,
                           allow_small_or_imprecise_dtypes=True).then_inc(q.filled, 1)
            pool.wait_ge(q.filled, 8)
            nc.gpsimd.affine_select(out=s.ident[:, :], in_=s.ident[:, :], compare_op=ALU.not_equal, fill=1.0,
                                    base=0, pattern=[[-1, P]], channel_multiplier=1).then_inc(q.made, 1)
            nc.gpsimd.affine_select(out=s.lower[:, :], in_=s.lower[:, :], compare_op=ALU.is_gt, fill=0.0,
                                    base=0, pattern=[[-1, P]], channel_multiplier=1).then_inc(q.made, 1)
            nc.gpsimd.affine_select(out=s.upper[:, :], in_=s.upper[:, :], compare_op=ALU.is_gt, fill=0.0,
                                    base=0, pattern=[[1, P]], channel_multiplier=-1).then_inc(q.made, 1)
            nc.gpsimd.affine_select(out=s.upper_in[:, :], in_=s.upper_in[:, :], compare_op=ALU.is_ge, fill=0.0,
                                    base=0, pattern=[[1, P]], channel_multiplier=-1).then_inc(q.made, 1)
            nc.gpsimd.affine_select(out=s.lower_in[:, :], in_=s.lower_in[:, :], compare_op=ALU.is_ge, fill=0.0,
                                    base=0, pattern=[[-1, P]], channel_multiplier=1).then_inc(q.made, 1)

        @block.vector
        def _(dve):
            dve.wait_ge(q.made, 5)
            nc.vector.tensor_copy(s.upper_b[:, :], s.upper[:, :])
            nc.vector.tensor_copy(s.lower_in_b[:, :], s.lower_in[:, :])
            nc.vector.tensor_copy(s.ones_b[:, :], s.ones[:, :])
            nc.vector.tensor_copy(s.iota256_b[:, :], s.iota256[:, :])


def zero_tables(nc, tables):
    part = 131
    with nc.sbuf_tensor("zeros", [P, part * W], F32) as zeros:
        with phase(nc, "zero", "cleared", "stored") as (block, q):
            @block.vector
            def _(dve):
                nc.vector.memset(zeros[:, :], 0.0).then_inc(q.cleared, 1)

            @block.sync
            def _(sp):
                sp.wait_ge(q.cleared, 1)
                n = 0
                for table in tables:
                    rows = table.rearrange("(p r) w -> p (r w)", p=P)
                    for c in range(ROWS // P // part):
                        sp.dma_start(rows[:, c * part * W:(c + 1) * part * W], zeros[:, :]).then_inc(q.stored, 16)
                        n += 1
                sp.wait_ge(q.stored, 16 * n)


def load_edges(nc, s, src, dst):
    whole = E // T
    rest = E - whole * T
    with nc.sbuf_tensor("keys_in", [P, T], I32) as keys, nc.sbuf_tensor("srcs_in", [P, T], I32) as srcs:
        with phase(nc, "edges", "padded", "loaded") as (block, q):
            @block.vector
            def _(dve):
                nc.vector.memset(keys[:, :], N).then_inc(q.padded, 1)
                nc.vector.memset(srcs[:, :], N).then_inc(q.padded, 1)
                dve.wait_ge(q.loaded, 64)
                nc.vector.tensor_copy(s.pairs[:, :, 0], keys[:, :])
                nc.vector.tensor_copy(s.pairs[:, :, 1], srcs[:, :])

            @block.sync
            def _(sp):
                sp.wait_ge(q.padded, 2)
                for sb, dram in ((keys, dst), (srcs, src)):
                    sp.dma_start(sb[0:whole, :], dram[0:whole * T].rearrange("(p t) -> p t", t=T)
                                 ).then_inc(q.loaded, 16)
                    sp.dma_start(sb[whole:whole + 1, 0:rest], row_of(dram[whole * T:E])).then_inc(q.loaded, 16)


def split_digit(nc, s, which):
    with phase(nc, f"digit{which}", "split") as (block, q):
        @block.vector
        def _(dve):
            op, by = (ALU.bitwise_and, 255) if which == 0 else (ALU.logical_shift_right, 8)
            nc.vector.tensor_scalar(s.digit_i[:, :], s.pairs[:, :, 0], by, None, op).then_inc(q.split, 1)
            dve.wait_ge(q.split, 1)
            nc.vector.tensor_copy(s.digits[:, :], s.digit_i[:, :])


def histogram(nc, s, which, counts, onehot):
    with phase(nc, f"hist{which}", "onehot_ready", "counted", "step") as (block, q):
        @block.vector
        def _(dve):
            def tile(i, k, first):
                n = i * 8 + k
                if not first or k >= 4:
                    dve.wait_ge(q.counted, n - 3)
                nc.vector.tensor_scalar(onehot[:, k % 4, :], s.iota256_b[:, :], s.digits[:, bass.ds(n, 1)], None,
                                        ALU.is_equal).then_inc(q.onehot_ready, 1)

            for k in range(8):
                tile(0, k, True)
            with dve.Fori(1, ITERS) as i:
                for k in range(8):
                    tile(i, k, False)
            dve.wait_ge(q.counted, T)
            nc.vector.tensor_copy(s.totals[:, :], counts[:, 0:256]).then_inc(q.step, 1)
            dve.wait_ge(q.step, 1)
            nc.vector.tensor_tensor_scan(s.base[:, :], s.totals[:, :], s.totals[:, :], 0.0, ALU.add,
                                         ALU.bypass).then_inc(q.step, 1)
            dve.wait_ge(q.step, 2)
            nc.vector.tensor_tensor(s.base[:, :], s.base[:, :], s.totals[:, :], ALU.subtract)

        @block.tensor
        def _(pe):
            def tile(n, k, first):
                pe.wait_ge(q.onehot_ready, n + 1)
                nc.tensor.matmul(counts[:, 0:256], s.ones_b[:, :], onehot[:, k % 4, :], start=first, stop=True,
                                 skip_group_check=True).then_inc(q.counted, 1)

            for k in range(8):
                tile(k, k, k == 0)
            with pe.Fori(1, ITERS) as i:
                for k in range(8):
                    tile(i * 8 + k, k, False)


def rank_edges(nc, s, which, counts, onehot):
    with phase(nc, f"rank{which}", "onehot_ready", "summed", "ranked", "advanced", "kept", "done") as (block, q):
        @block.vector
        def _(dve):
            def build(n, k, wait):
                if wait:
                    dve.wait_ge(q.advanced, n - 1)
                nc.vector.tensor_scalar(onehot[:, k % 2, :], s.iota256_b[:, :], s.digits[:, bass.ds(n, 1)], None,
                                        ALU.is_equal).then_inc(q.onehot_ready, 1)

            def block_of(i, first, last):
                for k in range(8):
                    n = i * 8 + k
                    if not (last and k == 7):
                        build(n + 1, k + 1, wait=not (first and k == 0))
                    dve.wait_ge(q.summed, n + 1)
                    if k == 0 and not first:
                        dve.wait_ge(q.kept, i)
                    if not (first and k == 0):
                        dve.wait_ge(q.ranked, n)
                    nc.vector.tensor_tensor_reduce(s.picked[:, :], counts[:, 0:256], onehot[:, k % 2, :], 1.0, 0.0,
                                                   ALU.mult, ALU.add, s.rank_ring[:, k:k + 1]).then_inc(q.ranked, 1)

            build(0, 0, wait=False)
            block_of(0, True, False)
            with dve.Fori(1, ITERS - 1) as i:
                block_of(i, False, False)
            block_of(ITERS - 1, False, True)

        @block.tensor
        def _(pe):
            def tile(n, k):
                pe.wait_ge(q.onehot_ready, n + 1)
                nc.tensor.matmul(counts[:, 0:256], s.upper_b[:, :], onehot[:, k % 2, :], start=False, stop=True,
                                 skip_group_check=True).then_inc(q.summed, 1)
                pe.wait_ge(q.ranked, n + 1)
                nc.tensor.matmul(counts[:, 0:256], s.lower_in_b[:, :], onehot[:, k % 2, :], start=False, stop=True,
                                 skip_group_check=True).then_inc(q.advanced, 1)

            nc.tensor.matmul(counts[:, 0:256], s.ident[:, :], s.base[:, :], start=True, stop=True,
                             skip_group_check=True)
            with pe.Fori(0, ITERS) as i:
                for k in range(8):
                    tile(i * 8 + k, k)

        @block.scalar
        def _(act):
            with act.Fori(0, ITERS) as i:
                act.wait_ge(q.ranked, i * 8 + 8)
                nc.scalar.copy(s.ranks[:, bass.ds(i * 8, 8)], s.rank_ring[:, :]).then_inc(q.kept, 1)


def place_edges(nc, s, which, out):
    with phase(nc, f"place{which}", "step", "ready", "stored_a", "stored_b", "passed") as (block, q):
        stored = [q.stored_a, q.stored_b]

        @block.vector
        def _(dve):
            steps = Steps(dve, q.step)
            steps.then(nc.vector.tensor_copy(s.place[:, :], s.ranks[:, :]))
            steps.wait()
            if which == 0:
                steps.then(nc.vector.tensor_scalar(s.digit_i[:, :], s.place[:, :], 127, None, ALU.bitwise_and))
                steps.then(nc.vector.tensor_scalar(s.place_hi[:, :], s.place[:, :], 7, None,
                                                   ALU.logical_shift_right))
                steps.wait()
                steps.then(nc.vector.scalar_tensor_tensor(s.place[:, :], s.digit_i[:, :], float(T),
                                                          s.place_hi[:, :], ALU.mult, ALU.add))
                steps.wait()

            def feed(i, half, wait):
                t0 = i * 8 + half * 4
                if wait:
                    dve.wait_ge(stored[half], i * 64)
                nc.vector.tensor_copy(s.place_ring[:, half, :], s.place[:, bass.ds(t0, 4)]).then_inc(q.ready, 1)
                nc.vector.tensor_copy(s.pair_ring[:, half, :, :], s.pairs[:, bass.ds(t0, 4), :]).then_inc(q.ready, 1)

            feed(0, 0, False)
            feed(0, 1, False)
            with dve.Fori(1, ITERS) as i:
                feed(i, 0, True)
                feed(i, 1, True)

        @block.gpsimd
        def _(pool):
            with pool.Fori(0, ITERS) as i:
                for half in range(2):
                    pool.wait_ge(q.ready, i * 4 + half * 2 + 2)
                    hold(pool, q.passed)
                    for k in range(4):
                        pool.indirect_dma_start(
                            out[:, :], bass.IndirectOffsetOnAxis(ap=s.place_ring[:, half, k:k + 1], axis=0),
                            s.pair_ring[:, half, k, :], None).then_inc(stored[half], 16)
            for half in range(2):
                pool.wait_ge(stored[half], ITERS * 64)


def reload_pairs(nc, s, table):
    with phase(nc, "reload", "loaded") as (block, q):
        @block.sync
        def _(sp):
            sp.dma_start(s.pairs[:, :, :], table.rearrange("(p t) w -> p t w", t=T)).then_inc(q.loaded, 16)
            sp.wait_ge(q.loaded, 16)


def sort_edges(nc, s, src, dst, half_sorted, sorted_pairs):
    load_edges(nc, s, src, dst)
    with nc.psum_tensor("counts", [P, 512], F32) as counts, \
            nc.sbuf_tensor("onehot", [P, 4, 256], BF16) as onehot:
        for which, out in enumerate((half_sorted, sorted_pairs)):
            if which:
                reload_pairs(nc, s, half_sorted)
            split_digit(nc, s, which)
            histogram(nc, s, which, counts, onehot)
            rank_edges(nc, s, which, counts, onehot)
            place_edges(nc, s, which, out)


def plan_segments(nc, s, sorted_pairs):
    flat = sorted_pairs
    with ExitStack() as ctx:
        def sb(name, shape, dt):
            return ctx.enter_context(nc.sbuf_tensor(name, shape, dt))

        before = sb("before", [P, T, 2], I32)
        after = sb("after", [P, T, 2], I32)
        key = sb("key", [P, T], F32)
        key_before = sb("key_before", [P, T], F32)
        key_after = sb("key_after", [P, T], F32)
        first = sb("first", [P, T], F32)
        target = sb("target", [P, T], F32)
        clipped = sb("clipped", [P, T, 2], F32)
        one = sb("one", [P, 8], F32)
        bcast = sb("bcast", [P, P], F32)
        rows = ctx.enter_context(nc.psum_tensor("plan_rows", [P, 4, P], F32))
        whole_rows = ctx.enter_context(nc.psum_tensor("plan_whole", [P, 4, P], F32))
        with phase(nc, "plan", "padded", "loaded", "step", "turn", "turned") as (block, q):
            @block.sync
            def _(sp):
                sp.dma_start(s.pairs[:, :, :], flat.rearrange("(p t) w -> p t w", t=T)).then_inc(q.loaded, 16)
                sp.wait_ge(q.padded, 2)
                sp.dma_start(before[0:1, 1:T, :], flat[0:T - 1, :].rearrange("(p t) w -> p t w", p=1)
                             ).then_inc(q.loaded, 16)
                sp.dma_start(before[1:P, :, :], flat[T - 1:SLOTS - 1, :].rearrange("(p t) w -> p t w", t=T)
                             ).then_inc(q.loaded, 16)
                sp.dma_start(after[0:P - 1, :, :], flat[1:SLOTS - T + 1, :].rearrange("(p t) w -> p t w", t=T)
                             ).then_inc(q.loaded, 16)
                sp.dma_start(after[P - 1:P, 0:T - 1, :], flat[SLOTS - T + 1:SLOTS, :].rearrange(
                    "(p t) w -> p t w", p=1)).then_inc(q.loaded, 16)

            @block.vector
            def _(dve):
                v = nc.vector
                v.memset(before[:, :, :], -1).then_inc(q.padded, 1)
                v.memset(after[:, :, :], -1).then_inc(q.padded, 1)
                dve.wait_ge(q.loaded, 80)
                steps = Steps(dve, q.step)
                steps.then(v.tensor_copy(key[:, :], s.pairs[:, :, 0]))
                steps.then(v.tensor_copy(key_before[:, :], before[:, :, 0]))
                steps.then(v.tensor_copy(key_after[:, :], after[:, :, 0]))
                steps.then(v.tensor_copy(s.source[:, :], s.pairs[:, :, 1]))
                steps.then(v.tensor_scalar(clipped[:, :, 0], s.pairs[:, :, 1], float(N - 1), None, ALU.min))
                steps.then(v.tensor_scalar(clipped[:, :, 1], s.pairs[:, :, 0], float(N - 1), None, ALU.min))
                steps.wait()
                steps.then(v.tensor_copy(s.gather_rows[:, :, :], clipped[:, :, :]))
                steps.then(v.tensor_tensor(s.same[:, :], key[:, :], key_before[:, :], ALU.is_equal))
                steps.then(v.tensor_tensor(s.goes_on[:, :], key[:, :], key_after[:, :], ALU.is_equal))
                steps.then(v.tensor_scalar(first[:, :], key[:, :], key[:, 0:1], None, ALU.is_equal))
                steps.wait()
                steps.then(v.tensor_copy(s.same_in[:, :], s.same[:, :]))
                steps.then(v.tensor_scalar(s.reset[:, :], s.same[:, :], -1.0, BIG, ALU.add, ALU.mult))
                steps.then(v.tensor_scalar(s.ends[:, :], s.goes_on[:, :], -1.0, 1.0, ALU.mult, ALU.add))
                steps.then(v.tensor_scalar(first[:, :], first[:, :], s.same[:, 0:1], None, ALU.mult))
                steps.then(v.tensor_tensor(one[:, 4:5], key[:, 0:1], key[:, T - 1:T], ALU.is_equal))
                steps.then(v.tensor_copy(one[:, 2:3], key[:, 0:1]))
                steps.then(v.tensor_copy(one[:, 3:4], key[:, T - 1:T]))
                steps.wait()
                steps.then(v.memset(s.same_in[:, 0:1], 0.0))
                steps.then(v.tensor_copy(s.reset_in[:, :], s.reset[:, :]))
                steps.then(v.tensor_tensor(one[:, 0:1], one[:, 4:5], s.same[:, 0:1], ALU.mult))
                steps.then(v.tensor_tensor(one[:, 1:2], one[:, 4:5], s.goes_on[:, T - 1:T], ALU.mult))
                steps.then(v.tensor_scalar(target[:, :], key[:, :], -1.0, s.dummy[:, 0:1], ALU.mult, ALU.add))
                steps.wait()
                steps.then(v.memset(s.reset_in[:, 0:1], -BIG))
                steps.then(v.tensor_tensor(target[:, :], target[:, :], first[:, :], ALU.mult))
                steps.wait()
                steps.then(v.tensor_tensor(target[:, :], target[:, :], key[:, :], ALU.add))
                steps.wait()
                steps.then(v.scalar_tensor_tensor(target[:, :], s.goes_on[:, :], SKIP, target[:, :], ALU.mult,
                                                  ALU.max))
                steps.wait()
                steps.then(v.memset(target[:, T - 1:T], SKIP))
                steps.wait()
                steps.then(v.tensor_copy(s.scatter_rows[:, :], target[:, :]))

                steps.then(v.tensor_scalar(one[:, 5:6], one[:, 4:5], -1.0, 1.0, ALU.mult, ALU.add))
                steps.wait()
                steps.then(v.tensor_tensor(one[:, 5:6], one[:, 5:6], s.same[:, 0:1], ALU.mult))
                steps.wait()
                steps.then(v.tensor_scalar(one[:, 5:6], one[:, 5:6], -SKIP, SKIP, ALU.mult, ALU.add))
                steps.then(v.tensor_scalar(one[:, 6:7], s.goes_on[:, T - 1:T], SKIP, None, ALU.mult))
                steps.wait()
                steps.then(v.tensor_tensor(one[:, 5:6], one[:, 5:6], one[:, 2:3], ALU.max))
                steps.then(v.tensor_tensor(one[:, 6:7], one[:, 6:7], one[:, 3:4], ALU.max))
                steps.wait()
                steps.then(v.tensor_copy(s.fix_rows[:, :], one[:, 5:7]))

                for j in range(4):
                    if j:
                        dve.wait_ge(q.turned, j)
                    nc.vector.tensor_copy(bcast[:, :], one[:, j:j + 1].to_broadcast([P, P])).then_inc(q.turn, 1)
                dve.wait_ge(q.turned, 4)
                steps.then(v.scalar_tensor_tensor(s.mask_first[:, :], rows[:, 2, :], one[:, 3:4], s.upper[:, :],
                                                  ALU.is_equal, ALU.mult))
                steps.then(v.scalar_tensor_tensor(s.mask_last[:, :], rows[:, 3, :], one[:, 3:4], s.upper_in[:, :],
                                                  ALU.is_equal, ALU.mult))
                steps.then(v.tensor_copy(s.chunk_same[:, :], rows[0:HEADS, 0, :]))
                steps.then(v.tensor_copy(s.chunk_goes_on[:, :], rows[0:HEADS, 1, :]))
                steps.then(v.tensor_scalar(s.chunk_reset[:, :], rows[0:HEADS, 0, :], -1.0, BIG, ALU.add, ALU.mult))

            @block.tensor
            def _(pe):
                for j in range(4):
                    pe.wait_ge(q.turn, j + 1)
                    nc.tensor.transpose(rows[:, j, :], bcast[:, :], s.ident[:, :]).then_inc(q.turned, 1)


def load_weights(nc, s, w):
    loads = []

    def to(sb, dram):
        loads.append((sb, dram))

    for n in range(2):
        mine, theirs = ("msg", "rev")
        to(s.w_edge[:, n, 0:D], w[f"{mine}_W1"][n * D:(n + 1) * D, :])
        to(s.w_edge[:, n, D:2 * D], w[f"{theirs}_W1"][(1 - n) * D:(2 - n) * D, :])
        to(s.w_msg2[:, n, :], w[("msg_W2", "rev_W2")[n]])
        to(s.b_edge[:, n * D:(n + 1) * D], row_of(w[("msg_b1", "rev_b1")[n]]).to_broadcast([P, D]))
        to(s.b_msg2[n:n + 1, :], row_of(w[("msg_b2", "rev_b2")[n]]))
        to(s.upd1[:, n, :], w["upd_W1"][n * D:(n + 1) * D, :])
        to(s.upd2[:, n, :], w["upd_W2"][n * D:(n + 1) * D, :])
    to(s.upd_b1[:, :], w["upd_b1"].rearrange("(c p) -> p c", p=P))
    to(s.upd_b2[:, :], row_of(w["upd_b2"]).to_broadcast([P, D]))
    for l in range(LAYERS):
        to(s.gat_w[:, l, :], w["gat_W"][l])
        to(s.gat_b[:, l, :], w["gat_bias"][l:l + 1, :].to_broadcast([P, D]))
        to(s.skip_w[:, l, :], w["skip_W"][l])
        to(s.skip_b[:, l, :], w["skip_b"][l:l + 1, :].to_broadcast([P, D]))
    with nc.sbuf_tensor("att_rows", [P, LAYERS, 2, HEADS * D], F32) as att_rows, \
            nc.sbuf_tensor("att_scratch", [P, 4, D], F32) as scratch:
        for l in range(LAYERS):
            for j, name in enumerate(("att_src", "att_dst")):
                to(att_rows[:, l, j, :], w[name][l:l + 1].rearrange("a h d -> a (h d)").to_broadcast([P, HEADS * D]))
        with phase(nc, "weights", "loaded", "step") as (block, q):
            @block.sync
            def _(sp):
                with nc.allow_non_contiguous_dma(reason="a bias of 256 numbers by partitions"):
                    for sb, dram in loads:
                        sp.dma_start(sb, dram).then_inc(q.loaded, 16)

            @block.vector
            def _(dve):
                dve.wait_ge(q.loaded, 16 * len(loads))
                n = 0
                for l in range(LAYERS):
                    for j in range(2):
                        for h in range(HEADS):
                            if n >= 4:
                                dve.wait_ge(q.step, n - 3)
                            nc.vector.tensor_tensor_reduce(
                                scratch[:, n % 4, :], s.gat_w[:, l, h * D:(h + 1) * D],
                                att_rows[:, l, j, h * D:(h + 1) * D], 1.0, 0.0, ALU.mult, ALU.add,
                                s.w_att[:, l, j * HEADS + h:j * HEADS + h + 1]).then_inc(q.step, 1)
                            n += 1


def message_edges(nc, s, x, sums_in, sums_out):
    with ExitStack() as ctx:
        def sb(name, shape, dt=F32):
            return ctx.enter_context(nc.sbuf_tensor(name, shape, dt))

        def pb(name, shape):
            return ctx.enter_context(nc.psum_tensor(name, shape, F32))

        gidx = sb("gidx", [P, 2, 4, 2], I32)
        sidx = sb("sidx", [P, 2, 4], I32)
        ridx = sb("ridx", [P, 2, 4], I32)
        ridx_f = sb("ridx_f", [P, 4])
        src4 = sb("src4", [P, 2, 4])
        repeats = sb("repeats", [P, 4])
        x_src = sb("x_src", [P, 2, 4, D])
        x_dst = sb("x_dst", [P, 2, 4, D])
        x_t = sb("x_t", [P, 2, 2, P])
        hidden = sb("hidden", [P, 2, 2, D])
        relus = sb("relus", [P, 2, 2, W])
        equal = sb("equal", [P, 2, P])
        pairs_scratch = sb("pairs_scratch", [P, P])
        rows = sb("rows", [P, 2, 4, W])
        rev_rows = sb("rev_rows", [P, 2, 4, W])
        turned = [pb(f"turned{j}", [P, 2, 256]) for j in range(2)]
        srcs_t = [pb(f"srcs_t{j}", [P, 512]) for j in range(2)]
        hid = [pb(f"hid{j}", [P, 2, 256]) for j in range(2)]
        dedup = [pb(f"dedup{j}", [P, 512]) for j in range(2)]

        with phase(nc, "msg_init", "x") as (block, q):
            @block.vector
            def _(dve):
                nc.vector.memset(relus[:, :, :, :], 0.0).then_inc(q.x, 1)
                nc.vector.memset(rows[:, :, :, :], 0.0)
                dve.wait_ge(q.x, 1)
                nc.vector.memset(relus[:, :, :, D:D + 1], 1.0)

        with phase(nc, "msg", "gidx_ready", "gathered_a", "gathered_b", "src4_ready", "sidx_ready",
                   "x_turned", "srcs_turned", "x_t_ready", "hid_ready", "hidden_ready", "relu_ready",
                   "equal_ready", "counted", "row_ready", "rev_summed", "rev_ready", "stored_a", "stored_b", "passed",
                   "rev_stored", "ridx_step") as (block, q):
            gathered = [q.gathered_a, q.gathered_b]
            stored = [q.stored_a, q.stored_b]

            @block.gpsimd
            def _(pool):
                def gather(i, half, k, wait_x):
                    if k == 0:
                        pool.wait_ge(q.gidx_ready, 2 * i + half + 1)
                        if wait_x:
                            pool.wait_ge(q.x_turned, 4 * (2 * i + half - 1))
                        hold(pool, q.passed)
                    for j, to in enumerate((x_src, x_dst)):
                        pool.indirect_dma_start(to[:, half, k, :], None, x[:, :], bass.IndirectOffsetOnAxis(
                            ap=gidx[:, half, k, j:j + 1], axis=0)).then_inc(gathered[half], 16)

                def scatter(i, half, k, first=False):
                    n = 8 * i + 4 * half + k
                    if k == 0:
                        pool.wait_ge(q.sidx_ready, 2 * i + half + 1)
                        pool.wait_ge(q.ridx_step, 3 * (2 * i + half + 1))
                    pool.wait_ge(q.row_ready, n + 1)
                    hold(pool, q.passed)
                    pool.indirect_dma_start(sums_in[:, :], bass.IndirectOffsetOnAxis(
                        ap=sidx[:, half, k:k + 1], axis=0), rows[:, half, k, :], None,
                        bounds_check=ROWS - 1, oob_is_err=False).then_inc(stored[half], 16)
                    pool.wait_ge(q.rev_ready, n + 1)
                    if not first:
                        pool.wait_ge(q.rev_stored, 16 * n)
                    hold(pool, q.passed)
                    pool.indirect_dma_start(sums_out[:, :], bass.IndirectOffsetOnAxis(
                        ap=ridx[:, half, k:k + 1], axis=0), rev_rows[:, half, k, :], None,
                        compute_op=ALU.add).then_inc(q.rev_stored, 16)

                for k in range(4):
                    gather(0, 0, k, False)
                for k in range(4):
                    gather(0, 1, k, False)
                for k in range(4):
                    gather(1, 0, k, True)
                    scatter(0, 0, k, first=k == 0)
                with pool.Fori(1, ITERS - 1) as i:
                    for k in range(4):
                        gather(i, 1, k, True)
                        scatter(i - 1, 1, k)
                    for k in range(4):
                        gather(i + 1, 0, k, True)
                        scatter(i, 0, k)
                for k in range(4):
                    gather(ITERS - 1, 1, k, True)
                    scatter(ITERS - 2, 1, k)
                for half in range(2):
                    for k in range(4):
                        scatter(ITERS - 1, half, k)
                for half in range(2):
                    pool.wait_ge(stored[half], 64 * ITERS)
                pool.wait_ge(q.rev_stored, 16 * T)

            @block.tensor
            def _(pe):
                def tile(i, half, k, first):
                    n = 8 * i + 4 * half + k
                    b = k % 2
                    if k == 0:
                        pe.wait_ge(gathered[half], 128 * (i + 1))
                        pe.wait_ge(q.src4_ready, 2 * i + half + 1)
                    if not (first and half == 0 and k < 2):
                        pe.wait_ge(q.x_t_ready, n - 1)
                    nc.tensor.transpose(turned[b][:, 0, 0:P], x_src[:, half, k, :], s.ident[:, :])
                    nc.tensor.transpose(turned[b][:, 1, 0:P], x_dst[:, half, k, :], s.ident[:, :]
                                        ).then_inc(q.x_turned, 1)
                    if not (first and half == 0 and k < 2):
                        pe.wait_ge(q.equal_ready, n - 1)
                    mm = nc.tensor.transpose(srcs_t[b][:, 0:P], src4[:, half, k:k + 1].to_broadcast([P, P]),
                                             s.ident[:, :])
                    mm.then_inc(q.srcs_turned, 1)
                    pe.wait_ge(q.x_t_ready, n + 1)
                    if not (first and half == 0 and k < 2):
                        pe.wait_ge(q.hidden_ready, n - 1)
                    for j in range(2):
                        mm = nc.tensor.matmul(hid[b][:, 0, 0:2 * D], x_t[:, b, j, :], s.w_edge[:, j, :],
                                              start=j == 0, stop=j == 1)
                    mm.then_inc(q.hid_ready, 1)
                    pe.wait_ge(q.relu_ready, n + 1)
                    if not (first and half == 0 and k < 2):
                        pe.wait_ge(q.rev_ready, n - 1)
                    nc.tensor.matmul(dedup[b][:, 0:W], equal[:, b, :], relus[:, b, 1, :], start=True, stop=True
                                     ).then_inc(q.rev_summed, 1)

                def block_of(i, first=False):
                    for half in range(2):
                        for k in range(4):
                            tile(i, half, k, first)

                block_of(0, first=True)
                with pe.Fori(1, ITERS) as i:
                    block_of(i)

            @block.scalar
            def _(act):
                def tile(i, half, k, first):
                    n = 8 * i + 4 * half + k
                    b = k % 2
                    early = first and half == 0 and k < 2
                    act.wait_ge(q.x_turned, n + 1)
                    if not early:
                        act.wait_ge(q.hid_ready, n - 1)
                    nc.scalar.copy(x_t[:, b, :, :], turned[b][:, :, 0:P]).then_inc(q.x_t_ready, 1)
                    act.wait_ge(q.hidden_ready, n + 1)
                    if not early:
                        act.wait_ge(q.rev_summed, n - 1)
                        act.wait_ge(q.row_ready, n - 1)
                    nc.scalar.activation(relus[:, b, :, 0:D], hidden[:, b, :, :], ACT.Relu).then_inc(q.relu_ready, 1)
                    act.wait_ge(q.rev_summed, n + 1)
                    if k == 0 and not first:
                        act.wait_ge(q.rev_stored, 16 * (8 * i + 4 * half - 4))
                    nc.scalar.copy(rev_rows[:, half, k, :], dedup[b][:, 0:W]).then_inc(q.rev_ready, 1)

                def block_of(i, first=False):
                    for half in range(2):
                        for k in range(4):
                            tile(i, half, k, first)

                block_of(0, first=True)
                with act.Fori(1, ITERS) as i:
                    block_of(i)

            @block.vector
            def _(dve):
                v = nc.vector

                def feed(i, half):
                    v.tensor_copy(gidx[:, half, :, :], s.gather_rows[:, bass.ds(8 * i + 4 * half, 4), :]
                                  ).then_inc(q.gidx_ready, 1)

                def half_block(i, half, first, last):
                    t0 = 8 * i + 4 * half
                    if not last:
                        dve.wait_ge(gathered[half], 128 * (i + 1))
                        feed(i + 1, half)
                    if not first:
                        dve.wait_ge(q.srcs_turned, 4 * (2 * i + half - 1))
                        dve.wait_ge(stored[half], 64 * i)
                        dve.wait_ge(q.rev_stored, 16 * (t0 - 4))
                        dve.wait_ge(q.ridx_step, 6 * i + 3 * half)
                    v.tensor_copy(src4[:, half, :], s.source[:, bass.ds(t0, 4)]).then_inc(q.src4_ready, 1)
                    v.tensor_copy(sidx[:, half, :], s.scatter_rows[:, bass.ds(t0, 4)]).then_inc(q.sidx_ready, 1)
                    dve.wait_ge(q.src4_ready, 2 * i + half + 1)
                    for k in range(4):
                        n = t0 + k
                        b = k % 2
                        early = first and half == 0 and k < 2
                        dve.wait_ge(q.srcs_turned, n + 1)
                        if not early:
                            dve.wait_ge(q.rev_summed, n - 1)
                        v.tensor_scalar(equal[:, b, :], srcs_t[b][:, 0:P], src4[:, half, k:k + 1], None,
                                        ALU.is_equal).then_inc(q.equal_ready, 1)
                        dve.wait_ge(q.hid_ready, n + 1)
                        if not early:
                            dve.wait_ge(q.relu_ready, n - 1)
                        v.tensor_tensor(hidden[:, b, :, :].rearrange("p a d -> p (a d)"), hid[b][:, 0, 0:2 * D],
                                        s.b_edge[:, :], ALU.add).then_inc(q.hidden_ready, 1)
                        dve.wait_ge(q.equal_ready, n + 1)
                        if not (first and half == 0 and k == 0):
                            dve.wait_ge(q.counted, n)
                        if k == 0 and not (first and half == 0):
                            dve.wait_ge(q.ridx_step, 6 * i + 3 * half)
                        v.tensor_tensor_reduce(pairs_scratch[:, :], equal[:, b, :], s.lower[:, :], 1.0, 0.0,
                                               ALU.mult, ALU.add, repeats[:, k:k + 1]).then_inc(q.counted, 1)
                        dve.wait_ge(q.relu_ready, n + 1)
                        if not (first and half == 0 and k == 0):
                            dve.wait_ge(q.row_ready, n)
                        before = rows[:, half, k - 1, :] if k else rows[:, 1 - half, 3, :]
                        v.scalar_tensor_tensor(rows[:, half, k, :], before, s.same_in[:, bass.ds(n, 1)],
                                               relus[:, b, 0, :], ALU.mult, ALU.add).then_inc(q.row_ready, 1)
                    dve.wait_ge(q.counted, t0 + 4)
                    v.tensor_scalar(ridx_f[:, :], repeats[:, :], 0.0, s.dummy[:, 0:1], ALU.is_gt, ALU.mult
                                    ).then_inc(q.ridx_step, 1)
                    dve.wait_ge(q.ridx_step, 6 * i + 3 * half + 1)
                    v.tensor_tensor(ridx_f[:, :], ridx_f[:, :], src4[:, half, :], ALU.max).then_inc(q.ridx_step, 1)
                    dve.wait_ge(q.ridx_step, 6 * i + 3 * half + 2)
                    v.tensor_copy(ridx[:, half, :], ridx_f[:, :]).then_inc(q.ridx_step, 1)

                feed(0, 0)
                feed(0, 1)
                half_block(0, 0, True, False)
                half_block(0, 1, True, False)
                with dve.Fori(1, ITERS - 1) as i:
                    half_block(i, 0, False, False)
                    half_block(i, 1, False, False)
                half_block(ITERS - 1, 0, False, True)
                half_block(ITERS - 1, 1, False, True)

        fixup(nc, s, "msg_fix", sums_in, rows[:, 1, 3, :], W, dedup)


def fixup(nc, s, name, table, last, cols, sums):
    with nc.sbuf_tensor(f"{name}_first", [P, W], F32) as first, \
            nc.sbuf_tensor(f"{name}_last", [P, W], F32) as total:
        with phase(nc, name, "loaded", "summed", "added", "stored") as (block, q):
            @block.sync
            def _(sp):
                sp.dma_start(first[:, :], table[SIDE:SIDE + P, :]).then_inc(q.loaded, 16)

            @block.tensor
            def _(pe):
                nc.tensor.matmul(sums[0][:, 0:cols], s.mask_first[:, :], last[:, 0:cols], start=True, stop=True
                                 ).then_inc(q.summed, 1)
                nc.tensor.matmul(sums[1][:, 0:cols], s.mask_last[:, :], last[:, 0:cols], start=True, stop=True
                                 ).then_inc(q.summed, 1)

            @block.vector
            def _(dve):
                dve.wait_ge(q.summed, 2)
                dve.wait_ge(q.loaded, 16)
                nc.vector.tensor_tensor(first[:, 0:cols], first[:, 0:cols], sums[0][:, 0:cols], ALU.add
                                        ).then_inc(q.added, 1)
                nc.vector.tensor_copy(total[:, 0:cols], sums[1][:, 0:cols]).then_inc(q.added, 1)
                if cols < W:
                    nc.vector.tensor_copy(total[:, cols:W], last[:, cols:W]).then_inc(q.added, 1)

            @block.gpsimd
            def _(pool):
                pool.wait_ge(q.added, 2 + (cols < W))
                for j, rows in enumerate((first, total)):
                    pool.indirect_dma_start(table[:, :], bass.IndirectOffsetOnAxis(ap=s.fix_rows[:, j:j + 1], axis=0),
                                            rows[:, :], None, bounds_check=ROWS - 1, oob_is_err=False
                                            ).then_inc(q.stored, 16)
                pool.wait_ge(q.stored, 32)


def nodes_of(dram, start):
    return dram[bass.ds(start, BLOCK), :].rearrange("(p c) w -> p c w", c=4)


def over_blocks(eng, step):
    step(0, 0, 0, True)
    step(1, 1, BLOCK, True)
    with eng.Fori(1, NBLOCKS // 2 - 1) as i:
        step(2 * i, 0, i * (2 * BLOCK), False)
        step(2 * i + 1, 1, i * (2 * BLOCK) + BLOCK, False)
    step(NBLOCKS - 2, 0, (NBLOCKS - 2) * BLOCK, False)
    step(NBLOCKS - 1, 1, N - BLOCK, False)


def loads_done(eng, sem, j, slot, n):
    eng.wait_ge(sem, 8 * n * (j - slot) + 16 * n)


def over_features(bias):
    return bias.rearrange("p (o d) -> p o d", o=1).to_broadcast([P, 4, D])


def head_rows(nc, s, steps, scores, rows, node_att, slot):
    v = nc.vector
    a = node_att[:, slot, :, :]
    r = rows[:, slot, :, :]
    steps.then(v.tensor_copy(r[:, :, D:D + HEADS], scores[:, :, 0:HEADS]))
    steps.then(v.tensor_copy(a[:, :, HEADS:2 * HEADS], scores[:, :, HEADS:2 * HEADS]))
    steps.wait()
    steps.then(v.tensor_tensor(a[:, :, 0:HEADS], r[:, :, D:D + HEADS], a[:, :, HEADS:2 * HEADS], ALU.add))
    steps.wait()
    steps.then(v.scalar_tensor_tensor(a[:, :, 0:HEADS], a[:, :, 0:HEADS], SLOPE, a[:, :, 0:HEADS], ALU.mult, ALU.max))


def deviation(nc, s, q, act, moments, rstd, before, j):
    act.wait_ge(q.step, before + 8)
    nc.scalar.activation(rstd[:, :], moments[:, :, 1], ACT.Sqrt, bias=s.eps[:, 0:1]).then_inc(q.rstd_ready, 1)


def layernorm(nc, q, steps, src, dst, stats, moments, rstd, j):
    v = nc.vector
    for c in range(4):
        steps.then(v.bn_stats(stats[:, c, :], src[:, c, :]))
    steps.wait()
    hold(steps.eng, q.passed)
    for c in range(4):
        steps.then(v.bn_aggr(moments[:, c, :], stats[:, c, :]))
    steps.wait()
    steps.eng.wait_ge(q.rstd_ready, j + 1)
    steps.then(v.reciprocal(rstd[:, :], rstd[:, :]))
    steps.wait()
    for c in range(4):
        steps.then(v.tensor_scalar(dst[:, c, 0:D], src[:, c, :], moments[:, c, 0:1], rstd[:, c:c + 1],
                                   ALU.subtract, ALU.mult))


NORM_STEPS = 4 + 4 + 1 + 4
HEAD_STEPS = 4


def store_rows(pool, q, stored, new, node_att, x_next, att_next, j, slot, start):
    pool.wait_ge(q.tail_step, HEAD_STEPS * (j + 1))
    if isinstance(j, int) and j == NBLOCKS - 1:
        pool.wait_ge(stored[0], 16 * NBLOCKS)
        pool.wait_ge(stored[1], 16 * (NBLOCKS - 2))
    pool.dma_start(nodes_of(x_next, start), new[:, slot, :, :]).then_inc(stored[slot], 16)
    pool.dma_start(nodes_of(att_next, start), node_att[:, slot, :, :]).then_inc(stored[slot], 16)


def update_nodes(nc, s, x, sums_in, sums_out, x_next, att_next):
    with ExitStack() as ctx:
        def sb(name, shape, dt=F32):
            return ctx.enter_context(nc.sbuf_tensor(name, shape, dt))

        def pb(name, shape):
            return ctx.enter_context(nc.psum_tensor(name, shape, F32))

        xs = sb("xs", [P, 2, 4, D])
        ins = sb("ins", [P, 2, 4, W])
        outs = sb("outs", [P, 2, 4, W])
        degrees = sb("degrees", [P, 2, 4, 2])
        x_t = sb("xs_t", [P, BLOCK])
        in_t = sb("ins_t", [P, BLOCK])
        out_t = sb("outs_t", [P, BLOCK])
        deg_t = sb("deg_t", [2, BLOCK])
        agg_t = sb("agg_t", [P, BLOCK])
        hid_t = sb("hid_t", [P, 2, BLOCK])
        base = sb("base_rows", [P, 2, 4, D])
        total = sb("total_rows", [P, 2, 4, D])
        new = sb("new_rows", [P, 2, 4, D + HEADS])
        new_t = sb("new_t", [P, BLOCK])
        node_att = sb("node_att", [P, 2, 4, 2 * HEADS])
        stats = sb("stats", [P, 4, 6])
        moments = sb("moments", [P, 4, 2])
        rstd = sb("rstd", [P, 4])
        p_x = pb("p_x", [P, BLOCK])
        p_in = pb("p_in", [P, BLOCK])
        p_out = pb("p_out", [P, BLOCK])
        p_deg = pb("p_deg", [P, BLOCK])
        p_agg = pb("p_agg", [P, BLOCK])
        p_hid = pb("p_hid", [P, BLOCK])
        p_new = pb("p_new", [P, 4, D])
        p_tail = pb("p_tail", [P, BLOCK])

        with phase(nc, "upd", "loaded_a", "loaded_b", "degrees_ready", "turned", "copied", "base_ready", "agg_ready",
                   "agg_copied", "hid_ready", "hid_copied", "new_ready", "step", "rows_turned", "rows_copied",
                   "scored", "tail_step", "stored_a", "stored_b", "passed", "doubled", "rstd_ready") as (block, q):
            loaded = [q.loaded_a, q.loaded_b]
            stored = [q.stored_a, q.stored_b]
            steps_of_block = 1 + NORM_STEPS

            @block.sync
            def _(sp):
                def step(j, slot, start, first):
                    if not first:
                        sp.wait_ge(q.turned, 4 * (j - 1))
                        sp.wait_ge(q.base_ready, j - 1)
                        hold(sp, q.passed)
                        sp.wait_ge(q.degrees_ready, 2 * (j - 1))
                        hold(sp, q.passed)
                    sp.dma_start(xs[:, slot, :, :], nodes_of(x, start)).then_inc(loaded[slot], 16)
                    sp.dma_start(ins[:, slot, :, :], nodes_of(sums_in, start)).then_inc(loaded[slot], 16)
                    sp.dma_start(outs[:, slot, :, :], nodes_of(sums_out, start)).then_inc(loaded[slot], 16)

                over_blocks(sp, step)

            @block.gpsimd
            def _(pool):
                def store(j, slot, start):
                    store_rows(pool, q, stored, new, node_att, x_next, att_next, j, slot, start)

                def step(j, slot, start, first):
                    loads_done(pool, loaded[slot], j, slot, 3)
                    if not first:
                        pool.wait_ge(q.step, steps_of_block * (j - 2) + 1)
                    nc.gpsimd.tensor_tensor(base[:, slot], xs[:, slot], xs[:, slot], ALU.add).then_inc(q.doubled, 1)
                    pool.wait_ge(q.doubled, j + 1)
                    nc.gpsimd.tensor_tensor(base[:, slot], base[:, slot], over_features(s.upd_b2[:, :]), ALU.add
                                            ).then_inc(q.base_ready, 1)
                    if not (first and slot == 0):
                        before = start - BLOCK if not (isinstance(j, int) and j == NBLOCKS - 1) else (NBLOCKS - 2) * BLOCK
                        store(j - 1, 1 - slot, before)

                over_blocks(pool, step)
                store(NBLOCKS - 1, 1, N - BLOCK)
                for slot in range(2):
                    pool.wait_ge(stored[slot], 16 * NBLOCKS)

            @block.tensor
            def _(pe):
                def tail(j, slot):
                    pe.wait_ge(q.step, steps_of_block * (j + 1))
                    if not (isinstance(j, int) and j == 0):
                        pe.wait_ge(q.tail_step, HEAD_STEPS * j)
                    for c in range(4):
                        mm = nc.tensor.transpose(p_tail[:, c * P:(c + 1) * P], new[:, slot, c, 0:D], s.ident[:, :])
                    mm.then_inc(q.rows_turned, 1)
                    pe.wait_ge(q.rows_copied, j + 1)
                    for c in range(4):
                        mm = nc.tensor.matmul(p_tail[:, c * 8:c * 8 + 8], new_t[:, c * P:(c + 1) * P],
                                              s.w_att[:, 0, :], start=True, stop=True)
                    mm.then_inc(q.scored, 1)

                def step(j, slot, start, first):
                    very_first = first and slot == 0
                    loads_done(pe, loaded[slot], j, slot, 3)
                    for m, (dst, src) in enumerate(((p_x, xs), (p_in, ins), (p_out, outs))):
                        if not very_first:
                            pe.wait_ge(q.copied, 4 * (j - 1) + m + 1)
                        for c in range(4):
                            mm = nc.tensor.transpose(dst[:, c * P:(c + 1) * P], src[:, slot, c, 0:D], s.ident[:, :])
                        mm.then_inc(q.turned, 1)
                    pe.wait_ge(q.degrees_ready, 2 * (j + 1))
                    if not very_first:
                        pe.wait_ge(q.copied, 4 * j)
                    for c in range(4):
                        mm = nc.tensor.transpose(p_deg[0:2, c * P:(c + 1) * P], degrees[:, slot, c, :],
                                                 s.ident[:, :])
                    mm.then_inc(q.turned, 1)
                    pe.wait_ge(q.copied, 4 * j + 4)
                    if not very_first:
                        pe.wait_ge(q.agg_copied, j)
                    nc.tensor.matmul(p_agg[:, :], s.w_msg2[:, 0, :], in_t[:, :], start=True, stop=False)
                    nc.tensor.matmul(p_agg[:, :], s.w_msg2[:, 1, :], out_t[:, :], start=False, stop=False)
                    nc.tensor.matmul(p_agg[:, :], s.b_msg2[:, :], deg_t[:, :], start=False, stop=True
                                     ).then_inc(q.agg_ready, 1)
                    if not very_first:
                        tail(j - 1, 1 - slot)
                    pe.wait_ge(q.agg_copied, j + 1)
                    for m in range(2):
                        if m or not very_first:
                            pe.wait_ge(q.hid_copied, 2 * j + m)
                        nc.tensor.matmul(p_hid[:, :], s.upd1[:, 0, m * P:(m + 1) * P], agg_t[:, :], start=True,
                                         stop=False)
                        nc.tensor.matmul(p_hid[:, :], s.upd1[:, 1, m * P:(m + 1) * P], x_t[:, :], start=False,
                                         stop=True).then_inc(q.hid_ready, 1)
                    pe.wait_ge(q.hid_copied, 2 * j + 2)
                    if not very_first:
                        pe.wait_ge(q.step, steps_of_block * (j - 1) + 1)
                    for c in range(4):
                        for m in range(2):
                            mm = nc.tensor.matmul(p_new[:, c, :], hid_t[:, m, c * P:(c + 1) * P], s.upd2[:, m, :],
                                                  start=m == 0, stop=m == 1)
                    mm.then_inc(q.new_ready, 1)

                over_blocks(pe, step)
                tail(NBLOCKS - 1, 1)

            @block.scalar
            def _(act):
                def copy_rows(j):
                    act.wait_ge(q.rows_turned, j + 1)
                    if not (isinstance(j, int) and j == 0):
                        act.wait_ge(q.scored, j)
                    nc.scalar.copy(new_t[:, :], p_tail[:, :]).then_inc(q.rows_copied, 1)

                def step(j, slot, start, first):
                    very_first = first and slot == 0
                    for m, (dst, src) in enumerate(((x_t, p_x), (in_t, p_in), (out_t, p_out), (deg_t, p_deg))):
                        act.wait_ge(q.turned, 4 * j + m + 1)
                        if m == 0 and not very_first:
                            act.wait_ge(q.hid_ready, 2 * j)
                        n = 2 if m == 3 else P
                        nc.scalar.copy(dst[0:n, :], src[0:n, :]).then_inc(q.copied, 1)
                        if m == 2 and not very_first:
                            deviation(nc, s, q, act, moments, rstd, steps_of_block * (j - 1) + 1, j - 1)
                    act.wait_ge(q.agg_ready, j + 1)
                    nc.scalar.copy(agg_t[:, :], p_agg[:, :]).then_inc(q.agg_copied, 1)
                    if not very_first:
                        copy_rows(j - 1)
                    for m in range(2):
                        act.wait_ge(q.hid_ready, 2 * j + m + 1)
                        if m == 0 and not very_first:
                            act.wait_ge(q.new_ready, j)
                        nc.scalar.activation(hid_t[:, m, :], p_hid[:, :], ACT.Relu, bias=s.upd_b1[:, m:m + 1]
                                             ).then_inc(q.hid_copied, 1)

                over_blocks(act, step)
                deviation(nc, s, q, act, moments, rstd, steps_of_block * (NBLOCKS - 1) + 1, NBLOCKS - 1)
                copy_rows(NBLOCKS - 1)

            @block.vector
            def _(dve):
                v = nc.vector

                def tail(j, slot):
                    dve.wait_ge(q.scored, j + 1)
                    steps = Steps(dve, q.tail_step, HEAD_STEPS * j)
                    head_rows(nc, s, steps, p_tail[:, 0:32].rearrange("p (c k) -> p c k", c=4), new, node_att, slot)

                def step(j, slot, start, first):
                    very_first = first and slot == 0
                    loads_done(dve, loaded[slot], j, slot, 3)
                    if not first:
                        dve.wait_ge(q.turned, 4 * (j - 1))
                    v.tensor_copy(degrees[:, slot, :, 0:1], ins[:, slot, :, D:D + 1]).then_inc(q.degrees_ready, 1)
                    v.tensor_copy(degrees[:, slot, :, 1:2], outs[:, slot, :, D:D + 1]).then_inc(q.degrees_ready, 1)
                    if not very_first:
                        tail(j - 1, 1 - slot)
                    dve.wait_ge(q.new_ready, j + 1)
                    dve.wait_ge(q.base_ready, j + 1)
                    steps = Steps(dve, q.step, steps_of_block * j)
                    steps.then(v.tensor_tensor(total[:, slot], base[:, slot], p_new[:, :, :], ALU.add))
                    steps.wait()
                    if not first:
                        dve.wait_ge(stored[slot], 16 * (j - slot))
                    layernorm(nc, q, steps, total[:, slot], new[:, slot], stats, moments, rstd, j)

                over_blocks(dve, step)
                tail(NBLOCKS - 1, 1)


def score_edges(nc, s, layer, x_rows, att_rows, turned_x):
    with ExitStack() as ctx:
        def sb(name, shape, dt=F32):
            return ctx.enter_context(nc.sbuf_tensor(f"{name}_{layer}", shape, dt))

        gidx = sb("gidx2", [P, 2, 4, 2], I32)
        rows = sb("src_rows", [P, 2, 4, D + HEADS])
        atts = sb("dst_atts", [P, 2, 4, 2 * HEADS])
        x_t = sb("src_t", [P, 2, BLOCK])
        banks = [ctx.enter_context(nc.psum_tensor(f"src_bank{h}_{layer}", [P, BLOCK], F32)) for h in range(2)]
        with phase(nc, f"score{layer}", "gidx_ready", "gathered_a", "gathered_b", "turned", "copied", "stored_a", "stored_b", "passed",
                   "scored") as (block, q):
            gathered = [q.gathered_a, q.gathered_b]
            stored = [q.stored_a, q.stored_b]

            def over_halves(eng, step):
                step(0, 0, True)
                step(0, 1, True)
                with eng.Fori(1, ITERS) as i:
                    step(i, 0, False)
                    step(i, 1, False)

            @block.gpsimd
            def _(pool):
                def step(i, half, first):
                    pool.wait_ge(q.gidx_ready, 2 * i + half + 1)
                    if not first:
                        pool.wait_ge(q.turned, 2 * i + half - 1)
                        pool.wait_ge(q.scored, 4 * i + 2 * half - 2)
                    hold(pool, q.passed)
                    for k in range(4):
                        pool.indirect_dma_start(rows[:, half, k, :], None, x_rows[:, :], bass.IndirectOffsetOnAxis(
                            ap=gidx[:, half, k, 0:1], axis=0)).then_inc(gathered[half], 16)
                        pool.indirect_dma_start(atts[:, half, k, :], None, att_rows[:, :], bass.IndirectOffsetOnAxis(
                            ap=gidx[:, half, k, 1:2], axis=0)).then_inc(gathered[half], 16)

                over_halves(pool, step)

            @block.tensor
            def _(pe):
                def step(i, half, first):
                    pe.wait_ge(gathered[half], 128 * i + 128)
                    if not first:
                        pe.wait_ge(q.copied, 2 * i + half - 1)
                    for k in range(4):
                        mm = nc.tensor.transpose(banks[half][:, k * P:(k + 1) * P], rows[:, half, k, 0:D],
                                                 s.ident[:, :])
                    mm.then_inc(q.turned, 1)

                over_halves(pe, step)

            @block.scalar
            def _(act):
                def step(i, half, first):
                    act.wait_ge(q.turned, 2 * i + half + 1)
                    if not first:
                        act.wait_ge(stored[half], 16 * i)
                    nc.scalar.copy(x_t[:, half, :], banks[half][:, :]).then_inc(q.copied, 1)

                over_halves(act, step)

            @block.sync
            def _(sp):
                def step(i, half, first):
                    sp.wait_ge(q.copied, 2 * i + half + 1)
                    hold(sp, q.passed)
                    sp.dma_start(turned_x[bass.ds((2 * i + half) * P, P), :], x_t[:, half, :]
                                 ).then_inc(stored[half], 16)

                over_halves(sp, step)
                for half in range(2):
                    sp.wait_ge(stored[half], 16 * ITERS)

            @block.vector
            def _(dve):
                v = nc.vector

                def feed(i, half, first):
                    v.tensor_copy(gidx[:, half, :, :], s.gather_rows[:, bass.ds(8 * i + 4 * half, 4), :]
                                  ).then_inc(q.gidx_ready, 1)

                def step(i, half, last):
                    dve.wait_ge(gathered[half], 128 * i + 128)
                    if not last:
                        feed(i + 1, half, False)
                    t = bass.ds(8 * i + 4 * half, 4)
                    v.tensor_tensor(s.edge_score[:, :, t].rearrange("p h k -> p k h"), rows[:, half, :, D:D + HEADS],
                                    atts[:, half, :, HEADS:2 * HEADS], ALU.add).then_inc(q.scored, 1)
                    v.tensor_copy(s.self_score[:, :, t].rearrange("p h k -> p k h"), atts[:, half, :, 0:HEADS]
                                  ).then_inc(q.scored, 1)

                feed(0, 0, True)
                feed(0, 1, True)
                with dve.Fori(0, ITERS - 1) as i:
                    step(i, 0, False)
                    step(i, 1, False)
                step(ITERS - 1, 0, True)
                step(ITERS - 1, 1, True)


def segment_total(nc, s, name, values, op, chunk, row_bank, col_bank):
    maximum = op == ALU.max
    join = ALU.add if maximum else ALU.mult
    inner = s.reset_in if maximum else s.same_in
    outer = s.reset if maximum else s.same
    chunk_step = s.chunk_reset if maximum else s.chunk_same
    start = -BIG if maximum else 0.0
    scan, ends, incoming, chunk_rows, shifted = chunk
    with phase(nc, name, "step", "turn", "turned") as (block, q):
        @block.vector
        def _(dve):
            v = nc.vector
            steps = Steps(dve, q.step)
            turns = [0]

            def across(edge, step_row, joined, op1, first, backwards):
                steps.then(v.tensor_copy(ends[:, :], edge))
                steps.wait()
                dve.sem_inc(q.turn, 1)
                turns[0] += 1
                dve.wait_ge(q.turned, turns[0])
                steps.then(v.tensor_copy(chunk_rows[:, 0, :], row_bank[0:HEADS, 0:P]))
                steps.then(v.memset(shifted[:, :], first))
                steps.wait()
                if backwards:
                    steps.then(v.tensor_tensor_scan(chunk_rows[:, 1, ::-1], step_row[:, ::-1],
                                                    chunk_rows[:, 0, ::-1], first, joined, op1))
                    steps.wait()
                    steps.then(v.tensor_copy(shifted[:, 0:P - 1], chunk_rows[:, 1, 1:P]))
                else:
                    steps.then(v.tensor_tensor_scan(chunk_rows[:, 1, :], step_row[:, :], chunk_rows[:, 0, :], first,
                                                    joined, op1))
                    steps.wait()
                    steps.then(v.tensor_copy(shifted[:, 1:P], chunk_rows[:, 1, 0:P - 1]))
                steps.wait()
                dve.sem_inc(q.turn, 1)
                turns[0] += 1
                dve.wait_ge(q.turned, turns[0])
                steps.then(v.tensor_copy(incoming[:, :], col_bank[:, 0:HEADS]))
                steps.wait()

            for h in range(HEADS):
                steps.then(v.tensor_tensor_scan(scan[:, h, :], inner[:, :], values[:, h, :], start, join, op))
            steps.wait()
            across(scan[:, :, T - 1], chunk_step, join, op, start, False)
            for h in range(HEADS):
                steps.then(v.tensor_tensor_scan(scan[:, h, :], outer[:, :], values[:, h, :], incoming[:, h:h + 1],
                                                join, op))
            steps.wait()
            for h in range(HEADS):
                steps.then(v.tensor_tensor(scan[:, h, :], scan[:, h, :], s.ends[:, :], ALU.mult))
            steps.wait()
            for h in range(HEADS):
                steps.then(v.tensor_tensor_scan(values[:, h, ::-1], s.goes_on[:, ::-1], scan[:, h, ::-1], 0.0,
                                                ALU.mult, ALU.add))
            steps.wait()
            across(values[:, :, 0], s.chunk_goes_on, ALU.mult, ALU.add, 0.0, True)
            for h in range(HEADS):
                steps.then(v.tensor_tensor_scan(values[:, h, ::-1], s.goes_on[:, ::-1], scan[:, h, ::-1],
                                                incoming[:, h:h + 1], ALU.mult, ALU.add))

        @block.tensor
        def _(pe):
            for n in range(2):
                pe.wait_ge(q.turn, 2 * n + 1)
                nc.tensor.transpose(row_bank[0:HEADS, 0:P], ends[:, :], s.ident[:, :]).then_inc(q.turned, 1)
                pe.wait_ge(q.turn, 2 * n + 2)
                nc.tensor.transpose(col_bank[:, 0:HEADS], shifted[:, :], s.ident[0:HEADS, 0:HEADS]
                                    ).then_inc(q.turned, 1)


def attention_weights(nc, s, layer):
    with ExitStack() as ctx:
        def sb(name, shape, dt=F32):
            return ctx.enter_context(nc.sbuf_tensor(f"{name}_{layer}", shape, dt))

        top = sb("top", [P, HEADS, T])
        chunk = (sb("scan", [P, HEADS, T]), sb("chunk_ends", [P, HEADS]), sb("incoming", [P, HEADS]),
                 sb("chunk_rows", [HEADS, 2, P]), sb("shifted", [HEADS, P]))
        row_bank = ctx.enter_context(nc.psum_tensor(f"row_bank_{layer}", [P, BLOCK], F32))
        col_bank = ctx.enter_context(nc.psum_tensor(f"col_bank_{layer}", [P, BLOCK], F32))
        e, own = s.edge_score, s.self_score

        with phase(nc, f"leaky{layer}", "step") as (block, q):
            @block.vector
            def _(dve):
                v = nc.vector
                v.scalar_tensor_tensor(e[:, :, :], e[:, :, :], SLOPE, e[:, :, :], ALU.mult, ALU.max
                                       ).then_inc(q.step, 1)
                dve.wait_ge(q.step, 1)
                v.tensor_tensor(top[:, :, :], e[:, :, :], own[:, :, :], ALU.max)

        segment_total(nc, s, f"max{layer}", top, ALU.max, chunk, row_bank, col_bank)

        with phase(nc, f"exp{layer}", "shifted", "exped") as (block, q):
            @block.vector
            def _(dve):
                v = nc.vector
                v.tensor_tensor(e[:, :, :], e[:, :, :], top[:, :, :], ALU.subtract).then_inc(q.shifted, 1)
                v.tensor_tensor(own[:, :, :], own[:, :, :], top[:, :, :], ALU.subtract).then_inc(q.shifted, 1)
                dve.wait_ge(q.shifted, 2)
                dve.wait_ge(q.exped, 2)
                v.tensor_copy(top[:, :, :], e[:, :, :])

            @block.scalar
            def _(act):
                act.wait_ge(q.shifted, 2)
                nc.scalar.activation(e[:, :, :], e[:, :, :], ACT.Exp).then_inc(q.exped, 1)
                nc.scalar.activation(own[:, :, :], own[:, :, :], ACT.Exp).then_inc(q.exped, 1)

        segment_total(nc, s, f"sum{layer}", top, ALU.add, chunk, row_bank, col_bank)

        with phase(nc, f"norm{layer}", "step") as (block, q):
            @block.vector
            def _(dve):
                v = nc.vector
                steps = Steps(dve, q.step)
                steps.then(v.tensor_tensor(top[:, :, :], top[:, :, :], own[:, :, :], ALU.add))
                steps.wait()
                steps.then(v.reciprocal(top[:, :, :], top[:, :, :]))
                steps.wait()
                steps.then(v.scalar_tensor_tensor(s.weights[:, 0:HEADS, :], e[:, :, :], 1.0 / HEADS, top[:, :, :],
                                                  ALU.mult, ALU.mult))
                steps.then(v.scalar_tensor_tensor(s.self_weights[:, :, :].rearrange("p t h -> p h t"), own[:, :, :],
                                                  1.0 / HEADS, top[:, :, :], ALU.mult, ALU.mult))
                steps.then(v.tensor_copy(s.weights[:, HEADS, :], s.same_in[:, :]))


def weigh_edges(nc, s, layer, turned_x, sums):
    with ExitStack() as ctx:
        def sb(name, shape, dt=F32):
            return ctx.enter_context(nc.sbuf_tensor(f"{name}_{layer}", shape, dt))

        x_t = sb("edge_t", [P, 2, BLOCK])
        sidx = sb("sidx2", [P, 2, 4], I32)
        weights = sb("weights4", [P, 2, HEADS + 1, 4])
        part = sb("part", [P, 2, 2, D])
        rows = sb("sum_rows", [P, 2, 4, W])
        banks = [ctx.enter_context(nc.psum_tensor(f"heads{b}_{layer}", [P, BLOCK], F32)) for b in range(4)]

        with phase(nc, f"weigh_init{layer}", "x") as (block, q):
            @block.vector
            def _(dve):
                nc.vector.memset(rows[:, :, :, :], 0.0).then_inc(q.x, 1)
                dve.wait_ge(q.x, 1)
                nc.vector.memset(rows[:, :, :, D + HEADS:D + HEADS + 1], 1.0)

        with phase(nc, f"weigh{layer}", "loaded_a", "loaded_b", "fed", "headed", "first_head", "step", "row_ready",
                   "extras_ready", "stored_a", "stored_b", "passed") as (block, q):
            loaded = [q.loaded_a, q.loaded_b]
            stored = [q.stored_a, q.stored_b]

            def over_halves(eng, step):
                step(0, 0, True)
                step(0, 1, True)
                with eng.Fori(1, ITERS) as i:
                    step(i, 0, False)
                    step(i, 1, False)

            @block.sync
            def _(sp):
                def step(i, half, first):
                    if not first:
                        sp.wait_ge(q.headed, 4 * (2 * i + half - 1))
                        hold(sp, q.passed)
                    sp.dma_start(x_t[:, half, :], turned_x[bass.ds((2 * i + half) * P, P), :]
                                 ).then_inc(loaded[half], 16)

                over_halves(sp, step)

            @block.tensor
            def _(pe):
                def step(i, half, first):
                    pe.wait_ge(loaded[half], 16 * i + 16)
                    for k in range(4):
                        n = 8 * i + 4 * half + k
                        if not (first and half == 0):
                            pe.wait_ge(q.step, 3 * (n - 3))
                        nc.tensor.matmul(banks[k][:, :], x_t[:, half, k * P:(k + 1) * P], s.gat_w[:, layer, :],
                                         start=True, stop=True).then_inc(q.headed, 1)

                over_halves(pe, step)

            @block.scalar
            def _(act):
                def step(i, half, first):
                    act.wait_ge(q.fed, 4 * i + 2 * half + 2)
                    if not first:
                        act.wait_ge(stored[half], 64 * i)
                    t0 = 8 * i + 4 * half
                    nc.scalar.copy(rows[:, half, :, D:D + HEADS], s.self_weights[:, bass.ds(t0, 4), :]
                                   ).then_inc(q.extras_ready, 1)
                    for k in range(4):
                        n = t0 + k
                        act.wait_ge(q.headed, n + 1)
                        if not (first and half == 0 and k < 2):
                            act.wait_ge(q.step, 3 * (n - 1))
                        nc.scalar.activation(part[:, k % 2, 0, :], banks[k][:, 0:D], ACT.Copy,
                                             scale=weights[:, half, 0, k:k + 1]).then_inc(q.first_head, 1)

                over_halves(act, step)

            @block.vector
            def _(dve):
                v = nc.vector

                def step(i, half, first):
                    t0 = 8 * i + 4 * half
                    if not first:
                        dve.wait_ge(q.first_head, t0 - 4)
                        dve.wait_ge(q.row_ready, t0 - 4)
                        dve.wait_ge(stored[half], 64 * i)
                    v.tensor_copy(weights[:, half, :, :], s.weights[:, :, bass.ds(t0, 4)]).then_inc(q.fed, 1)
                    v.tensor_copy(sidx[:, half, :], s.scatter_rows[:, bass.ds(t0, 4)]).then_inc(q.fed, 1)
                    dve.wait_ge(q.fed, 4 * i + 2 * half + 2)
                    for k in range(4):
                        n = t0 + k
                        dve.wait_ge(q.first_head, n + 1)
                        src = part[:, k % 2, 0, :]
                        for h in range(1, HEADS):
                            dst = part[:, k % 2, 1, :]
                            if h > 1:
                                dve.wait_ge(q.step, 3 * n + h - 1)
                            elif not (first and half == 0 and k < 2):
                                dve.wait_ge(q.row_ready, n - 1)
                            v.scalar_tensor_tensor(dst, banks[k][:, h * D:(h + 1) * D],
                                                   weights[:, half, h, k:k + 1], src, ALU.mult, ALU.add
                                                   ).then_inc(q.step, 1)
                            src = dst
                        dve.wait_ge(q.step, 3 * n + 3)
                        if not (first and half == 0 and k == 0):
                            dve.wait_ge(q.row_ready, n)
                        before = rows[:, half, k - 1, 0:D] if k else rows[:, 1 - half, 3, 0:D]
                        v.scalar_tensor_tensor(rows[:, half, k, 0:D], before, weights[:, half, HEADS, k:k + 1],
                                               part[:, k % 2, 1, :], ALU.mult, ALU.add).then_inc(q.row_ready, 1)

                over_halves(dve, step)

            @block.gpsimd
            def _(pool):
                def step(i, half, first):
                    pool.wait_ge(q.extras_ready, 2 * i + half + 1)
                    pool.wait_ge(q.fed, 4 * i + 2 * half + 2)
                    for k in range(4):
                        pool.wait_ge(q.row_ready, 8 * i + 4 * half + k + 1)
                        hold(pool, q.passed)
                        pool.indirect_dma_start(sums[:, :], bass.IndirectOffsetOnAxis(ap=sidx[:, half, k:k + 1],
                                                                                      axis=0),
                                                rows[:, half, k, :], None, bounds_check=ROWS - 1, oob_is_err=False
                                                ).then_inc(stored[half], 16)

                over_halves(pool, step)
                for half in range(2):
                    pool.wait_ge(stored[half], 64 * ITERS)

        fixup(nc, s, f"weigh_fix{layer}", sums, rows[:, 1, 3, :], D, banks)


def gat_nodes(nc, s, layer, x_rows, sums, x_next, att_next, x_first, out):
    last = layer == LAYERS - 1
    with ExitStack() as ctx:
        def sb(name, shape, dt=F32):
            return ctx.enter_context(nc.sbuf_tensor(f"{name}_{layer}", shape, dt))

        def pb(name, shape):
            return ctx.enter_context(nc.psum_tensor(f"{name}_{layer}", shape, F32))

        xs = sb("gx", [P, 2, 4, D + HEADS])
        ss = sb("gs", [P, 2, 4, W])
        firsts = sb("gf", [P, 2, 4, D + HEADS])
        own = sb("own", [P, 2, 4, HEADS])
        y = sb("y", [P, 2, 4, D])
        x_t = sb("gx_t", [P, 2, BLOCK])
        y_t = sb("gy_t", [P, BLOCK])
        base = sb("gbase", [P, 2, 4, D])
        total = sb("gtotal", [P, 2, 4, D])
        new = sb("gnew", [P, 2, 4, D + HEADS])
        new_t = sb("gnew_t", [P, BLOCK])
        node_att = sb("gatt", [P, 2, 4, 2 * HEADS])
        stats = sb("gstats", [P, 4, 6])
        moments = sb("gmoments", [P, 4, 2])
        rstd = sb("grstd", [P, 4])
        p_x = pb("gp_x", [P, BLOCK])
        heads = [pb(f"gp_h{c}", [P, BLOCK]) for c in range(4)]
        p_y = pb("gp_y", [P, BLOCK])
        p_skip = pb("gp_skip", [P, 4, D])
        p_tail = pb("gp_tail", [P, BLOCK])
        n_loads = 3 if last else 2
        own_steps = 2
        done_steps = 1 + (1 + NORM_STEPS if last else 1)
        stores = 1 if last else 2

        with phase(nc, f"gat{layer}", "loaded_a", "loaded_b", "turned", "copied", "y_base", "own_step", "headed",
                   "summed", "y_turned", "y_copied", "base_ready", "skipped", "step", "rows_turned", "rows_copied",
                   "scored", "tail_step", "stored_a", "stored_b", "passed", "rstd_ready") as (block, q):
            loaded = [q.loaded_a, q.loaded_b]
            stored = [q.stored_a, q.stored_b]

            @block.sync
            def _(sp):
                def step(j, slot, start, first):
                    if not first:
                        sp.wait_ge(q.turned, j - 1)
                        sp.wait_ge(q.y_base, j - 1)
                        hold(sp, q.passed)
                        sp.wait_ge(q.own_step, own_steps * (j - 1))
                        if last:
                            hold(sp, q.passed)
                            sp.wait_ge(q.step, done_steps * (j - 1))
                        hold(sp, q.passed)
                    sp.dma_start(xs[:, slot, :, :], nodes_of(x_rows, start)).then_inc(loaded[slot], 16)
                    sp.dma_start(ss[:, slot, :, :], nodes_of(sums, start)).then_inc(loaded[slot], 16)
                    if last:
                        sp.dma_start(firsts[:, slot, :, :], nodes_of(x_first, start)).then_inc(loaded[slot], 16)

                over_blocks(sp, step)

            @block.gpsimd
            def _(pool):
                def store(j, slot, start):
                    if not last:
                        store_rows(pool, q, stored, new, node_att, x_next, att_next, j, slot, start)
                        return
                    pool.wait_ge(q.step, done_steps * (j + 1))
                    if isinstance(j, int) and j == NBLOCKS - 1:
                        pool.wait_ge(stored[0], 8 * NBLOCKS)
                        pool.wait_ge(stored[1], 8 * (NBLOCKS - 2))
                    pool.dma_start(nodes_of(out, start), y_out(slot)).then_inc(stored[slot], 16)

                def y_out(slot):
                    return total[:, slot]

                def step(j, slot, start, first):
                    loads_done(pool, loaded[slot], j, slot, n_loads)
                    if not first:
                        pool.wait_ge(q.base_ready, j - 1)
                        pool.wait_ge(q.y_turned, j - 1)
                    nc.gpsimd.tensor_tensor(y[:, slot], ss[:, slot, :, 0:D], over_features(s.gat_b[:, layer, :]),
                                            ALU.add).then_inc(q.y_base, 1)
                    pool.wait_ge(q.summed, 16 * j + 16)
                    if not first:
                        pool.wait_ge(q.step, done_steps * (j - 2) + 1)
                    nc.gpsimd.tensor_tensor(base[:, slot], y[:, slot], over_features(s.skip_b[:, layer, :]), ALU.add
                                            ).then_inc(q.base_ready, 1)
                    if not (first and slot == 0):
                        before = (NBLOCKS - 2) * BLOCK if isinstance(j, int) and j == NBLOCKS - 1 else start - BLOCK
                        store(j - 1, 1 - slot, before)

                over_blocks(pool, step)
                store(NBLOCKS - 1, 1, N - BLOCK)
                for slot in range(2):
                    pool.wait_ge(stored[slot], 8 * stores * NBLOCKS)

            @block.tensor
            def _(pe):
                def tail(j, slot):
                    pe.wait_ge(q.step, done_steps * (j + 1))
                    if not (isinstance(j, int) and j == 0):
                        pe.wait_ge(q.tail_step, HEAD_STEPS * j)
                    for c in range(4):
                        mm = nc.tensor.transpose(p_tail[:, c * P:(c + 1) * P], new[:, slot, c, 0:D], s.ident[:, :])
                    mm.then_inc(q.rows_turned, 1)
                    pe.wait_ge(q.rows_copied, j + 1)
                    for c in range(4):
                        mm = nc.tensor.matmul(p_tail[:, c * 8:c * 8 + 8], new_t[:, c * P:(c + 1) * P],
                                              s.w_att[:, layer + 1, :], start=True, stop=True)
                    mm.then_inc(q.scored, 1)

                def step(j, slot, start, first):
                    very_first = first and slot == 0
                    loads_done(pe, loaded[slot], j, slot, n_loads)
                    if not very_first:
                        pe.wait_ge(q.copied, j)
                    for c in range(4):
                        mm = nc.tensor.transpose(p_x[:, c * P:(c + 1) * P], xs[:, slot, c, 0:D], s.ident[:, :])
                    mm.then_inc(q.turned, 1)
                    pe.wait_ge(q.copied, j + 1)
                    for c in range(4):
                        if not very_first:
                            pe.wait_ge(q.summed, 16 * (j - 1) + 4 * c + 4)
                        nc.tensor.matmul(heads[c][:, :], x_t[:, slot, c * P:(c + 1) * P], s.gat_w[:, layer, :],
                                         start=True, stop=True).then_inc(q.headed, 1)
                    if not last and not very_first:
                        tail(j - 1, 1 - slot)
                    pe.wait_ge(q.summed, 16 * j + 16)
                    if not very_first:
                        pe.wait_ge(q.y_copied, j)
                    for c in range(4):
                        mm = nc.tensor.transpose(p_y[:, c * P:(c + 1) * P], y[:, slot, c, :], s.ident[:, :])
                    mm.then_inc(q.y_turned, 1)
                    pe.wait_ge(q.y_copied, j + 1)
                    if not very_first:
                        pe.wait_ge(q.step, done_steps * (j - 1) + 1)
                    for c in range(4):
                        mm = nc.tensor.matmul(p_skip[:, c, :], y_t[:, c * P:(c + 1) * P], s.skip_w[:, layer, :],
                                              start=True, stop=True)
                    mm.then_inc(q.skipped, 1)

                over_blocks(pe, step)
                if not last:
                    tail(NBLOCKS - 1, 1)

            @block.scalar
            def _(act):
                def copy_rows(j):
                    act.wait_ge(q.rows_turned, j + 1)
                    if not (isinstance(j, int) and j == 0):
                        act.wait_ge(q.scored, j)
                    nc.scalar.copy(new_t[:, :], p_tail[:, :]).then_inc(q.rows_copied, 1)

                def step(j, slot, start, first):
                    very_first = first and slot == 0
                    act.wait_ge(q.turned, j + 1)
                    if not first:
                        act.wait_ge(q.headed, 4 * (j - 1))
                    nc.scalar.copy(x_t[:, slot, :], p_x[:, :]).then_inc(q.copied, 1)
                    if last and not very_first:
                        deviation(nc, s, q, act, moments, rstd, done_steps * (j - 1) + 2, j - 1)
                    elif not very_first:
                        copy_rows(j - 1)
                    act.wait_ge(q.y_turned, j + 1)
                    if not very_first:
                        act.wait_ge(q.skipped, j)
                    nc.scalar.copy(y_t[:, :], p_y[:, :]).then_inc(q.y_copied, 1)

                over_blocks(act, step)
                if last:
                    deviation(nc, s, q, act, moments, rstd, done_steps * (NBLOCKS - 1) + 2, NBLOCKS - 1)
                else:
                    copy_rows(NBLOCKS - 1)

            @block.vector
            def _(dve):
                v = nc.vector

                def tail(j, slot):
                    dve.wait_ge(q.scored, j + 1)
                    steps = Steps(dve, q.tail_step, HEAD_STEPS * j)
                    head_rows(nc, s, steps, p_tail[:, 0:32].rearrange("p (c k) -> p c k", c=4), new, node_att, slot)

                def step(j, slot, start, first):
                    very_first = first and slot == 0
                    loads_done(dve, loaded[slot], j, slot, n_loads)
                    if not first:
                        dve.wait_ge(q.summed, 16 * (j - 1))
                    flag = ss[:, slot, :, D + HEADS:D + HEADS + 1].to_broadcast([P, 4, HEADS])
                    v.tensor_scalar(own[:, slot], flag, -1.0 / HEADS, 1.0 / HEADS, ALU.mult, ALU.add
                                    ).then_inc(q.own_step, 1)
                    dve.wait_ge(q.own_step, own_steps * j + 1)
                    v.tensor_tensor(own[:, slot], own[:, slot], ss[:, slot, :, D:D + HEADS], ALU.add
                                    ).then_inc(q.own_step, 1)
                    dve.wait_ge(q.own_step, own_steps * j + 2)
                    dve.wait_ge(q.y_base, j + 1)
                    for c in range(4):
                        dve.wait_ge(q.headed, 4 * j + c + 1)
                        for h in range(HEADS):
                            if h:
                                dve.wait_ge(q.summed, 16 * j + 4 * c + h)
                            v.scalar_tensor_tensor(y[:, slot, c, :], heads[c][:, h * D:(h + 1) * D],
                                                   own[:, slot, c, h:h + 1], y[:, slot, c, :], ALU.mult, ALU.add
                                                   ).then_inc(q.summed, 1)
                    if not last and not very_first:
                        tail(j - 1, 1 - slot)
                    dve.wait_ge(q.skipped, j + 1)
                    dve.wait_ge(q.base_ready, j + 1)
                    if last and not first:
                        dve.wait_ge(stored[slot], 8 * (j - slot))
                    steps = Steps(dve, q.step, done_steps * j)
                    steps.then(v.tensor_tensor(total[:, slot], base[:, slot], p_skip[:, :, :], ALU.add))
                    steps.wait()
                    if last:
                        steps.then(v.tensor_tensor(base[:, slot], total[:, slot], firsts[:, slot, :, 0:D], ALU.add))
                        steps.wait()
                        layernorm(nc, q, steps, base[:, slot], total[:, slot], stats, moments, rstd, j)
                    else:
                        if not first:
                            dve.wait_ge(stored[slot], 16 * (j - slot))
                        steps.then(v.tensor_scalar(new[:, slot, :, 0:D], total[:, slot], 0.0, None, ALU.max))

                over_blocks(dve, step)
                if not last:
                    tail(NBLOCKS - 1, 1)


def build(nc, x, src, dst, w, out):
    def dram(name, shape, dt=F32):
        return nc.dram_tensor(name, shape, dt).ap()

    half_sorted = dram("half_sorted", (SLOTS, 2), I32)
    sorted_pairs = dram("sorted_pairs", (SLOTS, 2), I32)
    sums_in = dram("sums_in", (ROWS, W))
    sums_out = dram("sums_out", (ROWS, W))
    turned_x = dram("turned_x", (HALVES * P, BLOCK))
    x_rows = [dram(f"x_rows{l}", (N, D + HEADS)) for l in range(LAYERS)]
    att_rows = [dram(f"att_rows{l}", (N, 2 * HEADS)) for l in range(LAYERS)]

    with ExitStack() as ctx:
        def sb(name, shape, dt=F32):
            return ctx.enter_context(nc.sbuf_tensor(name, shape, dt))

        s = Buffers()
        s.ident = sb("ident", [P, P])
        s.lower = sb("lower", [P, P])
        s.upper = sb("upper", [P, P])
        s.upper_in = sb("upper_in", [P, P])
        s.lower_in = sb("lower_in", [P, P])
        s.ones = sb("ones", [P, P])
        s.eps = sb("eps", [P, 1])
        s.iota256 = sb("iota256", [P, 256])
        s.dummy = sb("dummy_row", [P, 1])
        s.upper_b = sb("upper_b", [P, P], BF16)
        s.lower_in_b = sb("lower_in_b", [P, P], BF16)
        s.ones_b = sb("ones_b", [P, P], BF16)
        s.iota256_b = sb("iota256_b", [P, 256], BF16)
        s.pairs = sb("pairs", [P, T, 2], I32)
        s.source = sb("source", [P, T])
        s.gather_rows = sb("gather_rows", [P, T, 2], I32)
        s.scatter_rows = sb("scatter_rows", [P, T], I32)
        s.same = sb("same", [P, T])
        s.same_in = sb("same_in", [P, T])
        s.reset = sb("reset", [P, T])
        s.reset_in = sb("reset_in", [P, T])
        s.ends = sb("ends", [P, T])
        s.goes_on = sb("goes_on", [P, T])
        s.fix_rows = sb("fix_rows", [P, 2], I32)
        s.mask_first = sb("mask_first", [P, P])
        s.mask_last = sb("mask_last", [P, P])
        s.chunk_same = sb("chunk_same", [HEADS, P])
        s.chunk_goes_on = sb("chunk_goes_on", [HEADS, P])
        s.chunk_reset = sb("chunk_reset", [HEADS, P])
        s.w_edge = sb("w_edge", [P, 2, 2 * D])
        s.w_msg2 = sb("w_msg2", [P, 2, D])
        s.b_edge = sb("b_edge", [P, 2 * D])
        s.b_msg2 = sb("b_msg2", [2, D])
        s.upd1 = sb("upd1", [P, 2, U])
        s.upd2 = sb("upd2", [P, 2, D])
        s.upd_b1 = sb("upd_b1", [P, 2])
        s.upd_b2 = sb("upd_b2", [P, D])
        s.gat_w = sb("gat_w", [P, LAYERS, HEADS * D])
        s.gat_b = sb("gat_b", [P, LAYERS, D])
        s.skip_w = sb("skip_w", [P, LAYERS, D])
        s.skip_b = sb("skip_b", [P, LAYERS, D])
        s.w_att = sb("w_att", [P, LAYERS, 2 * HEADS])
        make_constants(nc, s)
        zero_tables(nc, (sums_in, sums_out))
        load_weights(nc, s, w)
        with ExitStack() as sorting:
            def tmp(name, shape, dt=F32):
                return sorting.enter_context(nc.sbuf_tensor(name, shape, dt))

            s.digit_i, s.digits = tmp("digit_i", [P, T], I32), tmp("digits", [P, T])
            s.totals, s.base = tmp("totals", [P, 256]), tmp("base", [P, 256])
            s.picked, s.rank_ring = tmp("picked", [P, 256]), tmp("rank_ring", [P, 8])
            s.ranks, s.place = tmp("ranks", [P, T]), tmp("place", [P, T], I32)
            s.place_hi, s.place_ring = tmp("place_hi", [P, T], I32), tmp("place_ring", [P, 2, 4], I32)
            s.pair_ring = tmp("pair_ring", [P, 2, 4, 2], I32)
            sort_edges(nc, s, src, dst, half_sorted, sorted_pairs)
        plan_segments(nc, s, sorted_pairs)
        message_edges(nc, s, x, sums_in, sums_out)
        update_nodes(nc, s, x, sums_in, sums_out, x_rows[0], att_rows[0])
        for layer in range(LAYERS):
            with nc.sbuf_tensor(f"edge_weights{layer}", [P, HEADS + 1, T], F32) as weights, \
                    nc.sbuf_tensor(f"self_weights{layer}", [P, T, HEADS], F32) as self_weights:
                s.weights, s.self_weights = weights, self_weights
                with nc.sbuf_tensor(f"edge_score{layer}", [P, HEADS, T], F32) as edge_score, \
                        nc.sbuf_tensor(f"self_score{layer}", [P, HEADS, T], F32) as self_score:
                    s.edge_score, s.self_score = edge_score, self_score
                    score_edges(nc, s, layer, x_rows[layer], att_rows[layer], turned_x)
                    attention_weights(nc, s, layer)
                weigh_edges(nc, s, layer, turned_x, sums_in)
            after = min(layer + 1, LAYERS - 1)
            gat_nodes(nc, s, layer, x_rows[layer], sums_in, x_rows[after], att_rows[after], x_rows[0], out)


_INS = ["x", "src", "dst", "L0_gnn_msg_W1", "L0_gnn_msg_b1", "L0_gnn_msg_W2", "L0_gnn_msg_b2", "L0_gnn_rev_W1",
        "L0_gnn_rev_b1", "L0_gnn_rev_W2", "L0_gnn_rev_b2", "L0_gnn_upd_W1", "L0_gnn_upd_b1", "L0_gnn_upd_W2",
        "L0_gnn_upd_b2", "L1_gnn_W", "L1_gnn_att_src", "L1_gnn_att_dst", "L1_gnn_bias", "L1_gnn_skip_W",
        "L1_gnn_skip_b"]


def program(nc, shapes):
    args = {name: nc.dram_tensor(f"in_{name}", shape, dt, kind="ExternalInput").ap()
            for name, (shape, dt) in shapes.items()}
    out = nc.dram_tensor("out", (N, D), F32, kind="ExternalOutput").ap()
    w = {name[7:]: ap for name, ap in args.items() if name.startswith("L0_gnn_")}
    w |= {"gat_W": args["L1_gnn_W"], "gat_bias": args["L1_gnn_bias"], "skip_W": args["L1_gnn_skip_W"],
          "skip_b": args["L1_gnn_skip_b"], "att_src": args["L1_gnn_att_src"], "att_dst": args["L1_gnn_att_dst"]}
    build(nc, args["x"], args["src"], args["dst"], w, out)


def kernel(**inputs):
    import numpy as np
    import concourse.bacc as bacc
    from concourse.bass_utils import run_bass_kernel_spmd

    nc = bacc.Bacc("TRN2", target_bir_lowering=False, num_devices=1)
    arrays = {name: np.ascontiguousarray(inputs[name]) for name in _INS}
    program(nc, {name: (a.shape, mybir.dt.from_np(a.dtype)) for name, a in arrays.items()})
    r = run_bass_kernel_spmd(nc, [{f"in_{name}": a for name, a in arrays.items()}], core_ids=[0])
    return r.results[0]["out"]
```

```python
from collections import namedtuple
from contextlib import ExitStack, contextmanager

import concourse.bass as bass
from concourse import mybir

ALU = mybir.AluOpType
ACT = mybir.ActivationFunctionType
AX = mybir.AxisListType
F32 = mybir.dt.float32
BF16 = mybir.dt.bfloat16
I32 = mybir.dt.int32

P = 128
N = 50000
E = 50000
D = 128
U = 256
HEADS = 4
LAYERS = 3
T = -(-E // (P * 8)) * 8
SLOTS = P * T
HALVES = T // 4
ITERS = T // 8
W = 136
SIDE = SLOTS
ROWS = SLOTS + P
SKIP = float(1 << 20)
BLOCK = 512
NBLOCKS = -(-N // BLOCK)
BIG = 1.0e30
EPS = 1e-05
SLOPE = 0.2


@contextmanager
def phase(nc, name, *signals):
    sems = namedtuple("Signals", signals)(*[nc.alloc_semaphore(f"{name}_{s}") for s in signals])
    with nc.Block() as block:
        yield block, sems
    nc.clear_and_free_semaphores(list(sems))
    nc.all_engine_barrier()


class Buffers:
    pass


class Steps:

    def __init__(self, eng, sem, start=0, passed=None):
        self.eng, self.sem, self.n, self.passed = eng, sem, start, passed

    def then(self, ins):
        ins.then_inc(self.sem, 1)
        self.n = self.n + 1

    def wait(self):
        self.eng.wait_ge(self.sem, self.n)


def hold(eng, passed):
    eng.sem_inc(passed, 1)


def row_of(v):
    return v.rearrange("(a d) -> a d", a=1)


def make_constants(nc, s):
    with phase(nc, "const", "filled", "made") as (block, q):
        @block.gpsimd
        def _(pool):
            nc.gpsimd.memset(s.ident[:, :], 0.0).then_inc(q.filled, 1)
            nc.gpsimd.memset(s.lower[:, :], 1.0).then_inc(q.filled, 1)
            nc.gpsimd.memset(s.upper[:, :], 1.0).then_inc(q.filled, 1)
            nc.gpsimd.memset(s.upper_in[:, :], 1.0).then_inc(q.filled, 1)
            nc.gpsimd.memset(s.lower_in[:, :], 1.0).then_inc(q.filled, 1)
            nc.gpsimd.memset(s.ones[:, :], 1.0).then_inc(q.filled, 1)
            nc.gpsimd.memset(s.eps[:, :], EPS)
            nc.gpsimd.iota(s.iota256[:, :], [[1, 256]], base=0, channel_multiplier=0,
                           allow_small_or_imprecise_dtypes=True).then_inc(q.filled, 1)
            nc.gpsimd.iota(s.dummy[:, :], [[0, 1]], base=SIDE, channel_multiplier=1,
                           allow_small_or_imprecise_dtypes=True).then_inc(q.filled, 1)
            pool.wait_ge(q.filled, 8)
            nc.gpsimd.affine_select(out=s.ident[:, :], in_=s.ident[:, :], compare_op=ALU.not_equal, fill=1.0,
                                    base=0, pattern=[[-1, P]], channel_multiplier=1).then_inc(q.made, 1)
            nc.gpsimd.affine_select(out=s.lower[:, :], in_=s.lower[:, :], compare_op=ALU.is_gt, fill=0.0,
                                    base=0, pattern=[[-1, P]], channel_multiplier=1).then_inc(q.made, 1)
            nc.gpsimd.affine_select(out=s.upper[:, :], in_=s.upper[:, :], compare_op=ALU.is_gt, fill=0.0,
                                    base=0, pattern=[[1, P]], channel_multiplier=-1).then_inc(q.made, 1)
            nc.gpsimd.affine_select(out=s.upper_in[:, :], in_=s.upper_in[:, :], compare_op=ALU.is_ge, fill=0.0,
                                    base=0, pattern=[[1, P]], channel_multiplier=-1).then_inc(q.made, 1)
            nc.gpsimd.affine_select(out=s.lower_in[:, :], in_=s.lower_in[:, :], compare_op=ALU.is_ge, fill=0.0,
                                    base=0, pattern=[[-1, P]], channel_multiplier=1).then_inc(q.made, 1)

        @block.vector
        def _(dve):
            dve.wait_ge(q.made, 5)
            nc.vector.tensor_copy(s.upper_b[:, :], s.upper[:, :])
            nc.vector.tensor_copy(s.lower_in_b[:, :], s.lower_in[:, :])
            nc.vector.tensor_copy(s.ones_b[:, :], s.ones[:, :])
            nc.vector.tensor_copy(s.iota256_b[:, :], s.iota256[:, :])


def zero_tables(nc, tables):
    part = 131
    with nc.sbuf_tensor("zeros", [P, part * W], F32) as zeros:
        with phase(nc, "zero", "cleared", "stored") as (block, q):
            @block.vector
            def _(dve):
                nc.vector.memset(zeros[:, :], 0.0).then_inc(q.cleared, 1)

            @block.sync
            def _(sp):
                sp.wait_ge(q.cleared, 1)
                n = 0
                for table in tables:
                    rows = table.rearrange("(p r) w -> p (r w)", p=P)
                    for c in range(ROWS // P // part):
                        sp.dma_start(rows[:, c * part * W:(c + 1) * part * W], zeros[:, :]).then_inc(q.stored, 16)
                        n += 1
                sp.wait_ge(q.stored, 16 * n)


def load_edges(nc, s, src, dst):
    whole = E // T
    rest = E - whole * T
    with nc.sbuf_tensor("keys_in", [P, T], I32) as keys, nc.sbuf_tensor("srcs_in", [P, T], I32) as srcs:
        with phase(nc, "edges", "padded", "loaded") as (block, q):
            @block.vector
            def _(dve):
                nc.vector.memset(keys[:, :], N).then_inc(q.padded, 1)
                nc.vector.memset(srcs[:, :], N).then_inc(q.padded, 1)
                dve.wait_ge(q.loaded, 64)
                nc.vector.tensor_copy(s.pairs[:, :, 0], keys[:, :])
                nc.vector.tensor_copy(s.pairs[:, :, 1], srcs[:, :])

            @block.sync
            def _(sp):
                sp.wait_ge(q.padded, 2)
                for sb, dram in ((keys, dst), (srcs, src)):
                    sp.dma_start(sb[0:whole, :], dram[0:whole * T].rearrange("(p t) -> p t", t=T)
                                 ).then_inc(q.loaded, 16)
                    sp.dma_start(sb[whole:whole + 1, 0:rest], row_of(dram[whole * T:E])).then_inc(q.loaded, 16)


def split_digit(nc, s, which):
    with phase(nc, f"digit{which}", "split") as (block, q):
        @block.vector
        def _(dve):
            op, by = (ALU.bitwise_and, 255) if which == 0 else (ALU.logical_shift_right, 8)
            nc.vector.tensor_scalar(s.digit_i[:, :], s.pairs[:, :, 0], by, None, op).then_inc(q.split, 1)
            dve.wait_ge(q.split, 1)
            nc.vector.tensor_copy(s.digits[:, :], s.digit_i[:, :])


def histogram(nc, s, which, counts, onehot):
    with phase(nc, f"hist{which}", "onehot_ready", "counted", "step") as (block, q):
        @block.vector
        def _(dve):
            def tile(i, k, first):
                n = i * 8 + k
                if not first or k >= 4:
                    dve.wait_ge(q.counted, n - 3)
                nc.vector.tensor_scalar(onehot[:, k % 4, :], s.iota256_b[:, :], s.digits[:, bass.ds(n, 1)], None,
                                        ALU.is_equal).then_inc(q.onehot_ready, 1)

            for k in range(8):
                tile(0, k, True)
            with dve.Fori(1, ITERS) as i:
                for k in range(8):
                    tile(i, k, False)
            dve.wait_ge(q.counted, T)
            nc.vector.tensor_copy(s.totals[:, :], counts[:, 0:256]).then_inc(q.step, 1)
            dve.wait_ge(q.step, 1)
            nc.vector.tensor_tensor_scan(s.base[:, :], s.totals[:, :], s.totals[:, :], 0.0, ALU.add,
                                         ALU.bypass).then_inc(q.step, 1)
            dve.wait_ge(q.step, 2)
            nc.vector.tensor_tensor(s.base[:, :], s.base[:, :], s.totals[:, :], ALU.subtract)

        @block.tensor
        def _(pe):
            def tile(n, k, first):
                pe.wait_ge(q.onehot_ready, n + 1)
                nc.tensor.matmul(counts[:, 0:256], s.ones_b[:, :], onehot[:, k % 4, :], start=first, stop=True,
                                 skip_group_check=True).then_inc(q.counted, 1)

            for k in range(8):
                tile(k, k, k == 0)
            with pe.Fori(1, ITERS) as i:
                for k in range(8):
                    tile(i * 8 + k, k, False)


def rank_edges(nc, s, which, counts, onehot):
    with phase(nc, f"rank{which}", "onehot_ready", "summed", "ranked", "advanced", "kept", "done") as (block, q):
        @block.vector
        def _(dve):
            def build(n, k, wait):
                if wait:
                    dve.wait_ge(q.advanced, n - 1)
                nc.vector.tensor_scalar(onehot[:, k % 2, :], s.iota256_b[:, :], s.digits[:, bass.ds(n, 1)], None,
                                        ALU.is_equal).then_inc(q.onehot_ready, 1)

            def block_of(i, first, last):
                for k in range(8):
                    n = i * 8 + k
                    if not (last and k == 7):
                        build(n + 1, k + 1, wait=not (first and k == 0))
                    dve.wait_ge(q.summed, n + 1)
                    if k == 0 and not first:
                        dve.wait_ge(q.kept, i)
                    if not (first and k == 0):
                        dve.wait_ge(q.ranked, n)
                    nc.vector.tensor_tensor_reduce(s.picked[:, :], counts[:, 0:256], onehot[:, k % 2, :], 1.0, 0.0,
                                                   ALU.mult, ALU.add, s.rank_ring[:, k:k + 1]).then_inc(q.ranked, 1)

            build(0, 0, wait=False)
            block_of(0, True, False)
            with dve.Fori(1, ITERS - 1) as i:
                block_of(i, False, False)
            block_of(ITERS - 1, False, True)

        @block.tensor
        def _(pe):
            def tile(n, k):
                pe.wait_ge(q.onehot_ready, n + 1)
                nc.tensor.matmul(counts[:, 0:256], s.upper_b[:, :], onehot[:, k % 2, :], start=False, stop=True,
                                 skip_group_check=True).then_inc(q.summed, 1)
                pe.wait_ge(q.ranked, n + 1)
                nc.tensor.matmul(counts[:, 0:256], s.lower_in_b[:, :], onehot[:, k % 2, :], start=False, stop=True,
                                 skip_group_check=True).then_inc(q.advanced, 1)

            nc.tensor.matmul(counts[:, 0:256], s.ident[:, :], s.base[:, :], start=True, stop=True,
                             skip_group_check=True)
            with pe.Fori(0, ITERS) as i:
                for k in range(8):
                    tile(i * 8 + k, k)

        @block.scalar
        def _(act):
            with act.Fori(0, ITERS) as i:
                act.wait_ge(q.ranked, i * 8 + 8)
                nc.scalar.copy(s.ranks[:, bass.ds(i * 8, 8)], s.rank_ring[:, :]).then_inc(q.kept, 1)


def place_edges(nc, s, which, out):
    with phase(nc, f"place{which}", "step", "ready", "stored_a", "stored_b", "passed") as (block, q):
        stored = [q.stored_a, q.stored_b]

        @block.vector
        def _(dve):
            steps = Steps(dve, q.step)
            steps.then(nc.vector.tensor_copy(s.place[:, :], s.ranks[:, :]))
            steps.wait()
            if which == 0:
                steps.then(nc.vector.tensor_scalar(s.digit_i[:, :], s.place[:, :], 127, None, ALU.bitwise_and))
                steps.then(nc.vector.tensor_scalar(s.place_hi[:, :], s.place[:, :], 7, None,
                                                   ALU.logical_shift_right))
                steps.wait()
                steps.then(nc.vector.scalar_tensor_tensor(s.place[:, :], s.digit_i[:, :], float(T),
                                                          s.place_hi[:, :], ALU.mult, ALU.add))
                steps.wait()

            def feed(i, half, wait):
                t0 = i * 8 + half * 4
                if wait:
                    dve.wait_ge(stored[half], i * 64)
                nc.vector.tensor_copy(s.place_ring[:, half, :], s.place[:, bass.ds(t0, 4)]).then_inc(q.ready, 1)
                nc.vector.tensor_copy(s.pair_ring[:, half, :, :], s.pairs[:, bass.ds(t0, 4), :]).then_inc(q.ready, 1)

            feed(0, 0, False)
            feed(0, 1, False)
            with dve.Fori(1, ITERS) as i:
                feed(i, 0, True)
                feed(i, 1, True)

        @block.gpsimd
        def _(pool):
            with pool.Fori(0, ITERS) as i:
                for half in range(2):
                    pool.wait_ge(q.ready, i * 4 + half * 2 + 2)
                    hold(pool, q.passed)
                    for k in range(4):
                        pool.indirect_dma_start(
                            out[:, :], bass.IndirectOffsetOnAxis(ap=s.place_ring[:, half, k:k + 1], axis=0),
                            s.pair_ring[:, half, k, :], None).then_inc(stored[half], 16)
            for half in range(2):
                pool.wait_ge(stored[half], ITERS * 64)


def reload_pairs(nc, s, table):
    with phase(nc, "reload", "loaded") as (block, q):
        @block.sync
        def _(sp):
            sp.dma_start(s.pairs[:, :, :], table.rearrange("(p t) w -> p t w", t=T)).then_inc(q.loaded, 16)
            sp.wait_ge(q.loaded, 16)


def find_disorder(nc, s, sorted_pairs):
    with ExitStack() as ctx:
        def sb(name, shape, dt=F32):
            return ctx.enter_context(nc.sbuf_tensor(name, shape, dt))

        before = sb("order_before", [P, T, 2], I32)
        key = sb("order_key", [P, T])
        key_before = sb("order_key_before", [P, T])
        least = sb("order_least", [P, 1])
        least_row = sb("order_least_row", [1, 2])
        row = ctx.enter_context(nc.psum_tensor("order_row", [P, 512], F32))
        with phase(nc, "order", "padded", "stored", "loaded", "step", "turned") as (block, q):
            @block.sync
            def _(sp):
                sp.dma_start(sorted_pairs.rearrange("(p t) w -> p t w", t=T), s.pairs[:, :, :]).then_inc(q.stored, 16)
                sp.wait_ge(q.stored, 16)
                sp.wait_ge(q.padded, 1)
                sp.dma_start(before[0:1, 1:T, :], sorted_pairs[0:T - 1, :].rearrange("(p t) w -> p t w", p=1)
                             ).then_inc(q.loaded, 16)
                sp.dma_start(before[1:P, :, :], sorted_pairs[T - 1:SLOTS - 1, :].rearrange("(p t) w -> p t w", t=T)
                             ).then_inc(q.loaded, 16)

            @block.vector
            def _(dve):
                v = nc.vector
                v.memset(before[:, :, :], -1).then_inc(q.padded, 1)
                dve.wait_ge(q.loaded, 32)
                steps = Steps(dve, q.step)
                steps.then(v.tensor_copy(key[:, :], s.pairs[:, :, 0]))
                steps.then(v.tensor_copy(key_before[:, :], before[:, :, 0]))
                steps.wait()
                steps.then(v.tensor_tensor(key[:, :], key[:, :], key_before[:, :], ALU.subtract))
                steps.wait()
                steps.then(v.tensor_reduce(least[:, :], key[:, :], AX.X, ALU.min))
                dve.wait_ge(q.turned, 1)
                steps.then(v.tensor_reduce(least_row[:, 0:1], row[0:1, 0:P], AX.X, ALU.min))
                steps.wait()
                v.tensor_scalar(s.disorder[:, :], least_row[:, 0:1], 0.0, None, ALU.is_lt)

            @block.tensor
            def _(pe):
                pe.wait_ge(q.step, 4)
                nc.tensor.transpose(row[0:1, 0:P], least[:, :], s.ident[:, :]).then_inc(q.turned, 1)
    return nc.values_load(s.disorder[0:1, 0:1], min_val=0, max_val=1)


def sort_edges(nc, s, half_sorted, sorted_pairs):
    with nc.psum_tensor("counts", [P, 512], F32) as counts, \
            nc.sbuf_tensor("onehot", [P, 4, 256], BF16) as onehot:
        for which, out in enumerate((half_sorted, sorted_pairs)):
            if which:
                reload_pairs(nc, s, half_sorted)
            split_digit(nc, s, which)
            histogram(nc, s, which, counts, onehot)
            rank_edges(nc, s, which, counts, onehot)
            place_edges(nc, s, which, out)


def plan_segments(nc, s, sorted_pairs):
    flat = sorted_pairs
    with ExitStack() as ctx:
        def sb(name, shape, dt):
            return ctx.enter_context(nc.sbuf_tensor(name, shape, dt))

        before = sb("before", [P, T, 2], I32)
        after = sb("after", [P, T, 2], I32)
        key = sb("key", [P, T], F32)
        key_before = sb("key_before", [P, T], F32)
        key_after = sb("key_after", [P, T], F32)
        first = sb("first", [P, T], F32)
        target = sb("target", [P, T], F32)
        clipped = sb("clipped", [P, T, 2], F32)
        one = sb("one", [P, 8], F32)
        bcast = sb("bcast", [P, P], F32)
        rows = ctx.enter_context(nc.psum_tensor("plan_rows", [P, 4, P], F32))
        whole_rows = ctx.enter_context(nc.psum_tensor("plan_whole", [P, 4, P], F32))
        with phase(nc, "plan", "padded", "loaded", "step", "turn", "turned") as (block, q):
            @block.sync
            def _(sp):
                sp.dma_start(s.pairs[:, :, :], flat.rearrange("(p t) w -> p t w", t=T)).then_inc(q.loaded, 16)
                sp.wait_ge(q.padded, 2)
                sp.dma_start(before[0:1, 1:T, :], flat[0:T - 1, :].rearrange("(p t) w -> p t w", p=1)
                             ).then_inc(q.loaded, 16)
                sp.dma_start(before[1:P, :, :], flat[T - 1:SLOTS - 1, :].rearrange("(p t) w -> p t w", t=T)
                             ).then_inc(q.loaded, 16)
                sp.dma_start(after[0:P - 1, :, :], flat[1:SLOTS - T + 1, :].rearrange("(p t) w -> p t w", t=T)
                             ).then_inc(q.loaded, 16)
                sp.dma_start(after[P - 1:P, 0:T - 1, :], flat[SLOTS - T + 1:SLOTS, :].rearrange(
                    "(p t) w -> p t w", p=1)).then_inc(q.loaded, 16)

            @block.vector
            def _(dve):
                v = nc.vector
                v.memset(before[:, :, :], -1).then_inc(q.padded, 1)
                v.memset(after[:, :, :], -1).then_inc(q.padded, 1)
                dve.wait_ge(q.loaded, 80)
                steps = Steps(dve, q.step)
                steps.then(v.tensor_copy(key[:, :], s.pairs[:, :, 0]))
                steps.then(v.tensor_copy(key_before[:, :], before[:, :, 0]))
                steps.then(v.tensor_copy(key_after[:, :], after[:, :, 0]))
                steps.then(v.tensor_copy(s.source[:, :], s.pairs[:, :, 1]))
                steps.then(v.tensor_scalar(clipped[:, :, 0], s.pairs[:, :, 1], float(N - 1), None, ALU.min))
                steps.then(v.tensor_scalar(clipped[:, :, 1], s.pairs[:, :, 0], float(N - 1), None, ALU.min))
                steps.wait()
                steps.then(v.tensor_copy(s.gather_rows[:, :, :], clipped[:, :, :]))
                steps.then(v.tensor_tensor(s.same[:, :], key[:, :], key_before[:, :], ALU.is_equal))
                steps.then(v.tensor_tensor(s.goes_on[:, :], key[:, :], key_after[:, :], ALU.is_equal))
                steps.then(v.tensor_scalar(first[:, :], key[:, :], key[:, 0:1], None, ALU.is_equal))
                steps.wait()
                steps.then(v.tensor_copy(s.same_in[:, :], s.same[:, :]))
                steps.then(v.tensor_scalar(s.reset[:, :], s.same[:, :], -1.0, BIG, ALU.add, ALU.mult))
                steps.then(v.tensor_scalar(s.ends[:, :], s.goes_on[:, :], -1.0, 1.0, ALU.mult, ALU.add))
                steps.then(v.tensor_scalar(first[:, :], first[:, :], s.same[:, 0:1], None, ALU.mult))
                steps.then(v.tensor_tensor(one[:, 4:5], key[:, 0:1], key[:, T - 1:T], ALU.is_equal))
                steps.then(v.tensor_copy(one[:, 2:3], key[:, 0:1]))
                steps.then(v.tensor_copy(one[:, 3:4], key[:, T - 1:T]))
                steps.wait()
                steps.then(v.memset(s.same_in[:, 0:1], 0.0))
                steps.then(v.tensor_copy(s.reset_in[:, :], s.reset[:, :]))
                steps.then(v.tensor_tensor(one[:, 0:1], one[:, 4:5], s.same[:, 0:1], ALU.mult))
                steps.then(v.tensor_tensor(one[:, 1:2], one[:, 4:5], s.goes_on[:, T - 1:T], ALU.mult))
                steps.then(v.tensor_scalar(target[:, :], key[:, :], -1.0, s.dummy[:, 0:1], ALU.mult, ALU.add))
                steps.wait()
                steps.then(v.memset(s.reset_in[:, 0:1], -BIG))
                steps.then(v.tensor_tensor(target[:, :], target[:, :], first[:, :], ALU.mult))
                steps.wait()
                steps.then(v.tensor_tensor(target[:, :], target[:, :], key[:, :], ALU.add))
                steps.wait()
                steps.then(v.scalar_tensor_tensor(target[:, :], s.goes_on[:, :], SKIP, target[:, :], ALU.mult,
                                                  ALU.max))
                steps.wait()
                steps.then(v.memset(target[:, T - 1:T], SKIP))
                steps.wait()
                steps.then(v.tensor_copy(s.scatter_rows[:, :], target[:, :]))

                steps.then(v.tensor_scalar(one[:, 5:6], one[:, 4:5], -1.0, 1.0, ALU.mult, ALU.add))
                steps.wait()
                steps.then(v.tensor_tensor(one[:, 5:6], one[:, 5:6], s.same[:, 0:1], ALU.mult))
                steps.wait()
                steps.then(v.tensor_scalar(one[:, 5:6], one[:, 5:6], -SKIP, SKIP, ALU.mult, ALU.add))
                steps.then(v.tensor_scalar(one[:, 6:7], s.goes_on[:, T - 1:T], SKIP, None, ALU.mult))
                steps.wait()
                steps.then(v.tensor_tensor(one[:, 5:6], one[:, 5:6], one[:, 2:3], ALU.max))
                steps.then(v.tensor_tensor(one[:, 6:7], one[:, 6:7], one[:, 3:4], ALU.max))
                steps.wait()
                steps.then(v.tensor_copy(s.fix_rows[:, :], one[:, 5:7]))

                for j in range(4):
                    if j:
                        dve.wait_ge(q.turned, j)
                    nc.vector.tensor_copy(bcast[:, :], one[:, j:j + 1].to_broadcast([P, P])).then_inc(q.turn, 1)
                dve.wait_ge(q.turned, 4)
                steps.then(v.scalar_tensor_tensor(s.mask_first[:, :], rows[:, 2, :], one[:, 3:4], s.upper[:, :],
                                                  ALU.is_equal, ALU.mult))
                steps.then(v.scalar_tensor_tensor(s.mask_last[:, :], rows[:, 3, :], one[:, 3:4], s.upper_in[:, :],
                                                  ALU.is_equal, ALU.mult))
                steps.then(v.tensor_copy(s.chunk_same[:, :], rows[0:HEADS, 0, :]))
                steps.then(v.tensor_copy(s.chunk_goes_on[:, :], rows[0:HEADS, 1, :]))
                steps.then(v.tensor_scalar(s.chunk_reset[:, :], rows[0:HEADS, 0, :], -1.0, BIG, ALU.add, ALU.mult))

            @block.tensor
            def _(pe):
                for j in range(4):
                    pe.wait_ge(q.turn, j + 1)
                    nc.tensor.transpose(rows[:, j, :], bcast[:, :], s.ident[:, :]).then_inc(q.turned, 1)


def load_weights(nc, s, w):
    loads = []

    def to(sb, dram):
        loads.append((sb, dram))

    for n in range(2):
        mine, theirs = ("msg", "rev")
        to(s.w_edge[:, n, 0:D], w[f"{mine}_W1"][n * D:(n + 1) * D, :])
        to(s.w_edge[:, n, D:2 * D], w[f"{theirs}_W1"][(1 - n) * D:(2 - n) * D, :])
        to(s.w_msg2[:, n, :], w[("msg_W2", "rev_W2")[n]])
        to(s.b_edge[:, n * D:(n + 1) * D], row_of(w[("msg_b1", "rev_b1")[n]]).to_broadcast([P, D]))
        to(s.b_msg2[n:n + 1, :], row_of(w[("msg_b2", "rev_b2")[n]]))
        to(s.upd1[:, n, :], w["upd_W1"][n * D:(n + 1) * D, :])
        to(s.upd2[:, n, :], w["upd_W2"][n * D:(n + 1) * D, :])
    to(s.upd_b1[:, :], w["upd_b1"].rearrange("(c p) -> p c", p=P))
    to(s.upd_b2[:, :], row_of(w["upd_b2"]).to_broadcast([P, D]))
    for l in range(LAYERS):
        to(s.gat_w[:, l, :], w["gat_W"][l])
        to(s.gat_b[:, l, :], w["gat_bias"][l:l + 1, :].to_broadcast([P, D]))
        to(s.skip_w[:, l, :], w["skip_W"][l])
        to(s.skip_b[:, l, :], w["skip_b"][l:l + 1, :].to_broadcast([P, D]))
    with nc.sbuf_tensor("att_rows", [P, LAYERS, 2, HEADS * D], F32) as att_rows, \
            nc.sbuf_tensor("att_scratch", [P, 4, D], F32) as scratch:
        for l in range(LAYERS):
            for j, name in enumerate(("att_src", "att_dst")):
                to(att_rows[:, l, j, :], w[name][l:l + 1].rearrange("a h d -> a (h d)").to_broadcast([P, HEADS * D]))
        with phase(nc, "weights", "loaded", "step") as (block, q):
            @block.sync
            def _(sp):
                with nc.allow_non_contiguous_dma(reason="a bias of 256 numbers by partitions"):
                    for sb, dram in loads:
                        sp.dma_start(sb, dram).then_inc(q.loaded, 16)

            @block.vector
            def _(dve):
                dve.wait_ge(q.loaded, 16 * len(loads))
                n = 0
                for l in range(LAYERS):
                    for j in range(2):
                        for h in range(HEADS):
                            if n >= 4:
                                dve.wait_ge(q.step, n - 3)
                            nc.vector.tensor_tensor_reduce(
                                scratch[:, n % 4, :], s.gat_w[:, l, h * D:(h + 1) * D],
                                att_rows[:, l, j, h * D:(h + 1) * D], 1.0, 0.0, ALU.mult, ALU.add,
                                s.w_att[:, l, j * HEADS + h:j * HEADS + h + 1]).then_inc(q.step, 1)
                            n += 1


def message_edges(nc, s, x, sums_in, sums_out):
    with ExitStack() as ctx:
        def sb(name, shape, dt=F32):
            return ctx.enter_context(nc.sbuf_tensor(name, shape, dt))

        def pb(name, shape):
            return ctx.enter_context(nc.psum_tensor(name, shape, F32))

        gidx = sb("gidx", [P, 2, 4, 2], I32)
        sidx = sb("sidx", [P, 2, 4], I32)
        ridx = sb("ridx", [P, 2, 4], I32)
        ridx_f = sb("ridx_f", [P, 4])
        src4 = sb("src4", [P, 2, 4])
        repeats = sb("repeats", [P, 4])
        x_src = sb("x_src", [P, 2, 4, D])
        x_dst = sb("x_dst", [P, 2, 4, D])
        x_t = sb("x_t", [P, 2, 2, P])
        hidden = sb("hidden", [P, 2, 2, D])
        relus = sb("relus", [P, 2, 2, W])
        equal = sb("equal", [P, 2, P])
        pairs_scratch = sb("pairs_scratch", [P, P])
        rows = sb("rows", [P, 2, 4, W])
        rev_rows = sb("rev_rows", [P, 2, 4, W])
        turned = [pb(f"turned{j}", [P, 2, 256]) for j in range(2)]
        srcs_t = [pb(f"srcs_t{j}", [P, 512]) for j in range(2)]
        hid = [pb(f"hid{j}", [P, 2, 256]) for j in range(2)]
        dedup = [pb(f"dedup{j}", [P, 512]) for j in range(2)]

        with phase(nc, "msg_init", "x") as (block, q):
            @block.vector
            def _(dve):
                nc.vector.memset(relus[:, :, :, :], 0.0).then_inc(q.x, 1)
                nc.vector.memset(rows[:, :, :, :], 0.0)
                dve.wait_ge(q.x, 1)
                nc.vector.memset(relus[:, :, :, D:D + 1], 1.0)

        with phase(nc, "msg", "gidx_ready", "gathered_a", "gathered_b", "src4_ready", "sidx_ready",
                   "x_turned", "srcs_turned", "x_t_ready", "hid_ready", "hidden_ready", "relu_ready",
                   "equal_ready", "counted", "row_ready", "rev_summed", "rev_ready", "stored_a", "stored_b", "passed",
                   "rev_stored", "ridx_step") as (block, q):
            gathered = [q.gathered_a, q.gathered_b]
            stored = [q.stored_a, q.stored_b]

            @block.gpsimd
            def _(pool):
                def gather(i, half, k, wait_x):
                    if k == 0:
                        pool.wait_ge(q.gidx_ready, 2 * i + half + 1)
                        if wait_x:
                            pool.wait_ge(q.x_turned, 4 * (2 * i + half - 1))
                        hold(pool, q.passed)
                    for j, to in enumerate((x_src, x_dst)):
                        pool.indirect_dma_start(to[:, half, k, :], None, x[:, :], bass.IndirectOffsetOnAxis(
                            ap=gidx[:, half, k, j:j + 1], axis=0)).then_inc(gathered[half], 16)

                def scatter(i, half, k, first=False):
                    n = 8 * i + 4 * half + k
                    if k == 0:
                        pool.wait_ge(q.sidx_ready, 2 * i + half + 1)
                        pool.wait_ge(q.ridx_step, 3 * (2 * i + half + 1))
                    pool.wait_ge(q.row_ready, n + 1)
                    hold(pool, q.passed)
                    pool.indirect_dma_start(sums_in[:, :], bass.IndirectOffsetOnAxis(
                        ap=sidx[:, half, k:k + 1], axis=0), rows[:, half, k, :], None,
                        bounds_check=ROWS - 1, oob_is_err=False).then_inc(stored[half], 16)
                    pool.wait_ge(q.rev_ready, n + 1)
                    if not first:
                        pool.wait_ge(q.rev_stored, 16 * n)
                    hold(pool, q.passed)
                    pool.indirect_dma_start(sums_out[:, :], bass.IndirectOffsetOnAxis(
                        ap=ridx[:, half, k:k + 1], axis=0), rev_rows[:, half, k, :], None,
                        compute_op=ALU.add).then_inc(q.rev_stored, 16)

                for k in range(4):
                    gather(0, 0, k, False)
                for k in range(4):
                    gather(0, 1, k, False)
                for k in range(4):
                    gather(1, 0, k, True)
                    scatter(0, 0, k, first=k == 0)
                with pool.Fori(1, ITERS - 1) as i:
                    for k in range(4):
                        gather(i, 1, k, True)
                        scatter(i - 1, 1, k)
                    for k in range(4):
                        gather(i + 1, 0, k, True)
                        scatter(i, 0, k)
                for k in range(4):
                    gather(ITERS - 1, 1, k, True)
                    scatter(ITERS - 2, 1, k)
                for half in range(2):
                    for k in range(4):
                        scatter(ITERS - 1, half, k)
                for half in range(2):
                    pool.wait_ge(stored[half], 64 * ITERS)
                pool.wait_ge(q.rev_stored, 16 * T)

            @block.tensor
            def _(pe):
                def tile(i, half, k, first):
                    n = 8 * i + 4 * half + k
                    b = k % 2
                    if k == 0:
                        pe.wait_ge(gathered[half], 128 * (i + 1))
                        pe.wait_ge(q.src4_ready, 2 * i + half + 1)
                    if not (first and half == 0 and k < 2):
                        pe.wait_ge(q.x_t_ready, n - 1)
                    nc.tensor.transpose(turned[b][:, 0, 0:P], x_src[:, half, k, :], s.ident[:, :])
                    nc.tensor.transpose(turned[b][:, 1, 0:P], x_dst[:, half, k, :], s.ident[:, :]
                                        ).then_inc(q.x_turned, 1)
                    if not (first and half == 0 and k < 2):
                        pe.wait_ge(q.equal_ready, n - 1)
                    mm = nc.tensor.transpose(srcs_t[b][:, 0:P], src4[:, half, k:k + 1].to_broadcast([P, P]),
                                             s.ident[:, :])
                    mm.then_inc(q.srcs_turned, 1)
                    pe.wait_ge(q.x_t_ready, n + 1)
                    if not (first and half == 0 and k < 2):
                        pe.wait_ge(q.hidden_ready, n - 1)
                    for j in range(2):
                        mm = nc.tensor.matmul(hid[b][:, 0, 0:2 * D], x_t[:, b, j, :], s.w_edge[:, j, :],
                                              start=j == 0, stop=j == 1)
                    mm.then_inc(q.hid_ready, 1)
                    pe.wait_ge(q.relu_ready, n + 1)
                    if not (first and half == 0 and k < 2):
                        pe.wait_ge(q.rev_ready, n - 1)
                    nc.tensor.matmul(dedup[b][:, 0:W], equal[:, b, :], relus[:, b, 1, :], start=True, stop=True
                                     ).then_inc(q.rev_summed, 1)

                def block_of(i, first=False):
                    for half in range(2):
                        for k in range(4):
                            tile(i, half, k, first)

                block_of(0, first=True)
                with pe.Fori(1, ITERS) as i:
                    block_of(i)

            @block.scalar
            def _(act):
                def tile(i, half, k, first):
                    n = 8 * i + 4 * half + k
                    b = k % 2
                    early = first and half == 0 and k < 2
                    act.wait_ge(q.x_turned, n + 1)
                    if not early:
                        act.wait_ge(q.hid_ready, n - 1)
                    nc.scalar.copy(x_t[:, b, :, :], turned[b][:, :, 0:P]).then_inc(q.x_t_ready, 1)
                    act.wait_ge(q.hidden_ready, n + 1)
                    if not early:
                        act.wait_ge(q.rev_summed, n - 1)
                        act.wait_ge(q.row_ready, n - 1)
                    nc.scalar.activation(relus[:, b, :, 0:D], hidden[:, b, :, :], ACT.Relu).then_inc(q.relu_ready, 1)
                    act.wait_ge(q.rev_summed, n + 1)
                    if not first:
                        act.wait_ge(q.rev_stored, 16 * (n - 7))
                    nc.scalar.copy(rev_rows[:, half, k, :], dedup[b][:, 0:W]).then_inc(q.rev_ready, 1)

                def block_of(i, first=False):
                    for half in range(2):
                        for k in range(4):
                            tile(i, half, k, first)

                block_of(0, first=True)
                with act.Fori(1, ITERS) as i:
                    block_of(i)

            @block.vector
            def _(dve):
                v = nc.vector

                def feed(i, half):
                    v.tensor_copy(gidx[:, half, :, :], s.gather_rows[:, bass.ds(8 * i + 4 * half, 4), :]
                                  ).then_inc(q.gidx_ready, 1)

                def half_block(i, half, first, last):
                    t0 = 8 * i + 4 * half
                    if not last:
                        dve.wait_ge(gathered[half], 128 * (i + 1))
                        feed(i + 1, half)
                    if not first:
                        dve.wait_ge(q.srcs_turned, 4 * (2 * i + half - 1))
                        dve.wait_ge(q.ridx_step, 6 * i + 3 * half)
                    v.tensor_copy(src4[:, half, :], s.source[:, bass.ds(t0, 4)]).then_inc(q.src4_ready, 1)
                    dve.wait_ge(q.src4_ready, 2 * i + half + 1)
                    for k in range(4):
                        n = t0 + k
                        b = k % 2
                        early = first and half == 0 and k < 2
                        dve.wait_ge(q.srcs_turned, n + 1)
                        if not early:
                            dve.wait_ge(q.rev_summed, n - 1)
                        v.tensor_scalar(equal[:, b, :], srcs_t[b][:, 0:P], src4[:, half, k:k + 1], None,
                                        ALU.is_equal).then_inc(q.equal_ready, 1)
                        dve.wait_ge(q.hid_ready, n + 1)
                        if not early:
                            dve.wait_ge(q.relu_ready, n - 1)
                        v.tensor_tensor(hidden[:, b, :, :].rearrange("p a d -> p (a d)"), hid[b][:, 0, 0:2 * D],
                                        s.b_edge[:, :], ALU.add).then_inc(q.hidden_ready, 1)
                        dve.wait_ge(q.equal_ready, n + 1)
                        if not (first and half == 0 and k == 0):
                            dve.wait_ge(q.counted, n)
                        if k == 0 and not (first and half == 0):
                            dve.wait_ge(q.ridx_step, 6 * i + 3 * half)
                        v.tensor_tensor_reduce(pairs_scratch[:, :], equal[:, b, :], s.lower[:, :], 1.0, 0.0,
                                               ALU.mult, ALU.add, repeats[:, k:k + 1]).then_inc(q.counted, 1)
                        if k == 0:
                            if not first:
                                dve.wait_ge(stored[half], 64 * i)
                            v.tensor_copy(sidx[:, half, :], s.scatter_rows[:, bass.ds(t0, 4)]
                                          ).then_inc(q.sidx_ready, 1)
                        dve.wait_ge(q.relu_ready, n + 1)
                        if not (first and half == 0 and k == 0):
                            dve.wait_ge(q.row_ready, n)
                        before = rows[:, half, k - 1, :] if k else rows[:, 1 - half, 3, :]
                        v.scalar_tensor_tensor(rows[:, half, k, :], before, s.same_in[:, bass.ds(n, 1)],
                                               relus[:, b, 0, :], ALU.mult, ALU.add).then_inc(q.row_ready, 1)
                    dve.wait_ge(q.counted, t0 + 4)
                    v.tensor_scalar(ridx_f[:, :], repeats[:, :], 0.0, s.dummy[:, 0:1], ALU.is_gt, ALU.mult
                                    ).then_inc(q.ridx_step, 1)
                    dve.wait_ge(q.ridx_step, 6 * i + 3 * half + 1)
                    v.tensor_tensor(ridx_f[:, :], ridx_f[:, :], src4[:, half, :], ALU.max).then_inc(q.ridx_step, 1)
                    dve.wait_ge(q.ridx_step, 6 * i + 3 * half + 2)
                    if not first:
                        dve.wait_ge(q.rev_stored, 16 * (t0 - 4))
                    v.tensor_copy(ridx[:, half, :], ridx_f[:, :]).then_inc(q.ridx_step, 1)

                feed(0, 0)
                feed(0, 1)
                half_block(0, 0, True, False)
                half_block(0, 1, True, False)
                with dve.Fori(1, ITERS - 1) as i:
                    half_block(i, 0, False, False)
                    half_block(i, 1, False, False)
                half_block(ITERS - 1, 0, False, True)
                half_block(ITERS - 1, 1, False, True)

        fixup(nc, s, "msg_fix", sums_in, rows[:, 1, 3, :], W, dedup)


def fixup(nc, s, name, table, last, cols, sums):
    with nc.sbuf_tensor(f"{name}_first", [P, W], F32) as first, \
            nc.sbuf_tensor(f"{name}_last", [P, W], F32) as total:
        with phase(nc, name, "loaded", "summed", "added", "stored") as (block, q):
            @block.sync
            def _(sp):
                sp.dma_start(first[:, :], table[SIDE:SIDE + P, :]).then_inc(q.loaded, 16)

            @block.tensor
            def _(pe):
                nc.tensor.matmul(sums[0][:, 0:cols], s.mask_first[:, :], last[:, 0:cols], start=True, stop=True
                                 ).then_inc(q.summed, 1)
                nc.tensor.matmul(sums[1][:, 0:cols], s.mask_last[:, :], last[:, 0:cols], start=True, stop=True
                                 ).then_inc(q.summed, 1)

            @block.vector
            def _(dve):
                dve.wait_ge(q.summed, 2)
                dve.wait_ge(q.loaded, 16)
                nc.vector.tensor_tensor(first[:, 0:cols], first[:, 0:cols], sums[0][:, 0:cols], ALU.add
                                        ).then_inc(q.added, 1)
                nc.vector.tensor_copy(total[:, 0:cols], sums[1][:, 0:cols]).then_inc(q.added, 1)
                if cols < W:
                    nc.vector.tensor_copy(total[:, cols:W], last[:, cols:W]).then_inc(q.added, 1)

            @block.gpsimd
            def _(pool):
                pool.wait_ge(q.added, 2 + (cols < W))
                for j, rows in enumerate((first, total)):
                    pool.indirect_dma_start(table[:, :], bass.IndirectOffsetOnAxis(ap=s.fix_rows[:, j:j + 1], axis=0),
                                            rows[:, :], None, bounds_check=ROWS - 1, oob_is_err=False
                                            ).then_inc(q.stored, 16)
                pool.wait_ge(q.stored, 32)


def nodes_of(dram, start):
    return dram[bass.ds(start, BLOCK), :].rearrange("(p c) w -> p c w", c=4)


def over_blocks(eng, step):
    step(0, 0, True)
    step(1, 1, True)
    with eng.Fori(1, NBLOCKS // 2 - 1) as i:
        step(2 * i, 0, False)
        step(2 * i + 1, 1, False)
    step(NBLOCKS - 2, 0, False)
    step(NBLOCKS - 1, 1, False)


def is_block(j, n):
    return isinstance(j, int) and j == n


def start_of(j):
    return N - BLOCK if is_block(j, NBLOCKS - 1) else j * BLOCK


def loads_done(eng, sem, j, slot, n):
    eng.wait_ge(sem, 8 * n * (j - slot) + 16 * n)


def over_features(bias):
    return bias.rearrange("p (o d) -> p o d", o=1).to_broadcast([P, 4, D])


def head_rows(nc, s, steps, scores, rows, node_att, slot):
    v = nc.vector
    a = node_att[:, slot, :, :]
    r = rows[:, slot, :, :]
    steps.then(v.tensor_copy(r[:, :, D:D + HEADS], scores[:, :, 0:HEADS]))
    steps.then(v.tensor_copy(a[:, :, HEADS:2 * HEADS], scores[:, :, HEADS:2 * HEADS]))
    steps.wait()
    steps.then(v.tensor_tensor(a[:, :, 0:HEADS], r[:, :, D:D + HEADS], a[:, :, HEADS:2 * HEADS], ALU.add))
    steps.wait()
    steps.then(v.scalar_tensor_tensor(a[:, :, 0:HEADS], a[:, :, 0:HEADS], SLOPE, a[:, :, 0:HEADS], ALU.mult, ALU.max))


def deviation(nc, s, q, act, moments, rstd, j, slot, moment_steps):
    act.wait_ge(q.step, moment_steps * (j + 1))
    nc.scalar.activation(rstd[:, slot, :], moments[:, slot, :, 1], ACT.Sqrt, bias=s.eps[:, 0:1]
                         ).then_inc(q.rstd_ready, 1)


def row_moments(nc, steps, rows, stats, moments):
    for c in range(4):
        steps.then(nc.vector.bn_stats(stats[:, c, :], rows[:, c, :]))
    steps.wait()
    hold(steps.eng, steps.passed)
    for c in range(4):
        steps.then(nc.vector.bn_aggr(moments[:, c, :], stats[:, c, :]))


def normalise(nc, q, dve, rows, dst, moments, rstd, j, slot):
    v = nc.vector
    dve.wait_ge(q.rstd_ready, j + 1)
    v.reciprocal(rstd[:, slot, :], rstd[:, slot, :]).then_inc(q.inverted, 1)
    dve.wait_ge(q.inverted, j + 1)
    for c in range(4):
        v.tensor_scalar(dst[:, c, 0:D], rows[:, c, :], moments[:, slot, c, 0:1], rstd[:, slot, c:c + 1],
                        ALU.subtract, ALU.mult).then_inc(q.normed, 1)


MOMENT_STEPS = 4 + 4
HEAD_STEPS = 4


def store_rows(pool, q, stored, new, node_att, x_next, att_next, j, slot):
    pool.wait_ge(q.tail_step, HEAD_STEPS * (j + 1))
    if is_block(j, NBLOCKS - 1):
        pool.wait_ge(stored[0], 16 * NBLOCKS)
        pool.wait_ge(stored[1], 16 * (NBLOCKS - 2))
    pool.dma_start(nodes_of(x_next, start_of(j)), new[:, slot, :, :]).then_inc(stored[slot], 16)
    pool.dma_start(nodes_of(att_next, start_of(j)), node_att[:, slot, :, :]).then_inc(stored[slot], 16)


def score_rows(nc, s, q, pe, bank, new, new_t, layer, j, slot):
    pe.wait_ge(q.normed, 4 * (j + 1))
    if not is_block(j, 0):
        pe.wait_ge(q.tail_step, HEAD_STEPS * j)
    for c in range(4):
        mm = nc.tensor.transpose(bank[:, c * P:(c + 1) * P], new[:, slot, c, 0:D], s.ident[:, :])
    mm.then_inc(q.rows_turned, 1)
    pe.wait_ge(q.rows_copied, j + 1)
    for c in range(4):
        mm = nc.tensor.matmul(bank[:, c * 8:c * 8 + 8], new_t[:, c * P:(c + 1) * P], s.w_att[:, layer, :],
                              start=True, stop=True)
    mm.then_inc(q.scored, 1)


def copy_rows(nc, q, act, bank, new_t, j):
    act.wait_ge(q.rows_turned, j + 1)
    if not is_block(j, 0):
        act.wait_ge(q.scored, j)
    nc.scalar.copy(new_t[:, :], bank[:, :]).then_inc(q.rows_copied, 1)


def update_nodes(nc, s, x, sums_in, sums_out, x_next, att_next):
    with ExitStack() as ctx:
        def sb(name, shape, dt=F32):
            return ctx.enter_context(nc.sbuf_tensor(name, shape, dt))

        def pb(name, shape):
            return ctx.enter_context(nc.psum_tensor(name, shape, F32))

        xs = sb("xs", [P, 2, 4, D])
        ins = sb("ins", [P, 2, 4, W])
        outs = sb("outs", [P, 2, 4, W])
        degrees = sb("degrees", [P, 2, 4, 2])
        x_t = sb("xs_t", [P, 2, BLOCK])
        in_t = sb("ins_t", [P, BLOCK])
        out_t = sb("outs_t", [P, BLOCK])
        deg_t = sb("deg_t", [2, BLOCK])
        agg_t = sb("agg_t", [P, BLOCK])
        hid_t = sb("hid_t", [P, 2, BLOCK])
        base = sb("base_rows", [P, 2, 4, D])
        total = sb("total_rows", [P, 2, 4, D])
        new = sb("new_rows", [P, 2, 4, D + HEADS])
        new_t = sb("new_t", [P, BLOCK])
        node_att = sb("node_att", [P, 2, 4, 2 * HEADS])
        stats = sb("stats", [P, 4, 6])
        moments = sb("moments", [P, 2, 4, 2])
        rstd = sb("rstd", [P, 2, 4])
        p_x = pb("p_x", [P, BLOCK])
        p_in = pb("p_in", [P, BLOCK])
        p_out = pb("p_out", [P, BLOCK])
        p_agg = pb("p_agg", [P, BLOCK])
        p_hid = [pb(f"p_hid{m}", [P, BLOCK]) for m in range(2)]
        p_new = pb("p_new", [P, 4, D])
        p_tail = pb("p_tail", [P, BLOCK])

        with phase(nc, "upd", "loaded_a", "loaded_b", "degrees_ready", "turned", "deg_turned", "copied",
                   "deg_copied", "doubled", "base_ready", "agg_ready", "agg_copied", "hid_ready", "hid_copied",
                   "new_ready", "step", "rstd_ready", "inverted", "normed", "rows_turned", "rows_copied", "scored",
                   "tail_step", "stored_a", "stored_b", "passed") as (block, q):
            loaded = [q.loaded_a, q.loaded_b]
            stored = [q.stored_a, q.stored_b]
            moment_steps = 1 + MOMENT_STEPS

            @block.sync
            def _(sp):
                def step(j, slot, first):
                    if not first:
                        sp.wait_ge(q.turned, 3 * (j - 1))
                        sp.wait_ge(q.base_ready, j - 1)
                        hold(sp, q.passed)
                        sp.wait_ge(q.degrees_ready, 2 * (j - 1))
                        hold(sp, q.passed)
                    for rows, table in ((xs, x), (ins, sums_in), (outs, sums_out)):
                        sp.dma_start(rows[:, slot, :, :], nodes_of(table, start_of(j))).then_inc(loaded[slot], 16)

                over_blocks(sp, step)

            @block.gpsimd
            def _(pool):
                def step(j, slot, first):
                    loads_done(pool, loaded[slot], j, slot, 3)
                    if not first:
                        pool.wait_ge(q.step, moment_steps * (j - 2) + 1)
                    nc.gpsimd.tensor_tensor(base[:, slot], xs[:, slot], xs[:, slot], ALU.add).then_inc(q.doubled, 1)
                    pool.wait_ge(q.doubled, j + 1)
                    nc.gpsimd.tensor_tensor(base[:, slot], base[:, slot], over_features(s.upd_b2[:, :]), ALU.add
                                            ).then_inc(q.base_ready, 1)
                    if not first:
                        store_rows(pool, q, stored, new, node_att, x_next, att_next, j - 2, slot)

                over_blocks(pool, step)
                for j in (NBLOCKS - 2, NBLOCKS - 1):
                    store_rows(pool, q, stored, new, node_att, x_next, att_next, j, j % 2)
                for slot in range(2):
                    pool.wait_ge(stored[slot], 16 * NBLOCKS)

            @block.tensor
            def _(pe):
                def messages(j, slot, very_first):
                    pe.wait_ge(q.degrees_ready, 2 * (j + 1))
                    pe.wait_ge(q.copied, 3 * j + 1)
                    for c in range(4):
                        mm = nc.tensor.transpose(p_x[0:2, c * P:(c + 1) * P], degrees[:, slot, c, :], s.ident[:, :])
                    mm.then_inc(q.deg_turned, 1)
                    pe.wait_ge(q.copied, 3 * j + 3)
                    if not very_first:
                        pe.wait_ge(q.agg_copied, j)
                    nc.tensor.matmul(p_agg[:, :], s.w_msg2[:, 0, :], in_t[:, :], start=True, stop=False)
                    nc.tensor.matmul(p_agg[:, :], s.w_msg2[:, 1, :], out_t[:, :], start=False, stop=False)
                    pe.wait_ge(q.deg_copied, j + 1)
                    nc.tensor.matmul(p_agg[:, :], s.b_msg2[:, :], deg_t[:, :], start=False, stop=True
                                     ).then_inc(q.agg_ready, 1)

                def hidden(j, slot, very_first):
                    pe.wait_ge(q.agg_copied, j + 1)
                    for m in range(2):
                        if not very_first:
                            pe.wait_ge(q.hid_copied, 2 * j + m - 1)
                        nc.tensor.matmul(p_hid[m][:, :], s.upd1[:, 0, m * P:(m + 1) * P], agg_t[:, :], start=True,
                                         stop=False)
                        nc.tensor.matmul(p_hid[m][:, :], s.upd1[:, 1, m * P:(m + 1) * P], x_t[:, slot, :],
                                         start=False, stop=True).then_inc(q.hid_ready, 1)

                def output(j, very_first):
                    pe.wait_ge(q.hid_copied, 2 * j + 2)
                    if not very_first:
                        pe.wait_ge(q.step, moment_steps * (j - 1) + 1)
                    for c in range(4):
                        for m in range(2):
                            mm = nc.tensor.matmul(p_new[:, c, :], hid_t[:, m, c * P:(c + 1) * P], s.upd2[:, m, :],
                                                  start=m == 0, stop=m == 1)
                    mm.then_inc(q.new_ready, 1)

                def tail(j, slot):
                    score_rows(nc, s, q, pe, p_tail, new, new_t, 0, j, slot)

                def step(j, slot, first):
                    very_first = first and slot == 0
                    loads_done(pe, loaded[slot], j, slot, 3)
                    for m, (dst, src) in enumerate(((p_x, xs), (p_in, ins), (p_out, outs))):
                        if m == 0 and not very_first:
                            pe.wait_ge(q.deg_copied, j)
                        elif not very_first:
                            pe.wait_ge(q.copied, 3 * j)
                        for c in range(4):
                            mm = nc.tensor.transpose(dst[:, c * P:(c + 1) * P], src[:, slot, c, 0:D], s.ident[:, :])
                        mm.then_inc(q.turned, 1)
                    if not very_first:
                        hidden(j - 1, 1 - slot, is_block(j, 1))
                    messages(j, slot, very_first)
                    if not very_first:
                        output(j - 1, is_block(j, 1))
                    if not first:
                        tail(j - 2, slot)

                over_blocks(pe, step)
                tail(NBLOCKS - 2, 0)
                hidden(NBLOCKS - 1, 1, False)
                output(NBLOCKS - 1, False)
                tail(NBLOCKS - 1, 1)

            @block.scalar
            def _(act):
                def hidden(j, very_first):
                    for m in range(2):
                        act.wait_ge(q.hid_ready, 2 * j + m + 1)
                        if m == 0 and not very_first:
                            act.wait_ge(q.new_ready, j)
                        nc.scalar.activation(hid_t[:, m, :], p_hid[m][:, :], ACT.Relu, bias=s.upd_b1[:, m:m + 1]
                                             ).then_inc(q.hid_copied, 1)

                def step(j, slot, first):
                    very_first = first and slot == 0
                    for m, (dst, src) in enumerate(((x_t[:, slot, :], p_x), (in_t[:, :], p_in),
                                                    (out_t[:, :], p_out))):
                        act.wait_ge(q.turned, 3 * j + m + 1)
                        if m == 0 and not first:
                            act.wait_ge(q.hid_ready, 2 * (j - 1))
                        if m == 1 and not very_first:
                            act.wait_ge(q.agg_ready, j)
                        nc.scalar.copy(dst, src[:, :]).then_inc(q.copied, 1)
                    if not first:
                        deviation(nc, s, q, act, moments, rstd, j - 2, slot, moment_steps)
                    if not very_first:
                        hidden(j - 1, is_block(j, 1))
                    act.wait_ge(q.deg_turned, j + 1)
                    nc.scalar.copy(deg_t[:, :], p_x[0:2, :]).then_inc(q.deg_copied, 1)
                    act.wait_ge(q.agg_ready, j + 1)
                    if not very_first:
                        act.wait_ge(q.hid_ready, 2 * j)
                    nc.scalar.copy(agg_t[:, :], p_agg[:, :]).then_inc(q.agg_copied, 1)
                    if not first:
                        copy_rows(nc, q, act, p_tail, new_t, j - 2)

                over_blocks(act, step)
                deviation(nc, s, q, act, moments, rstd, NBLOCKS - 2, 0, moment_steps)
                copy_rows(nc, q, act, p_tail, new_t, NBLOCKS - 2)
                hidden(NBLOCKS - 1, False)
                deviation(nc, s, q, act, moments, rstd, NBLOCKS - 1, 1, moment_steps)
                copy_rows(nc, q, act, p_tail, new_t, NBLOCKS - 1)

            @block.vector
            def _(dve):
                v = nc.vector

                def total_and_moments(j, slot, first):
                    dve.wait_ge(q.new_ready, j + 1)
                    dve.wait_ge(q.base_ready, j + 1)
                    if not first:
                        dve.wait_ge(q.normed, 4 * (j - 1))
                    steps = Steps(dve, q.step, moment_steps * j, q.passed)
                    steps.then(v.tensor_tensor(total[:, slot], base[:, slot], p_new[:, :, :], ALU.add))
                    steps.wait()
                    row_moments(nc, steps, total[:, slot], stats, moments[:, slot])

                def finish(j, slot, first):
                    if not first:
                        dve.wait_ge(stored[slot], 16 * (j - slot))
                    normalise(nc, q, dve, total[:, slot], new[:, slot], moments, rstd, j, slot)

                def tail(j, slot):
                    dve.wait_ge(q.scored, j + 1)
                    steps = Steps(dve, q.tail_step, HEAD_STEPS * j)
                    head_rows(nc, s, steps, p_tail[:, 0:32].rearrange("p (c k) -> p c k", c=4), new, node_att, slot)

                def step(j, slot, first):
                    very_first = first and slot == 0
                    loads_done(dve, loaded[slot], j, slot, 3)
                    if not first:
                        dve.wait_ge(q.deg_turned, j - 1)
                    v.tensor_copy(degrees[:, slot, :, 0:1], ins[:, slot, :, D:D + 1]).then_inc(q.degrees_ready, 1)
                    v.tensor_copy(degrees[:, slot, :, 1:2], outs[:, slot, :, D:D + 1]).then_inc(q.degrees_ready, 1)
                    if not first:
                        finish(j - 2, slot, is_block(j, 2) or is_block(j, 3))
                    if not very_first:
                        total_and_moments(j - 1, 1 - slot, is_block(j, 1))
                    if not first:
                        tail(j - 2, slot)

                over_blocks(dve, step)
                finish(NBLOCKS - 2, 0, False)
                tail(NBLOCKS - 2, 0)
                total_and_moments(NBLOCKS - 1, 1, False)
                finish(NBLOCKS - 1, 1, False)
                tail(NBLOCKS - 1, 1)


def score_edges(nc, s, layer, x_rows, att_rows, turned_x):
    with ExitStack() as ctx:
        def sb(name, shape, dt=F32):
            return ctx.enter_context(nc.sbuf_tensor(f"{name}_{layer}", shape, dt))

        gidx = sb("gidx2", [P, 2, 4, 2], I32)
        rows = sb("src_rows", [P, 2, 4, D + HEADS])
        atts = sb("dst_atts", [P, 2, 4, 2 * HEADS])
        x_t = sb("src_t", [P, 2, BLOCK])
        banks = [ctx.enter_context(nc.psum_tensor(f"src_bank{h}_{layer}", [P, BLOCK], F32)) for h in range(2)]
        with phase(nc, f"score{layer}", "gidx_ready", "gathered_a", "gathered_b", "turned", "copied", "stored_a", "stored_b", "passed",
                   "scored") as (block, q):
            gathered = [q.gathered_a, q.gathered_b]
            stored = [q.stored_a, q.stored_b]

            def over_halves(eng, step):
                step(0, 0, True)
                step(0, 1, True)
                with eng.Fori(1, ITERS) as i:
                    step(i, 0, False)
                    step(i, 1, False)

            @block.gpsimd
            def _(pool):
                def step(i, half, first):
                    pool.wait_ge(q.gidx_ready, 2 * i + half + 1)
                    if not first:
                        pool.wait_ge(q.turned, 2 * i + half - 1)
                        pool.wait_ge(q.scored, 4 * i + 2 * half - 2)
                    hold(pool, q.passed)
                    for k in range(4):
                        pool.indirect_dma_start(rows[:, half, k, :], None, x_rows[:, :], bass.IndirectOffsetOnAxis(
                            ap=gidx[:, half, k, 0:1], axis=0)).then_inc(gathered[half], 16)
                        pool.indirect_dma_start(atts[:, half, k, :], None, att_rows[:, :], bass.IndirectOffsetOnAxis(
                            ap=gidx[:, half, k, 1:2], axis=0)).then_inc(gathered[half], 16)

                over_halves(pool, step)

            @block.tensor
            def _(pe):
                def step(i, half, first):
                    pe.wait_ge(gathered[half], 128 * i + 128)
                    if not first:
                        pe.wait_ge(q.copied, 2 * i + half - 1)
                    for k in range(4):
                        mm = nc.tensor.transpose(banks[half][:, k * P:(k + 1) * P], rows[:, half, k, 0:D],
                                                 s.ident[:, :])
                    mm.then_inc(q.turned, 1)

                over_halves(pe, step)

            @block.scalar
            def _(act):
                def step(i, half, first):
                    act.wait_ge(q.turned, 2 * i + half + 1)
                    if not first:
                        act.wait_ge(stored[half], 16 * i)
                    nc.scalar.copy(x_t[:, half, :], banks[half][:, :]).then_inc(q.copied, 1)

                over_halves(act, step)

            @block.sync
            def _(sp):
                def step(i, half, first):
                    sp.wait_ge(q.copied, 2 * i + half + 1)
                    hold(sp, q.passed)
                    sp.dma_start(turned_x[bass.ds((2 * i + half) * P, P), :], x_t[:, half, :]
                                 ).then_inc(stored[half], 16)

                over_halves(sp, step)
                for half in range(2):
                    sp.wait_ge(stored[half], 16 * ITERS)

            @block.vector
            def _(dve):
                v = nc.vector

                def feed(i, half, first):
                    v.tensor_copy(gidx[:, half, :, :], s.gather_rows[:, bass.ds(8 * i + 4 * half, 4), :]
                                  ).then_inc(q.gidx_ready, 1)

                def step(i, half, last):
                    dve.wait_ge(gathered[half], 128 * i + 128)
                    if not last:
                        feed(i + 1, half, False)
                    t = bass.ds(8 * i + 4 * half, 4)
                    v.tensor_tensor(s.edge_score[:, :, t].rearrange("p h k -> p k h"), rows[:, half, :, D:D + HEADS],
                                    atts[:, half, :, HEADS:2 * HEADS], ALU.add).then_inc(q.scored, 1)
                    v.tensor_copy(s.self_score[:, :, t].rearrange("p h k -> p k h"), atts[:, half, :, 0:HEADS]
                                  ).then_inc(q.scored, 1)

                feed(0, 0, True)
                feed(0, 1, True)
                with dve.Fori(0, ITERS - 1) as i:
                    step(i, 0, False)
                    step(i, 1, False)
                step(ITERS - 1, 0, True)
                step(ITERS - 1, 1, True)


def segment_total(nc, s, name, values, op, chunk, row_bank, col_bank):
    maximum = op == ALU.max
    join = ALU.add if maximum else ALU.mult
    inner = s.reset_in if maximum else s.same_in
    outer = s.reset if maximum else s.same
    chunk_step = s.chunk_reset if maximum else s.chunk_same
    start = -BIG if maximum else 0.0
    scan, ends, incoming, chunk_rows, shifted = chunk
    with phase(nc, name, "step", "turn", "turned") as (block, q):
        @block.vector
        def _(dve):
            v = nc.vector
            steps = Steps(dve, q.step)
            turns = [0]

            def across(edge, step_row, joined, op1, first, backwards):
                steps.then(v.tensor_copy(ends[:, :], edge))
                steps.wait()
                dve.sem_inc(q.turn, 1)
                turns[0] += 1
                dve.wait_ge(q.turned, turns[0])
                steps.then(v.tensor_copy(chunk_rows[:, 0, :], row_bank[0:HEADS, 0:P]))
                steps.then(v.memset(shifted[:, :], first))
                steps.wait()
                if backwards:
                    steps.then(v.tensor_tensor_scan(chunk_rows[:, 1, ::-1], step_row[:, ::-1],
                                                    chunk_rows[:, 0, ::-1], first, joined, op1))
                    steps.wait()
                    steps.then(v.tensor_copy(shifted[:, 0:P - 1], chunk_rows[:, 1, 1:P]))
                else:
                    steps.then(v.tensor_tensor_scan(chunk_rows[:, 1, :], step_row[:, :], chunk_rows[:, 0, :], first,
                                                    joined, op1))
                    steps.wait()
                    steps.then(v.tensor_copy(shifted[:, 1:P], chunk_rows[:, 1, 0:P - 1]))
                steps.wait()
                dve.sem_inc(q.turn, 1)
                turns[0] += 1
                dve.wait_ge(q.turned, turns[0])
                steps.then(v.tensor_copy(incoming[:, :], col_bank[:, 0:HEADS]))
                steps.wait()

            for h in range(HEADS):
                steps.then(v.tensor_tensor_scan(scan[:, h, :], inner[:, :], values[:, h, :], start, join, op))
            steps.wait()
            across(scan[:, :, T - 1], chunk_step, join, op, start, False)
            for h in range(HEADS):
                steps.then(v.tensor_tensor_scan(scan[:, h, :], outer[:, :], values[:, h, :], incoming[:, h:h + 1],
                                                join, op))
            steps.wait()
            for h in range(HEADS):
                steps.then(v.tensor_tensor(scan[:, h, :], scan[:, h, :], s.ends[:, :], ALU.mult))
            steps.wait()
            for h in range(HEADS):
                steps.then(v.tensor_tensor_scan(values[:, h, ::-1], s.goes_on[:, ::-1], scan[:, h, ::-1], 0.0,
                                                ALU.mult, ALU.add))
            steps.wait()
            across(values[:, :, 0], s.chunk_goes_on, ALU.mult, ALU.add, 0.0, True)
            for h in range(HEADS):
                steps.then(v.tensor_tensor_scan(values[:, h, ::-1], s.goes_on[:, ::-1], scan[:, h, ::-1],
                                                incoming[:, h:h + 1], ALU.mult, ALU.add))

        @block.tensor
        def _(pe):
            for n in range(2):
                pe.wait_ge(q.turn, 2 * n + 1)
                nc.tensor.transpose(row_bank[0:HEADS, 0:P], ends[:, :], s.ident[:, :]).then_inc(q.turned, 1)
                pe.wait_ge(q.turn, 2 * n + 2)
                nc.tensor.transpose(col_bank[:, 0:HEADS], shifted[:, :], s.ident[0:HEADS, 0:HEADS]
                                    ).then_inc(q.turned, 1)


def attention_weights(nc, s, layer):
    with ExitStack() as ctx:
        def sb(name, shape, dt=F32):
            return ctx.enter_context(nc.sbuf_tensor(f"{name}_{layer}", shape, dt))

        top = sb("top", [P, HEADS, T])
        chunk = (sb("scan", [P, HEADS, T]), sb("chunk_ends", [P, HEADS]), sb("incoming", [P, HEADS]),
                 sb("chunk_rows", [HEADS, 2, P]), sb("shifted", [HEADS, P]))
        row_bank = ctx.enter_context(nc.psum_tensor(f"row_bank_{layer}", [P, BLOCK], F32))
        col_bank = ctx.enter_context(nc.psum_tensor(f"col_bank_{layer}", [P, BLOCK], F32))
        e, own = s.edge_score, s.self_score

        with phase(nc, f"leaky{layer}", "step") as (block, q):
            @block.vector
            def _(dve):
                v = nc.vector
                v.scalar_tensor_tensor(e[:, :, :], e[:, :, :], SLOPE, e[:, :, :], ALU.mult, ALU.max
                                       ).then_inc(q.step, 1)
                dve.wait_ge(q.step, 1)
                v.tensor_tensor(top[:, :, :], e[:, :, :], own[:, :, :], ALU.max)

        segment_total(nc, s, f"max{layer}", top, ALU.max, chunk, row_bank, col_bank)

        with phase(nc, f"exp{layer}", "shifted", "exped") as (block, q):
            @block.vector
            def _(dve):
                v = nc.vector
                v.tensor_tensor(e[:, :, :], e[:, :, :], top[:, :, :], ALU.subtract).then_inc(q.shifted, 1)
                v.tensor_tensor(own[:, :, :], own[:, :, :], top[:, :, :], ALU.subtract).then_inc(q.shifted, 1)
                dve.wait_ge(q.shifted, 2)
                dve.wait_ge(q.exped, 2)
                v.tensor_copy(top[:, :, :], e[:, :, :])

            @block.scalar
            def _(act):
                act.wait_ge(q.shifted, 2)
                nc.scalar.activation(e[:, :, :], e[:, :, :], ACT.Exp).then_inc(q.exped, 1)
                nc.scalar.activation(own[:, :, :], own[:, :, :], ACT.Exp).then_inc(q.exped, 1)

        segment_total(nc, s, f"sum{layer}", top, ALU.add, chunk, row_bank, col_bank)

        with phase(nc, f"norm{layer}", "step") as (block, q):
            @block.vector
            def _(dve):
                v = nc.vector
                steps = Steps(dve, q.step)
                steps.then(v.tensor_tensor(top[:, :, :], top[:, :, :], own[:, :, :], ALU.add))
                steps.wait()
                steps.then(v.reciprocal(top[:, :, :], top[:, :, :]))
                steps.wait()
                steps.then(v.scalar_tensor_tensor(s.weights[:, 0:HEADS, :], e[:, :, :], 1.0 / HEADS, top[:, :, :],
                                                  ALU.mult, ALU.mult))
                steps.then(v.scalar_tensor_tensor(s.self_weights[:, :, :].rearrange("p t h -> p h t"), own[:, :, :],
                                                  1.0 / HEADS, top[:, :, :], ALU.mult, ALU.mult))
                steps.then(v.tensor_copy(s.weights[:, HEADS, :], s.same_in[:, :]))


def weigh_edges(nc, s, layer, turned_x, sums):
    with ExitStack() as ctx:
        def sb(name, shape, dt=F32):
            return ctx.enter_context(nc.sbuf_tensor(f"{name}_{layer}", shape, dt))

        x_t = sb("edge_t", [P, 2, BLOCK])
        sidx = sb("sidx2", [P, 2, 4], I32)
        weights = sb("weights4", [P, 2, HEADS + 1, 4])
        part = sb("part", [P, 4, 2, D])
        rows = sb("sum_rows", [P, 2, 4, W])
        banks = [ctx.enter_context(nc.psum_tensor(f"heads{b}_{layer}", [P, BLOCK], F32)) for b in range(4)]

        with phase(nc, f"weigh_init{layer}", "x") as (block, q):
            @block.vector
            def _(dve):
                nc.vector.memset(rows[:, :, :, :], 0.0).then_inc(q.x, 1)
                dve.wait_ge(q.x, 1)
                nc.vector.memset(rows[:, :, :, D + HEADS:D + HEADS + 1], 1.0)

        with phase(nc, f"weigh{layer}", "loaded_a", "loaded_b", "fed", "headed", "first_head", "step", "row_ready",
                   "extras_ready", "stored_a", "stored_b", "passed") as (block, q):
            loaded = [q.loaded_a, q.loaded_b]
            stored = [q.stored_a, q.stored_b]

            def over_halves(eng, step):
                step(0, 0, True)
                step(0, 1, True)
                with eng.Fori(1, ITERS) as i:
                    step(i, 0, False)
                    step(i, 1, False)

            @block.sync
            def _(sp):
                def step(i, half, first):
                    if not first:
                        sp.wait_ge(q.headed, 4 * (2 * i + half - 1))
                        hold(sp, q.passed)
                    sp.dma_start(x_t[:, half, :], turned_x[bass.ds((2 * i + half) * P, P), :]
                                 ).then_inc(loaded[half], 16)

                over_halves(sp, step)

            @block.tensor
            def _(pe):
                def step(i, half, first):
                    pe.wait_ge(loaded[half], 16 * i + 16)
                    for k in range(4):
                        n = 8 * i + 4 * half + k
                        if not (first and half == 0):
                            pe.wait_ge(q.step, 6 * (4 * i + 2 * half + k // 2 - 2) + 5 + k % 2)
                        nc.tensor.matmul(banks[k][:, :], x_t[:, half, k * P:(k + 1) * P], s.gat_w[:, layer, :],
                                         start=True, stop=True).then_inc(q.headed, 1)

                over_halves(pe, step)

            @block.scalar
            def _(act):
                def step(i, half, first):
                    act.wait_ge(q.fed, 4 * i + 2 * half + 2)
                    if not first:
                        act.wait_ge(stored[half], 64 * i)
                    t0 = 8 * i + 4 * half
                    nc.scalar.copy(rows[:, half, :, D:D + HEADS], s.self_weights[:, bass.ds(t0, 4), :]
                                   ).then_inc(q.extras_ready, 1)
                    for k in range(4):
                        n = t0 + k
                        act.wait_ge(q.headed, n + 1)
                        if not (first and half == 0):
                            act.wait_ge(q.step, 6 * (4 * i + 2 * half + k // 2 - 2) + 1 + k % 2)
                        nc.scalar.activation(part[:, k, 0, :], banks[k][:, 0:D], ACT.Copy,
                                             scale=weights[:, half, 0, k:k + 1]).then_inc(q.first_head, 1)

                over_halves(act, step)

            @block.vector
            def _(dve):
                v = nc.vector

                def step(i, half, first):
                    t0 = 8 * i + 4 * half
                    if not first:
                        dve.wait_ge(q.first_head, t0 - 4)
                        dve.wait_ge(q.row_ready, t0 - 4)
                        dve.wait_ge(stored[half], 64 * i)
                    v.tensor_copy(weights[:, half, :, :], s.weights[:, :, bass.ds(t0, 4)]).then_inc(q.fed, 1)
                    v.tensor_copy(sidx[:, half, :], s.scatter_rows[:, bass.ds(t0, 4)]).then_inc(q.fed, 1)
                    dve.wait_ge(q.fed, 4 * i + 2 * half + 2)
                    for pair in range(2):
                        done = 6 * (4 * i + 2 * half + pair)
                        for h in range(1, HEADS):
                            for k in (2 * pair, 2 * pair + 1):
                                if h == 1:
                                    dve.wait_ge(q.first_head, t0 + k + 1)
                                    if not (first and half == 0):
                                        dve.wait_ge(q.row_ready, t0 + k - 3)
                                else:
                                    dve.wait_ge(q.step, done + 2 * (h - 2) + k % 2 + 1)
                                v.scalar_tensor_tensor(part[:, k, 1, :], banks[k][:, h * D:(h + 1) * D],
                                                       weights[:, half, h, k:k + 1],
                                                       part[:, k, 0 if h == 1 else 1, :], ALU.mult, ALU.add
                                                       ).then_inc(q.step, 1)
                        for k in (2 * pair, 2 * pair + 1):
                            n = t0 + k
                            dve.wait_ge(q.step, done + 5 + k % 2)
                            if not (first and half == 0 and k == 0):
                                dve.wait_ge(q.row_ready, n)
                            before = rows[:, half, k - 1, 0:D] if k else rows[:, 1 - half, 3, 0:D]
                            v.scalar_tensor_tensor(rows[:, half, k, 0:D], before,
                                                   weights[:, half, HEADS, k:k + 1], part[:, k, 1, :], ALU.mult,
                                                   ALU.add).then_inc(q.row_ready, 1)

                over_halves(dve, step)

            @block.gpsimd
            def _(pool):
                def step(i, half, first):
                    pool.wait_ge(q.extras_ready, 2 * i + half + 1)
                    pool.wait_ge(q.fed, 4 * i + 2 * half + 2)
                    for k in range(4):
                        pool.wait_ge(q.row_ready, 8 * i + 4 * half + k + 1)
                        hold(pool, q.passed)
                        pool.indirect_dma_start(sums[:, :], bass.IndirectOffsetOnAxis(ap=sidx[:, half, k:k + 1],
                                                                                      axis=0),
                                                rows[:, half, k, :], None, bounds_check=ROWS - 1, oob_is_err=False
                                                ).then_inc(stored[half], 16)

                over_halves(pool, step)
                for half in range(2):
                    pool.wait_ge(stored[half], 64 * ITERS)

        fixup(nc, s, f"weigh_fix{layer}", sums, rows[:, 1, 3, :], D, banks)


def gat_nodes(nc, s, layer, x_rows, sums, x_next, att_next, x_first, out):
    last = layer == LAYERS - 1
    with ExitStack() as ctx:
        def sb(name, shape, dt=F32):
            return ctx.enter_context(nc.sbuf_tensor(f"{name}_{layer}", shape, dt))

        def pb(name, shape):
            return ctx.enter_context(nc.psum_tensor(f"{name}_{layer}", shape, F32))

        xs = sb("gx", [P, 2, 4, D + HEADS])
        ss = sb("gs", [P, 2, 4, W])
        firsts = sb("gf", [P, 2, 4, D + HEADS])
        own = sb("own", [P, 2, 4, HEADS])
        y = sb("y", [P, 2, 4, D])
        x_t = sb("gx_t", [P, 2, BLOCK])
        normal = sb("gnormal", [P, 2, 4, D])
        y_t = sb("gy_t", [P, BLOCK])
        base = sb("gbase", [P, 2, 4, D])
        total = sb("gtotal", [P, 2, 4, D])
        new = sb("gnew", [P, 2, 4, D + HEADS])
        new_t = sb("gnew_t", [P, BLOCK])
        node_att = sb("gatt", [P, 2, 4, 2 * HEADS])
        stats = sb("gstats", [P, 4, 6])
        moments = sb("gmoments", [P, 2, 4, 2])
        rstd = sb("grstd", [P, 2, 4])
        p_x = pb("gp_x", [P, BLOCK])
        heads = [pb(f"gp_h{c}", [P, BLOCK]) for c in range(4)]
        p_y = pb("gp_y", [P, BLOCK])
        p_skip = pb("gp_skip", [P, 4, D])
        p_tail = pb("gp_tail", [P, BLOCK])
        n_loads = 3 if last else 2
        own_steps = 2
        back_steps = 2 + MOMENT_STEPS if last else 1
        stores = 1 if last else 2

        with phase(nc, f"gat{layer}", "loaded_a", "loaded_b", "turned", "copied", "y_base", "own_step", "headed",
                   "summed", "y_turned", "y_copied", "base_ready", "skipped", "step", "rstd_ready", "inverted",
                   "normed", "rows_turned", "rows_copied", "scored", "tail_step", "stored_a", "stored_b", "passed"
                   ) as (block, q):
            loaded = [q.loaded_a, q.loaded_b]
            stored = [q.stored_a, q.stored_b]

            @block.sync
            def _(sp):
                def step(j, slot, first):
                    if not first:
                        sp.wait_ge(q.turned, j - 1)
                        sp.wait_ge(q.y_base, j - 1)
                        hold(sp, q.passed)
                        sp.wait_ge(q.own_step, own_steps * (j - 1))
                        if last:
                            hold(sp, q.passed)
                            sp.wait_ge(q.step, back_steps * (j - 1))
                        hold(sp, q.passed)
                    sp.dma_start(xs[:, slot, :, :], nodes_of(x_rows, start_of(j))).then_inc(loaded[slot], 16)
                    sp.dma_start(ss[:, slot, :, :], nodes_of(sums, start_of(j))).then_inc(loaded[slot], 16)
                    if last:
                        sp.dma_start(firsts[:, slot, :, :], nodes_of(x_first, start_of(j))).then_inc(loaded[slot], 16)

                over_blocks(sp, step)

            @block.gpsimd
            def _(pool):
                def store(j, slot):
                    if not last:
                        store_rows(pool, q, stored, new, node_att, x_next, att_next, j, slot)
                        return
                    pool.wait_ge(q.normed, 4 * (j + 1))
                    if is_block(j, NBLOCKS - 1):
                        pool.wait_ge(stored[0], 8 * NBLOCKS)
                        pool.wait_ge(stored[1], 8 * (NBLOCKS - 2))
                    pool.dma_start(nodes_of(out, start_of(j)), normal[:, slot]).then_inc(stored[slot], 16)

                def skip_base(j, slot, first):
                    pool.wait_ge(q.summed, 16 * j + 16)
                    if not first:
                        pool.wait_ge(q.skipped, j)
                    nc.gpsimd.tensor_tensor(base[:, slot], y[:, slot], over_features(s.skip_b[:, layer, :]), ALU.add
                                            ).then_inc(q.base_ready, 1)

                def step(j, slot, first):
                    loads_done(pool, loaded[slot], j, slot, n_loads)
                    if not first:
                        pool.wait_ge(q.base_ready, j - 1)
                        pool.wait_ge(q.y_turned, j - 1)
                    nc.gpsimd.tensor_tensor(y[:, slot], ss[:, slot, :, 0:D], over_features(s.gat_b[:, layer, :]),
                                            ALU.add).then_inc(q.y_base, 1)
                    if not (first and slot == 0):
                        skip_base(j - 1, 1 - slot, is_block(j, 1))
                    if not first:
                        store(j - 2, slot)

                over_blocks(pool, step)
                skip_base(NBLOCKS - 1, 1, False)
                store(NBLOCKS - 2, 0)
                store(NBLOCKS - 1, 1)
                for slot in range(2):
                    pool.wait_ge(stored[slot], 8 * stores * NBLOCKS)

            @block.tensor
            def _(pe):
                def skip(j, slot, very_first):
                    pe.wait_ge(q.summed, 16 * j + 16)
                    if not very_first:
                        pe.wait_ge(q.y_copied, j)
                    for c in range(4):
                        mm = nc.tensor.transpose(p_y[:, c * P:(c + 1) * P], y[:, slot, c, :], s.ident[:, :])
                    mm.then_inc(q.y_turned, 1)
                    pe.wait_ge(q.y_copied, j + 1)
                    if not very_first:
                        pe.wait_ge(q.step, back_steps * (j - 1) + 1)
                    for c in range(4):
                        mm = nc.tensor.matmul(p_skip[:, c, :], y_t[:, c * P:(c + 1) * P], s.skip_w[:, layer, :],
                                              start=True, stop=True)
                    mm.then_inc(q.skipped, 1)

                def tail(j, slot):
                    if not last:
                        score_rows(nc, s, q, pe, p_tail, new, new_t, layer + 1, j, slot)

                def step(j, slot, first):
                    very_first = first and slot == 0
                    loads_done(pe, loaded[slot], j, slot, n_loads)
                    if not very_first:
                        pe.wait_ge(q.copied, j)
                    for c in range(4):
                        mm = nc.tensor.transpose(p_x[:, c * P:(c + 1) * P], xs[:, slot, c, 0:D], s.ident[:, :])
                    mm.then_inc(q.turned, 1)
                    pe.wait_ge(q.copied, j + 1)
                    for c in range(4):
                        if not very_first:
                            pe.wait_ge(q.summed, 16 * (j - 1) + 8 * (c // 2) + 7 + c % 2)
                        nc.tensor.matmul(heads[c][:, :], x_t[:, slot, c * P:(c + 1) * P], s.gat_w[:, layer, :],
                                         start=True, stop=True).then_inc(q.headed, 1)
                    if not very_first:
                        skip(j - 1, 1 - slot, is_block(j, 1))
                    if not first:
                        tail(j - 2, slot)

                over_blocks(pe, step)
                skip(NBLOCKS - 1, 1, False)
                tail(NBLOCKS - 2, 0)
                tail(NBLOCKS - 1, 1)

            @block.scalar
            def _(act):
                def copy_y(j, very_first):
                    act.wait_ge(q.y_turned, j + 1)
                    if not very_first:
                        act.wait_ge(q.skipped, j)
                    nc.scalar.copy(y_t[:, :], p_y[:, :]).then_inc(q.y_copied, 1)

                def tail(j, slot):
                    if last:
                        deviation(nc, s, q, act, moments, rstd, j, slot, back_steps)
                    else:
                        copy_rows(nc, q, act, p_tail, new_t, j)

                def step(j, slot, first):
                    act.wait_ge(q.turned, j + 1)
                    if not first:
                        act.wait_ge(q.headed, 4 * (j - 1))
                    nc.scalar.copy(x_t[:, slot, :], p_x[:, :]).then_inc(q.copied, 1)
                    if last and not first:
                        tail(j - 2, slot)
                    if not (first and slot == 0):
                        copy_y(j - 1, is_block(j, 1))
                    if not last and not first:
                        tail(j - 2, slot)

                over_blocks(act, step)
                copy_y(NBLOCKS - 1, False)
                tail(NBLOCKS - 2, 0)
                tail(NBLOCKS - 1, 1)

            @block.vector
            def _(dve):
                v = nc.vector

                def back(j, slot, first):
                    dve.wait_ge(q.skipped, j + 1)
                    dve.wait_ge(q.base_ready, j + 1)
                    if last and not first:
                        dve.wait_ge(q.normed, 4 * (j - 1))
                    steps = Steps(dve, q.step, back_steps * j, q.passed)
                    steps.then(v.tensor_tensor(total[:, slot], base[:, slot], p_skip[:, :, :], ALU.add))
                    steps.wait()
                    if last:
                        steps.then(v.tensor_tensor(total[:, slot], total[:, slot], firsts[:, slot, :, 0:D], ALU.add))
                        steps.wait()
                        row_moments(nc, steps, total[:, slot], stats, moments[:, slot])
                    else:
                        if not first:
                            dve.wait_ge(stored[slot], 16 * (j - slot))
                        v.tensor_scalar(new[:, slot, :, 0:D], total[:, slot], 0.0, None, ALU.max
                                        ).then_inc(q.normed, 4)

                def tail(j, slot, first):
                    if last:
                        if not first:
                            dve.wait_ge(stored[slot], 8 * (j - slot))
                        normalise(nc, q, dve, total[:, slot], normal[:, slot], moments, rstd, j, slot)
                        return
                    dve.wait_ge(q.scored, j + 1)
                    steps = Steps(dve, q.tail_step, HEAD_STEPS * j)
                    head_rows(nc, s, steps, p_tail[:, 0:32].rearrange("p (c k) -> p c k", c=4), new, node_att, slot)

                def step(j, slot, first):
                    very_first = first and slot == 0
                    loads_done(dve, loaded[slot], j, slot, n_loads)
                    if not first:
                        dve.wait_ge(q.summed, 16 * (j - 1))
                    flag = ss[:, slot, :, D + HEADS:D + HEADS + 1].to_broadcast([P, 4, HEADS])
                    v.tensor_scalar(own[:, slot], flag, -1.0 / HEADS, 1.0 / HEADS, ALU.mult, ALU.add
                                    ).then_inc(q.own_step, 1)
                    dve.wait_ge(q.own_step, own_steps * j + 1)
                    v.tensor_tensor(own[:, slot], own[:, slot], ss[:, slot, :, D:D + HEADS], ALU.add
                                    ).then_inc(q.own_step, 1)
                    dve.wait_ge(q.own_step, own_steps * j + 2)
                    dve.wait_ge(q.y_base, j + 1)
                    for pair in range(2):
                        done = 16 * j + 8 * pair
                        for h in range(HEADS):
                            for c in (2 * pair, 2 * pair + 1):
                                if h:
                                    dve.wait_ge(q.summed, done + 2 * (h - 1) + c % 2 + 1)
                                else:
                                    dve.wait_ge(q.headed, 4 * j + c + 1)
                                v.scalar_tensor_tensor(y[:, slot, c, :], heads[c][:, h * D:(h + 1) * D],
                                                       own[:, slot, c, h:h + 1], y[:, slot, c, :], ALU.mult, ALU.add
                                                       ).then_inc(q.summed, 1)
                    if last and not first:
                        tail(j - 2, slot, is_block(j, 2) or is_block(j, 3))
                    if not very_first:
                        back(j - 1, 1 - slot, is_block(j, 1) or is_block(j, 2))
                    if not last and not first:
                        tail(j - 2, slot, False)

                over_blocks(dve, step)
                if last:
                    tail(NBLOCKS - 2, 0, False)
                back(NBLOCKS - 1, 1, False)
                if not last:
                    tail(NBLOCKS - 2, 0, False)
                tail(NBLOCKS - 1, 1, False)


def build(nc, x, src, dst, w, out):
    def dram(name, shape, dt=F32):
        return nc.dram_tensor(name, shape, dt).ap()

    half_sorted = dram("half_sorted", (SLOTS, 2), I32)
    sorted_pairs = dram("sorted_pairs", (SLOTS, 2), I32)
    sums_in = dram("sums_in", (ROWS, W))
    sums_out = dram("sums_out", (ROWS, W))
    turned_x = dram("turned_x", (HALVES * P, BLOCK))
    x_rows = [dram(f"x_rows{l}", (N, D + HEADS)) for l in range(LAYERS)]
    att_rows = [dram(f"att_rows{l}", (N, 2 * HEADS)) for l in range(LAYERS)]

    with ExitStack() as ctx:
        def sb(name, shape, dt=F32):
            return ctx.enter_context(nc.sbuf_tensor(name, shape, dt))

        s = Buffers()
        s.ident = sb("ident", [P, P])
        s.lower = sb("lower", [P, P])
        s.upper = sb("upper", [P, P])
        s.upper_in = sb("upper_in", [P, P])
        s.lower_in = sb("lower_in", [P, P])
        s.ones = sb("ones", [P, P])
        s.eps = sb("eps", [P, 1])
        s.iota256 = sb("iota256", [P, 256])
        s.dummy = sb("dummy_row", [P, 1])
        s.upper_b = sb("upper_b", [P, P], BF16)
        s.lower_in_b = sb("lower_in_b", [P, P], BF16)
        s.ones_b = sb("ones_b", [P, P], BF16)
        s.iota256_b = sb("iota256_b", [P, 256], BF16)
        s.disorder = sb("disorder", [1, 1], I32)
        s.pairs = sb("pairs", [P, T, 2], I32)
        s.source = sb("source", [P, T])
        s.gather_rows = sb("gather_rows", [P, T, 2], I32)
        s.scatter_rows = sb("scatter_rows", [P, T], I32)
        s.same = sb("same", [P, T])
        s.same_in = sb("same_in", [P, T])
        s.reset = sb("reset", [P, T])
        s.reset_in = sb("reset_in", [P, T])
        s.ends = sb("ends", [P, T])
        s.goes_on = sb("goes_on", [P, T])
        s.fix_rows = sb("fix_rows", [P, 2], I32)
        s.mask_first = sb("mask_first", [P, P])
        s.mask_last = sb("mask_last", [P, P])
        s.chunk_same = sb("chunk_same", [HEADS, P])
        s.chunk_goes_on = sb("chunk_goes_on", [HEADS, P])
        s.chunk_reset = sb("chunk_reset", [HEADS, P])
        s.w_edge = sb("w_edge", [P, 2, 2 * D])
        s.w_msg2 = sb("w_msg2", [P, 2, D])
        s.b_edge = sb("b_edge", [P, 2 * D])
        s.b_msg2 = sb("b_msg2", [2, D])
        s.upd1 = sb("upd1", [P, 2, U])
        s.upd2 = sb("upd2", [P, 2, D])
        s.upd_b1 = sb("upd_b1", [P, 2])
        s.upd_b2 = sb("upd_b2", [P, D])
        s.gat_w = sb("gat_w", [P, LAYERS, HEADS * D])
        s.gat_b = sb("gat_b", [P, LAYERS, D])
        s.skip_w = sb("skip_w", [P, LAYERS, D])
        s.skip_b = sb("skip_b", [P, LAYERS, D])
        s.w_att = sb("w_att", [P, LAYERS, 2 * HEADS])
        make_constants(nc, s)
        zero_tables(nc, (sums_in, sums_out))
        load_weights(nc, s, w)
        with ExitStack() as sorting:
            def tmp(name, shape, dt=F32):
                return sorting.enter_context(nc.sbuf_tensor(name, shape, dt))

            s.digit_i, s.digits = tmp("digit_i", [P, T], I32), tmp("digits", [P, T])
            s.totals, s.base = tmp("totals", [P, 256]), tmp("base", [P, 256])
            s.picked, s.rank_ring = tmp("picked", [P, 256]), tmp("rank_ring", [P, 8])
            s.ranks, s.place = tmp("ranks", [P, T]), tmp("place", [P, T], I32)
            s.place_hi, s.place_ring = tmp("place_hi", [P, T], I32), tmp("place_ring", [P, 2, 4], I32)
            s.pair_ring = tmp("pair_ring", [P, 2, 4, 2], I32)
            load_edges(nc, s, src, dst)
            disorder = find_disorder(nc, s, sorted_pairs)
            with nc.If(disorder > 0):
                nc.all_engine_barrier()
                sort_edges(nc, s, half_sorted, sorted_pairs)
        plan_segments(nc, s, sorted_pairs)
        message_edges(nc, s, x, sums_in, sums_out)
        update_nodes(nc, s, x, sums_in, sums_out, x_rows[0], att_rows[0])
        for layer in range(LAYERS):
            with nc.sbuf_tensor(f"edge_weights{layer}", [P, HEADS + 1, T], F32) as weights, \
                    nc.sbuf_tensor(f"self_weights{layer}", [P, T, HEADS], F32) as self_weights:
                s.weights, s.self_weights = weights, self_weights
                with nc.sbuf_tensor(f"edge_score{layer}", [P, HEADS, T], F32) as edge_score, \
                        nc.sbuf_tensor(f"self_score{layer}", [P, HEADS, T], F32) as self_score:
                    s.edge_score, s.self_score = edge_score, self_score
                    score_edges(nc, s, layer, x_rows[layer], att_rows[layer], turned_x)
                    attention_weights(nc, s, layer)
                weigh_edges(nc, s, layer, turned_x, sums_in)
            after = min(layer + 1, LAYERS - 1)
            gat_nodes(nc, s, layer, x_rows[layer], sums_in, x_rows[after], att_rows[after], x_rows[0], out)


_INS = ["x", "src", "dst", "L0_gnn_msg_W1", "L0_gnn_msg_b1", "L0_gnn_msg_W2", "L0_gnn_msg_b2", "L0_gnn_rev_W1",
        "L0_gnn_rev_b1", "L0_gnn_rev_W2", "L0_gnn_rev_b2", "L0_gnn_upd_W1", "L0_gnn_upd_b1", "L0_gnn_upd_W2",
        "L0_gnn_upd_b2", "L1_gnn_W", "L1_gnn_att_src", "L1_gnn_att_dst", "L1_gnn_bias", "L1_gnn_skip_W",
        "L1_gnn_skip_b"]


def program(nc, shapes):
    args = {name: nc.dram_tensor(f"in_{name}", shape, dt, kind="ExternalInput").ap()
            for name, (shape, dt) in shapes.items()}
    out = nc.dram_tensor("out", (N, D), F32, kind="ExternalOutput").ap()
    w = {name[7:]: ap for name, ap in args.items() if name.startswith("L0_gnn_")}
    w |= {"gat_W": args["L1_gnn_W"], "gat_bias": args["L1_gnn_bias"], "skip_W": args["L1_gnn_skip_W"],
          "skip_b": args["L1_gnn_skip_b"], "att_src": args["L1_gnn_att_src"], "att_dst": args["L1_gnn_att_dst"]}
    build(nc, args["x"], args["src"], args["dst"], w, out)


def kernel(**inputs):
    import numpy as np
    import concourse.bacc as bacc
    from concourse.bass_utils import run_bass_kernel_spmd

    nc = bacc.Bacc("TRN2", target_bir_lowering=False, num_devices=1)
    arrays = {name: np.ascontiguousarray(inputs[name]) for name in _INS}
    program(nc, {name: (a.shape, mybir.dt.from_np(a.dtype)) for name, a in arrays.items()})
    r = run_bass_kernel_spmd(nc, [{f"in_{name}": a for name, a in arrays.items()}], core_ids=[0])
    return r.results[0]["out"]
```

```python
from collections import namedtuple
from contextlib import ExitStack, contextmanager

import concourse.bass as bass
from concourse import mybir

ALU = mybir.AluOpType
ACT = mybir.ActivationFunctionType
AX = mybir.AxisListType
F32 = mybir.dt.float32
BF16 = mybir.dt.bfloat16
I32 = mybir.dt.int32

P = 128
N = 50000
E = 50000
D = 128
U = 256
HEADS = 4
LAYERS = 3
T = -(-E // (P * 8)) * 8
SLOTS = P * T
HALVES = T // 4
ITERS = T // 8
W = 136
SIDE = SLOTS
ROWS = SLOTS + P
SKIP = float(1 << 20)
BLOCK = 512
NBLOCKS = -(-N // BLOCK)
BIG = 1.0e30
EPS = 1e-05
SLOPE = 0.2


@contextmanager
def phase(nc, name, *signals):
    sems = namedtuple("Signals", signals)(*[nc.alloc_semaphore(f"{name}_{s}") for s in signals])
    with nc.Block() as block:
        yield block, sems
    nc.clear_and_free_semaphores(list(sems))
    nc.all_engine_barrier()


class Buffers:
    pass


class Steps:

    def __init__(self, eng, sem, start=0, passed=None):
        self.eng, self.sem, self.n, self.passed = eng, sem, start, passed

    def then(self, ins):
        ins.then_inc(self.sem, 1)
        self.n = self.n + 1

    def wait(self):
        self.eng.wait_ge(self.sem, self.n)


def hold(eng, passed):
    eng.sem_inc(passed, 1)


def row_of(v):
    return v.rearrange("(a d) -> a d", a=1)


def make_constants(nc, s):
    with phase(nc, "const", "filled", "made") as (block, q):
        @block.gpsimd
        def _(pool):
            nc.gpsimd.memset(s.ident[:, :], 0.0).then_inc(q.filled, 1)
            nc.gpsimd.memset(s.lower[:, :], 1.0).then_inc(q.filled, 1)
            nc.gpsimd.memset(s.upper[:, :], 1.0).then_inc(q.filled, 1)
            nc.gpsimd.memset(s.upper_in[:, :], 1.0).then_inc(q.filled, 1)
            nc.gpsimd.memset(s.lower_in[:, :], 1.0).then_inc(q.filled, 1)
            nc.gpsimd.memset(s.ones[:, :], 1.0).then_inc(q.filled, 1)
            nc.gpsimd.memset(s.eps[:, :], EPS)
            nc.gpsimd.iota(s.iota256[:, :], [[1, 256]], base=0, channel_multiplier=0,
                           allow_small_or_imprecise_dtypes=True).then_inc(q.filled, 1)
            nc.gpsimd.iota(s.dummy[:, :], [[0, 1]], base=SIDE, channel_multiplier=1,
                           allow_small_or_imprecise_dtypes=True).then_inc(q.filled, 1)
            pool.wait_ge(q.filled, 8)
            nc.gpsimd.affine_select(out=s.ident[:, :], in_=s.ident[:, :], compare_op=ALU.not_equal, fill=1.0,
                                    base=0, pattern=[[-1, P]], channel_multiplier=1).then_inc(q.made, 1)
            nc.gpsimd.affine_select(out=s.lower[:, :], in_=s.lower[:, :], compare_op=ALU.is_gt, fill=0.0,
                                    base=0, pattern=[[-1, P]], channel_multiplier=1).then_inc(q.made, 1)
            nc.gpsimd.affine_select(out=s.upper[:, :], in_=s.upper[:, :], compare_op=ALU.is_gt, fill=0.0,
                                    base=0, pattern=[[1, P]], channel_multiplier=-1).then_inc(q.made, 1)
            nc.gpsimd.affine_select(out=s.upper_in[:, :], in_=s.upper_in[:, :], compare_op=ALU.is_ge, fill=0.0,
                                    base=0, pattern=[[1, P]], channel_multiplier=-1).then_inc(q.made, 1)
            nc.gpsimd.affine_select(out=s.lower_in[:, :], in_=s.lower_in[:, :], compare_op=ALU.is_ge, fill=0.0,
                                    base=0, pattern=[[-1, P]], channel_multiplier=1).then_inc(q.made, 1)

        @block.vector
        def _(dve):
            dve.wait_ge(q.made, 5)
            nc.vector.tensor_copy(s.upper_b[:, :], s.upper[:, :])
            nc.vector.tensor_copy(s.lower_in_b[:, :], s.lower_in[:, :])
            nc.vector.tensor_copy(s.ones_b[:, :], s.ones[:, :])
            nc.vector.tensor_copy(s.iota256_b[:, :], s.iota256[:, :])


@contextmanager
def zero_tables(nc, tables):
    part = 131
    counts = []
    stored = nc.alloc_semaphore("zeros_stored")
    with nc.sbuf_tensor("zeros", [P, part * W], F32) as zeros:
        with phase(nc, "zero", "cleared") as (block, q):
            @block.vector
            def _(dve):
                nc.vector.memset(zeros[:, :], 0.0).then_inc(q.cleared, 1)

            @block.sync
            def _(sp):
                sp.wait_ge(q.cleared, 1)
                n = 0
                for table in tables:
                    rows = table.rearrange("(p r) w -> p (r w)", p=P)
                    width = rows.shape[1]
                    for c in range(0, width, part * W):
                        n_cols = min(part * W, width - c)
                        sp.dma_start(rows[:, c:c + n_cols], zeros[:, 0:n_cols]).then_inc(stored, 16)
                        n += 1
                counts.append(n)

        yield
        with phase(nc, "zeroed") as (block, q):
            @block.sync
            def _(sp):
                sp.wait_ge(stored, 16 * counts[0])
    nc.clear_and_free_semaphores([stored])
    nc.all_engine_barrier()


def load_edges(nc, s, src, dst):
    whole = E // T
    rest = E - whole * T
    with nc.sbuf_tensor("keys_in", [P, T], I32) as keys, nc.sbuf_tensor("srcs_in", [P, T], I32) as srcs:
        with phase(nc, "edges", "padded", "loaded") as (block, q):
            @block.vector
            def _(dve):
                nc.vector.memset(keys[:, :], N).then_inc(q.padded, 1)
                nc.vector.memset(srcs[:, :], N).then_inc(q.padded, 1)
                dve.wait_ge(q.loaded, 64)
                nc.vector.tensor_copy(s.pairs[:, :, 0], keys[:, :])
                nc.vector.tensor_copy(s.pairs[:, :, 1], srcs[:, :])

            @block.sync
            def _(sp):
                sp.wait_ge(q.padded, 2)
                for sb, dram in ((keys, dst), (srcs, src)):
                    sp.dma_start(sb[0:whole, :], dram[0:whole * T].rearrange("(p t) -> p t", t=T)
                                 ).then_inc(q.loaded, 16)
                    sp.dma_start(sb[whole:whole + 1, 0:rest], row_of(dram[whole * T:E])).then_inc(q.loaded, 16)


def split_digit(nc, s, which):
    with phase(nc, f"digit{which}", "split") as (block, q):
        @block.vector
        def _(dve):
            op, by = (ALU.bitwise_and, 255) if which == 0 else (ALU.logical_shift_right, 8)
            nc.vector.tensor_scalar(s.digit_i[:, :], s.pairs[:, :, 0], by, None, op).then_inc(q.split, 1)
            dve.wait_ge(q.split, 1)
            nc.vector.tensor_copy(s.digits[:, :], s.digit_i[:, :])


def histogram(nc, s, which, counts, onehot):
    with phase(nc, f"hist{which}", "onehot_ready", "counted", "step") as (block, q):
        @block.vector
        def _(dve):
            def tile(i, k, first):
                n = i * 8 + k
                if not first or k >= 4:
                    dve.wait_ge(q.counted, n - 3)
                nc.vector.tensor_scalar(onehot[:, k % 4, :], s.iota256_b[:, :], s.digits[:, bass.ds(n, 1)], None,
                                        ALU.is_equal).then_inc(q.onehot_ready, 1)

            for k in range(8):
                tile(0, k, True)
            with dve.Fori(1, ITERS) as i:
                for k in range(8):
                    tile(i, k, False)
            dve.wait_ge(q.counted, T)
            nc.vector.tensor_copy(s.totals[:, :], counts[:, 0:256]).then_inc(q.step, 1)
            dve.wait_ge(q.step, 1)
            nc.vector.tensor_tensor_scan(s.base[:, :], s.totals[:, :], s.totals[:, :], 0.0, ALU.add,
                                         ALU.bypass).then_inc(q.step, 1)
            dve.wait_ge(q.step, 2)
            nc.vector.tensor_tensor(s.base[:, :], s.base[:, :], s.totals[:, :], ALU.subtract)

        @block.tensor
        def _(pe):
            def tile(n, k, first):
                pe.wait_ge(q.onehot_ready, n + 1)
                nc.tensor.matmul(counts[:, 0:256], s.ones_b[:, :], onehot[:, k % 4, :], start=first, stop=True,
                                 skip_group_check=True).then_inc(q.counted, 1)

            for k in range(8):
                tile(k, k, k == 0)
            with pe.Fori(1, ITERS) as i:
                for k in range(8):
                    tile(i * 8 + k, k, False)


def rank_edges(nc, s, which, counts, onehot):
    with phase(nc, f"rank{which}", "onehot_ready", "summed", "ranked", "advanced", "kept", "done") as (block, q):
        @block.vector
        def _(dve):
            def build(n, k, wait):
                if wait:
                    dve.wait_ge(q.advanced, n - 1)
                nc.vector.tensor_scalar(onehot[:, k % 2, :], s.iota256_b[:, :], s.digits[:, bass.ds(n, 1)], None,
                                        ALU.is_equal).then_inc(q.onehot_ready, 1)

            def block_of(i, first, last):
                for k in range(8):
                    n = i * 8 + k
                    if not (last and k == 7):
                        build(n + 1, k + 1, wait=not (first and k == 0))
                    dve.wait_ge(q.summed, n + 1)
                    if k == 0 and not first:
                        dve.wait_ge(q.kept, i)
                    if not (first and k == 0):
                        dve.wait_ge(q.ranked, n)
                    nc.vector.tensor_tensor_reduce(s.picked[:, :], counts[:, 0:256], onehot[:, k % 2, :], 1.0, 0.0,
                                                   ALU.mult, ALU.add, s.rank_ring[:, k:k + 1]).then_inc(q.ranked, 1)

            build(0, 0, wait=False)
            block_of(0, True, False)
            with dve.Fori(1, ITERS - 1) as i:
                block_of(i, False, False)
            block_of(ITERS - 1, False, True)

        @block.tensor
        def _(pe):
            def tile(n, k):
                pe.wait_ge(q.onehot_ready, n + 1)
                nc.tensor.matmul(counts[:, 0:256], s.upper_b[:, :], onehot[:, k % 2, :], start=False, stop=True,
                                 skip_group_check=True).then_inc(q.summed, 1)
                pe.wait_ge(q.ranked, n + 1)
                nc.tensor.matmul(counts[:, 0:256], s.lower_in_b[:, :], onehot[:, k % 2, :], start=False, stop=True,
                                 skip_group_check=True).then_inc(q.advanced, 1)

            nc.tensor.matmul(counts[:, 0:256], s.ident[:, :], s.base[:, :], start=True, stop=True,
                             skip_group_check=True)
            with pe.Fori(0, ITERS) as i:
                for k in range(8):
                    tile(i * 8 + k, k)

        @block.scalar
        def _(act):
            with act.Fori(0, ITERS) as i:
                act.wait_ge(q.ranked, i * 8 + 8)
                nc.scalar.copy(s.ranks[:, bass.ds(i * 8, 8)], s.rank_ring[:, :]).then_inc(q.kept, 1)


def place_edges(nc, s, which, out):
    with phase(nc, f"place{which}", "step", "ready", "stored_a", "stored_b", "passed") as (block, q):
        stored = [q.stored_a, q.stored_b]

        @block.vector
        def _(dve):
            steps = Steps(dve, q.step)
            steps.then(nc.vector.tensor_copy(s.place[:, :], s.ranks[:, :]))
            steps.wait()
            if which == 0:
                steps.then(nc.vector.tensor_scalar(s.digit_i[:, :], s.place[:, :], 127, None, ALU.bitwise_and))
                steps.then(nc.vector.tensor_scalar(s.place_hi[:, :], s.place[:, :], 7, None,
                                                   ALU.logical_shift_right))
                steps.wait()
                steps.then(nc.vector.scalar_tensor_tensor(s.place[:, :], s.digit_i[:, :], float(T),
                                                          s.place_hi[:, :], ALU.mult, ALU.add))
                steps.wait()

            def feed(i, half, wait):
                t0 = i * 8 + half * 4
                if wait:
                    dve.wait_ge(stored[half], i * 64)
                nc.vector.tensor_copy(s.place_ring[:, half, :], s.place[:, bass.ds(t0, 4)]).then_inc(q.ready, 1)
                nc.vector.tensor_copy(s.pair_ring[:, half, :, :], s.pairs[:, bass.ds(t0, 4), :]).then_inc(q.ready, 1)

            feed(0, 0, False)
            feed(0, 1, False)
            with dve.Fori(1, ITERS) as i:
                feed(i, 0, True)
                feed(i, 1, True)

        @block.gpsimd
        def _(pool):
            with pool.Fori(0, ITERS) as i:
                for half in range(2):
                    pool.wait_ge(q.ready, i * 4 + half * 2 + 2)
                    hold(pool, q.passed)
                    for k in range(4):
                        pool.indirect_dma_start(
                            out[:, :], bass.IndirectOffsetOnAxis(ap=s.place_ring[:, half, k:k + 1], axis=0),
                            s.pair_ring[:, half, k, :], None).then_inc(stored[half], 16)
            for half in range(2):
                pool.wait_ge(stored[half], ITERS * 64)


def reload_pairs(nc, s, table):
    with phase(nc, "reload", "loaded") as (block, q):
        @block.sync
        def _(sp):
            sp.dma_start(s.pairs[:, :, :], table.rearrange("(p t) w -> p t w", t=T)).then_inc(q.loaded, 16)
            sp.wait_ge(q.loaded, 16)


def find_disorder(nc, s, sorted_pairs):
    with ExitStack() as ctx:
        def sb(name, shape, dt=F32):
            return ctx.enter_context(nc.sbuf_tensor(name, shape, dt))

        before = sb("order_before", [P, T, 2], I32)
        key = sb("order_key", [P, T])
        key_before = sb("order_key_before", [P, T])
        least = sb("order_least", [P, 1])
        least_row = sb("order_least_row", [1, 2])
        row = ctx.enter_context(nc.psum_tensor("order_row", [P, 512], F32))
        with phase(nc, "order", "padded", "stored", "loaded", "step", "turned") as (block, q):
            @block.sync
            def _(sp):
                sp.dma_start(sorted_pairs.rearrange("(p t) w -> p t w", t=T), s.pairs[:, :, :]).then_inc(q.stored, 16)
                sp.wait_ge(q.stored, 16)
                sp.wait_ge(q.padded, 1)
                sp.dma_start(before[0:1, 1:T, :], sorted_pairs[0:T - 1, :].rearrange("(p t) w -> p t w", p=1)
                             ).then_inc(q.loaded, 16)
                sp.dma_start(before[1:P, :, :], sorted_pairs[T - 1:SLOTS - 1, :].rearrange("(p t) w -> p t w", t=T)
                             ).then_inc(q.loaded, 16)

            @block.vector
            def _(dve):
                v = nc.vector
                v.memset(before[:, :, :], -1).then_inc(q.padded, 1)
                dve.wait_ge(q.loaded, 32)
                steps = Steps(dve, q.step)
                steps.then(v.tensor_copy(key[:, :], s.pairs[:, :, 0]))
                steps.then(v.tensor_copy(key_before[:, :], before[:, :, 0]))
                steps.wait()
                steps.then(v.tensor_tensor(key[:, :], key[:, :], key_before[:, :], ALU.subtract))
                steps.wait()
                steps.then(v.tensor_reduce(least[:, :], key[:, :], AX.X, ALU.min))
                dve.wait_ge(q.turned, 1)
                steps.then(v.tensor_reduce(least_row[:, 0:1], row[0:1, 0:P], AX.X, ALU.min))
                steps.wait()
                v.tensor_scalar(s.disorder[:, :], least_row[:, 0:1], 0.0, None, ALU.is_lt)

            @block.tensor
            def _(pe):
                pe.wait_ge(q.step, 4)
                nc.tensor.transpose(row[0:1, 0:P], least[:, :], s.ident[:, :]).then_inc(q.turned, 1)
    return nc.values_load(s.disorder[0:1, 0:1], min_val=0, max_val=1)


def sort_edges(nc, s, half_sorted, sorted_pairs):
    with nc.psum_tensor("counts", [P, 512], F32) as counts, \
            nc.sbuf_tensor("onehot", [P, 4, 256], BF16) as onehot:
        for which, out in enumerate((half_sorted, sorted_pairs)):
            if which:
                reload_pairs(nc, s, half_sorted)
            split_digit(nc, s, which)
            histogram(nc, s, which, counts, onehot)
            rank_edges(nc, s, which, counts, onehot)
            place_edges(nc, s, which, out)


def plan_segments(nc, s, sorted_pairs):
    flat = sorted_pairs
    with ExitStack() as ctx:
        def sb(name, shape, dt):
            return ctx.enter_context(nc.sbuf_tensor(name, shape, dt))

        before = sb("before", [P, T, 2], I32)
        after = sb("after", [P, T, 2], I32)
        key = sb("key", [P, T], F32)
        key_before = sb("key_before", [P, T], F32)
        key_after = sb("key_after", [P, T], F32)
        first = sb("first", [P, T], F32)
        target = sb("target", [P, T], F32)
        clipped = sb("clipped", [P, T, 2], F32)
        one = sb("one", [P, 8], F32)
        slot_number = sb("slot_number", [P, T], I32)
        bcast = sb("bcast", [P, P], F32)
        rows = ctx.enter_context(nc.psum_tensor("plan_rows", [P, 4, P], F32))
        whole_rows = ctx.enter_context(nc.psum_tensor("plan_whole", [P, 4, P], F32))
        with phase(nc, "plan", "padded", "loaded", "numbered", "step", "turn", "turned") as (block, q):
            @block.sync
            def _(sp):
                sp.dma_start(s.pairs[:, :, :], flat.rearrange("(p t) w -> p t w", t=T)).then_inc(q.loaded, 16)
                sp.wait_ge(q.padded, 2)
                sp.dma_start(before[0:1, 1:T, :], flat[0:T - 1, :].rearrange("(p t) w -> p t w", p=1)
                             ).then_inc(q.loaded, 16)
                sp.dma_start(before[1:P, :, :], flat[T - 1:SLOTS - 1, :].rearrange("(p t) w -> p t w", t=T)
                             ).then_inc(q.loaded, 16)
                sp.dma_start(after[0:P - 1, :, :], flat[1:SLOTS - T + 1, :].rearrange("(p t) w -> p t w", t=T)
                             ).then_inc(q.loaded, 16)
                sp.dma_start(after[P - 1:P, 0:T - 1, :], flat[SLOTS - T + 1:SLOTS, :].rearrange(
                    "(p t) w -> p t w", p=1)).then_inc(q.loaded, 16)

            @block.gpsimd
            def _(pool):
                nc.gpsimd.iota(slot_number[:, :], pattern=[[1, T]], base=0, channel_multiplier=T
                               ).then_inc(q.numbered, 1)

            @block.vector
            def _(dve):
                v = nc.vector
                dve.wait_ge(q.numbered, 1)
                v.tensor_copy(s.position[:, :], slot_number[:, :]).then_inc(q.numbered, 1)
                dve.wait_ge(q.numbered, 2)
                v.tensor_scalar(s.position[:, :], s.position[:, :], -SKIP, None, ALU.add)
                v.memset(before[:, :, :], -1).then_inc(q.padded, 1)
                v.memset(after[:, :, :], -1).then_inc(q.padded, 1)
                dve.wait_ge(q.loaded, 80)
                steps = Steps(dve, q.step)
                steps.then(v.tensor_copy(key[:, :], s.pairs[:, :, 0]))
                steps.then(v.tensor_copy(key_before[:, :], before[:, :, 0]))
                steps.then(v.tensor_copy(key_after[:, :], after[:, :, 0]))
                steps.then(v.tensor_copy(s.source[:, :], s.pairs[:, :, 1]))
                steps.then(v.tensor_scalar(clipped[:, :, 0], s.pairs[:, :, 1], float(N - 1), None, ALU.min))
                steps.then(v.tensor_scalar(clipped[:, :, 1], s.pairs[:, :, 0], float(N - 1), None, ALU.min))
                steps.wait()
                steps.then(v.tensor_copy(s.gather_rows[:, :, :], clipped[:, :, :]))
                steps.then(v.tensor_tensor(s.same[:, :], key[:, :], key_before[:, :], ALU.is_equal))
                steps.then(v.tensor_tensor(s.goes_on[:, :], key[:, :], key_after[:, :], ALU.is_equal))
                steps.then(v.tensor_scalar(first[:, :], key[:, :], key[:, 0:1], None, ALU.is_equal))
                steps.wait()
                steps.then(v.tensor_copy(s.same_in[:, :], s.same[:, :]))
                steps.then(v.tensor_scalar(s.reset[:, :], s.same[:, :], -1.0, BIG, ALU.add, ALU.mult))
                steps.then(v.tensor_scalar(s.ends[:, :], s.goes_on[:, :], -1.0, 1.0, ALU.mult, ALU.add))
                steps.then(v.tensor_scalar(first[:, :], first[:, :], s.same[:, 0:1], None, ALU.mult))
                steps.then(v.tensor_tensor(one[:, 4:5], key[:, 0:1], key[:, T - 1:T], ALU.is_equal))
                steps.then(v.tensor_copy(one[:, 2:3], key[:, 0:1]))
                steps.then(v.tensor_copy(one[:, 3:4], key[:, T - 1:T]))
                steps.wait()
                steps.then(v.memset(s.same_in[:, 0:1], 0.0))
                steps.then(v.tensor_copy(s.reset_in[:, :], s.reset[:, :]))
                steps.then(v.tensor_tensor(one[:, 0:1], one[:, 4:5], s.same[:, 0:1], ALU.mult))
                steps.then(v.tensor_tensor(one[:, 1:2], one[:, 4:5], s.goes_on[:, T - 1:T], ALU.mult))
                steps.then(v.tensor_scalar(target[:, :], key[:, :], -1.0, s.dummy[:, 0:1], ALU.mult, ALU.add))
                steps.wait()
                steps.then(v.memset(s.reset_in[:, 0:1], -BIG))
                steps.then(v.tensor_tensor(target[:, :], target[:, :], first[:, :], ALU.mult))
                steps.wait()
                steps.then(v.tensor_tensor(target[:, :], target[:, :], key[:, :], ALU.add))
                steps.wait()
                steps.then(v.scalar_tensor_tensor(target[:, :], s.goes_on[:, :], SKIP, target[:, :], ALU.mult,
                                                  ALU.max))
                steps.wait()
                steps.then(v.memset(target[:, T - 1:T], SKIP))
                steps.wait()
                steps.then(v.tensor_copy(s.scatter_rows[:, :], target[:, :]))

                steps.then(v.tensor_scalar(one[:, 5:6], one[:, 4:5], -1.0, 1.0, ALU.mult, ALU.add))
                steps.wait()
                steps.then(v.tensor_tensor(one[:, 5:6], one[:, 5:6], s.same[:, 0:1], ALU.mult))
                steps.wait()
                steps.then(v.tensor_scalar(one[:, 5:6], one[:, 5:6], -SKIP, SKIP, ALU.mult, ALU.add))
                steps.then(v.tensor_scalar(one[:, 6:7], s.goes_on[:, T - 1:T], SKIP, None, ALU.mult))
                steps.wait()
                steps.then(v.tensor_tensor(one[:, 5:6], one[:, 5:6], one[:, 2:3], ALU.max))
                steps.then(v.tensor_tensor(one[:, 6:7], one[:, 6:7], one[:, 3:4], ALU.max))
                steps.wait()
                steps.then(v.tensor_copy(s.fix_rows[:, :], one[:, 5:7]))

                for j in range(4):
                    if j:
                        dve.wait_ge(q.turned, j)
                    nc.vector.tensor_copy(bcast[:, :], one[:, j:j + 1].to_broadcast([P, P])).then_inc(q.turn, 1)
                dve.wait_ge(q.turned, 4)
                steps.then(v.scalar_tensor_tensor(s.mask_first[:, :], rows[:, 2, :], one[:, 3:4], s.upper[:, :],
                                                  ALU.is_equal, ALU.mult))
                steps.then(v.scalar_tensor_tensor(s.mask_last[:, :], rows[:, 3, :], one[:, 3:4], s.upper_in[:, :],
                                                  ALU.is_equal, ALU.mult))
                steps.then(v.tensor_copy(s.chunk_same[:, :], rows[0:HEADS, 0, :]))
                steps.then(v.tensor_copy(s.chunk_goes_on[:, :], rows[0:2 * HEADS, 1, :]))
                steps.then(v.tensor_scalar(s.chunk_reset[:, :], rows[0:HEADS, 0, :], -1.0, BIG, ALU.add, ALU.mult))

            @block.tensor
            def _(pe):
                for j in range(4):
                    pe.wait_ge(q.turn, j + 1)
                    nc.tensor.transpose(rows[:, j, :], bcast[:, :], s.ident[:, :]).then_inc(q.turned, 1)


def load_weights(nc, s, w):
    loads = []

    def to(sb, dram):
        loads.append((sb, dram))

    for n in range(2):
        mine, theirs = ("msg", "rev")
        to(s.w_edge[:, n, 0:D], w[f"{mine}_W1"][n * D:(n + 1) * D, :])
        to(s.w_edge[:, n, D:2 * D], w[f"{theirs}_W1"][(1 - n) * D:(2 - n) * D, :])
        to(s.w_msg2[:, n, :], w[("msg_W2", "rev_W2")[n]])
        to(s.b_edge[:, n * D:(n + 1) * D], row_of(w[("msg_b1", "rev_b1")[n]]).to_broadcast([P, D]))
        to(s.b_msg2[n:n + 1, :], row_of(w[("msg_b2", "rev_b2")[n]]))
        to(s.upd1[:, n, :], w["upd_W1"][n * D:(n + 1) * D, :])
        to(s.upd2[:, n, :], w["upd_W2"][n * D:(n + 1) * D, :])
    to(s.upd_b1[:, :], w["upd_b1"].rearrange("(c p) -> p c", p=P))
    to(s.upd_b2[:, :], row_of(w["upd_b2"]).to_broadcast([P, D]))
    for l in range(LAYERS):
        to(s.gat_w[:, l, :], w["gat_W"][l])
        to(s.skip_w[:, l, :], w["skip_W"][l])
        to(s.skip_b[:, l, :], w["skip_b"][l:l + 1, :].to_broadcast([P, D]))
    with nc.sbuf_tensor("att_rows", [P, LAYERS, 2, HEADS * D], F32) as att_rows, \
            nc.sbuf_tensor("att_scratch", [P, 4, D], F32) as scratch, \
            nc.sbuf_tensor("gat_b", [P, LAYERS], F32) as gat_b, \
            nc.sbuf_tensor("gat_b_wide", [P, LAYERS, P], F32) as gat_b_wide, \
            nc.psum_tensor("bias_sums", [P, LAYERS, D], F32) as bias_sums:
        to(gat_b[:, :], w["gat_bias"].rearrange("l p -> p l"))
        for l in range(LAYERS):
            for j, name in enumerate(("att_src", "att_dst")):
                to(att_rows[:, l, j, :], w[name][l:l + 1].rearrange("a h d -> a (h d)").to_broadcast([P, HEADS * D]))
        with phase(nc, "weights", "loaded", "step", "skip_ready", "bias_summed") as (block, q):
            @block.sync
            def _(sp):
                with nc.allow_non_contiguous_dma(reason="a few biases by partitions"):
                    for sb, dram in loads:
                        sp.dma_start(sb, dram).then_inc(q.loaded, 16)

            @block.vector
            def _(dve):
                dve.wait_ge(q.loaded, 16 * len(loads))
                for l in range(LAYERS):
                    nc.vector.tensor_tensor(s.skip_w[:, l, :], s.skip_w[:, l, :], s.ident[:, :], ALU.add
                                            ).then_inc(q.skip_ready, 1)
                    nc.vector.tensor_copy(gat_b_wide[:, l, :], gat_b[:, l:l + 1].to_broadcast([P, P])
                                          ).then_inc(q.skip_ready, 1)
                n = 0
                for l in range(LAYERS):
                    for j in range(2):
                        for h in range(HEADS):
                            if n >= 4:
                                dve.wait_ge(q.step, n - 3)
                            nc.vector.tensor_tensor_reduce(
                                scratch[:, n % 4, :], s.gat_w[:, l, h * D:(h + 1) * D],
                                att_rows[:, l, j, h * D:(h + 1) * D], 1.0, 0.0, ALU.mult, ALU.add,
                                s.w_att[:, l, j * HEADS + h:j * HEADS + h + 1]).then_inc(q.step, 1)
                            n += 1
                dve.wait_ge(q.bias_summed, 1)
                nc.vector.tensor_tensor(s.skip_b[:, :, :], s.skip_b[:, :, :], bias_sums[:, :, :], ALU.add)

            @block.tensor
            def _(pe):
                pe.wait_ge(q.skip_ready, 2 * LAYERS)
                for l in range(LAYERS):
                    mm = nc.tensor.matmul(bias_sums[:, l, :], gat_b_wide[:, l, :], s.skip_w[:, l, :], start=True,
                                          stop=True)
                mm.then_inc(q.bias_summed, 1)


def message_edges(nc, s, x, sums_in, sums_out):
    with ExitStack() as ctx:
        def sb(name, shape, dt=F32):
            return ctx.enter_context(nc.sbuf_tensor(name, shape, dt))

        def pb(name, shape):
            return ctx.enter_context(nc.psum_tensor(name, shape, F32))

        gidx = sb("gidx", [P, 2, 4, 2], I32)
        sidx = sb("sidx", [P, 2, 4], I32)
        ridx = sb("ridx", [P, 2, 4], I32)
        ridx_f = sb("ridx_f", [P, 4])
        src4 = sb("src4", [P, 2, 4])
        repeats = sb("repeats", [P, 4])
        x_src = sb("x_src", [P, 2, 4, D])
        x_dst = sb("x_dst", [P, 2, 4, D])
        x_t = sb("x_t", [P, 2, 2, P])
        hidden = sb("hidden", [P, 2, 2, D])
        relus = sb("relus", [P, 2, 2, W])
        equal = sb("equal", [P, 2, P])
        pairs_scratch = sb("pairs_scratch", [P, P])
        rows = sb("rows", [P, 2, 4, W])
        rev_rows = sb("rev_rows", [P, 2, 4, W])
        turned = [pb(f"turned{j}", [P, 2, 256]) for j in range(2)]
        srcs_t = [pb(f"srcs_t{j}", [P, 512]) for j in range(2)]
        hid = [pb(f"hid{j}", [P, 2, 256]) for j in range(2)]
        dedup = [pb(f"dedup{j}", [P, 512]) for j in range(2)]

        with phase(nc, "msg_init", "x") as (block, q):
            @block.vector
            def _(dve):
                nc.vector.memset(relus[:, :, :, :], 0.0).then_inc(q.x, 1)
                nc.vector.memset(rows[:, :, :, :], 0.0)
                dve.wait_ge(q.x, 1)
                nc.vector.memset(relus[:, :, :, D:D + 1], 1.0)

        with phase(nc, "msg", "gidx_ready", "gathered_a", "gathered_b", "gathered_c", "gathered_d", "src4_ready", "sidx_ready",
                   "x_turned", "srcs_turned", "x_t_ready", "hid_ready", "hidden_ready", "relu_ready",
                   "equal_ready", "counted", "row_ready", "rev_summed", "rev_ready", "stored_a", "stored_b", "passed",
                   "rev_stored", "ridx_step") as (block, q):
            gathered = [q.gathered_a, q.gathered_b, q.gathered_c, q.gathered_d]
            stored = [q.stored_a, q.stored_b]

            @block.gpsimd
            def _(pool):
                def gather(i, half, k, wait_x):
                    if k == 0:
                        pool.wait_ge(q.gidx_ready, 2 * i + half + 1)
                        if wait_x:
                            pool.wait_ge(q.x_turned, 4 * (2 * i + half - 1))
                        hold(pool, q.passed)
                    for j, to in enumerate((x_src, x_dst)):
                        pool.indirect_dma_start(to[:, half, k, :], None, x[:, :], bass.IndirectOffsetOnAxis(
                            ap=gidx[:, half, k, j:j + 1], axis=0)).then_inc(gathered[2 * half + k // 2], 16)

                def scatter(i, half, k, first=False):
                    n = 8 * i + 4 * half + k
                    if k == 0:
                        pool.wait_ge(q.sidx_ready, 2 * (2 * i + half + 1))
                        pool.wait_ge(q.ridx_step, 3 * (2 * i + half + 1))
                    pool.wait_ge(q.row_ready, n + 1)
                    hold(pool, q.passed)
                    pool.indirect_dma_start(sums_in[:, :], bass.IndirectOffsetOnAxis(
                        ap=sidx[:, half, k:k + 1], axis=0), rows[:, half, k, :], None,
                        bounds_check=ROWS - 1, oob_is_err=False).then_inc(stored[half], 16)
                    pool.wait_ge(q.rev_ready, n + 1)
                    if not first:
                        pool.wait_ge(q.rev_stored, 16 * n)
                    hold(pool, q.passed)
                    pool.indirect_dma_start(sums_out[:, :], bass.IndirectOffsetOnAxis(
                        ap=ridx[:, half, k:k + 1], axis=0), rev_rows[:, half, k, :], None,
                        compute_op=ALU.add).then_inc(q.rev_stored, 16)

                for k in range(4):
                    gather(0, 0, k, False)
                for k in range(4):
                    gather(0, 1, k, False)
                for k in range(4):
                    gather(1, 0, k, True)
                    scatter(0, 0, k, first=k == 0)
                with pool.Fori(1, ITERS - 1) as i:
                    for k in range(4):
                        gather(i, 1, k, True)
                        scatter(i - 1, 1, k)
                    for k in range(4):
                        gather(i + 1, 0, k, True)
                        scatter(i, 0, k)
                for k in range(4):
                    gather(ITERS - 1, 1, k, True)
                    scatter(ITERS - 2, 1, k)
                for half in range(2):
                    for k in range(4):
                        scatter(ITERS - 1, half, k)
                for half in range(2):
                    pool.wait_ge(stored[half], 64 * ITERS)
                pool.wait_ge(q.rev_stored, 16 * T)

            @block.tensor
            def _(pe):
                def add_up(n, b, early):
                    pe.wait_ge(q.relu_ready, n + 1)
                    if not early:
                        pe.wait_ge(q.rev_ready, n - 1)
                    nc.tensor.matmul(dedup[b][:, 0:W], equal[:, b, :], relus[:, b, 1, :], start=True, stop=True
                                     ).then_inc(q.rev_summed, 1)

                def tile(i, half, k, first):
                    n = 8 * i + 4 * half + k
                    b = k % 2
                    if k % 2 == 0:
                        pe.wait_ge(gathered[2 * half + k // 2], 64 * (i + 1))
                    if k == 0:
                        pe.wait_ge(q.src4_ready, 2 * i + half + 1)
                    if not (first and half == 0 and k < 2):
                        pe.wait_ge(q.x_t_ready, n - 1)
                    nc.tensor.transpose(turned[b][:, 0, 0:P], x_src[:, half, k, :], s.ident[:, :])
                    nc.tensor.transpose(turned[b][:, 1, 0:P], x_dst[:, half, k, :], s.ident[:, :]
                                        ).then_inc(q.x_turned, 1)
                    if not (first and half == 0 and k < 2):
                        pe.wait_ge(q.equal_ready, n - 1)
                    mm = nc.tensor.transpose(srcs_t[b][:, 0:P], src4[:, half, k:k + 1].to_broadcast([P, P]),
                                             s.ident[:, :])
                    mm.then_inc(q.srcs_turned, 1)
                    if not (first and half == 0 and k == 0):
                        add_up(n - 1, 1 - b, first and half == 0 and k < 3)
                    pe.wait_ge(q.x_t_ready, n + 1)
                    if not (first and half == 0 and k < 2):
                        pe.wait_ge(q.hidden_ready, n - 1)
                    for j in range(2):
                        mm = nc.tensor.matmul(hid[b][:, 0, 0:2 * D], x_t[:, b, j, :], s.w_edge[:, j, :],
                                              start=j == 0, stop=j == 1)
                    mm.then_inc(q.hid_ready, 1)

                def block_of(i, first=False):
                    for half in range(2):
                        for k in range(4):
                            tile(i, half, k, first)

                block_of(0, first=True)
                with pe.Fori(1, ITERS) as i:
                    block_of(i)
                add_up(T - 1, 1, False)

            @block.scalar
            def _(act):
                def copy_sums(n, place, early):
                    act.wait_ge(q.rev_summed, n + 1)
                    if not early:
                        act.wait_ge(q.rev_stored, 16 * (n - 7))
                    nc.scalar.copy(rev_rows[:, place // 4, place % 4, :], dedup[place % 2][:, 0:W]
                                   ).then_inc(q.rev_ready, 1)

                def tile(i, half, k, first):
                    n = 8 * i + 4 * half + k
                    b = k % 2
                    early = first and half == 0 and k < 2
                    act.wait_ge(q.x_turned, n + 1)
                    if not early:
                        act.wait_ge(q.hid_ready, n - 1)
                    nc.scalar.copy(x_t[:, b, :, :], turned[b][:, :, 0:P]).then_inc(q.x_t_ready, 1)
                    if not (first and half == 0 and k == 0):
                        before = 4 * half + k - 1 if 4 * half + k else 7
                        copy_sums(n - 1, before, first or (is_block(i, 1) and before == 7))
                    act.wait_ge(q.hidden_ready, n + 1)
                    if not early:
                        act.wait_ge(q.rev_summed, n - 1)
                        act.wait_ge(q.row_ready, n - 1)
                    nc.scalar.activation(relus[:, b, :, 0:D], hidden[:, b, :, :], ACT.Relu).then_inc(q.relu_ready, 1)

                def block_of(i, first=False):
                    for half in range(2):
                        for k in range(4):
                            tile(i, half, k, first)

                block_of(0, first=True)
                block_of(1)
                with act.Fori(2, ITERS) as i:
                    block_of(i)
                copy_sums(T - 1, 7, False)

            @block.vector
            def _(dve):
                v = nc.vector

                def feed(i, half):
                    v.tensor_copy(gidx[:, half, :, :], s.gather_rows[:, bass.ds(8 * i + 4 * half, 4), :]
                                  ).then_inc(q.gidx_ready, 1)

                def half_block(i, half, first, last):
                    t0 = 8 * i + 4 * half
                    if not last:
                        for pair in range(2):
                            dve.wait_ge(gathered[2 * half + pair], 64 * (i + 1))
                        feed(i + 1, half)
                    if not first:
                        dve.wait_ge(q.srcs_turned, 4 * (2 * i + half - 1))
                        dve.wait_ge(q.ridx_step, 6 * i + 3 * half)
                    v.tensor_copy(src4[:, half, :], s.source[:, bass.ds(t0, 4)]).then_inc(q.src4_ready, 1)
                    dve.wait_ge(q.src4_ready, 2 * i + half + 1)
                    for k in range(4):
                        n = t0 + k
                        b = k % 2
                        early = first and half == 0 and k < 2
                        dve.wait_ge(q.srcs_turned, n + 1)
                        if not early:
                            dve.wait_ge(q.rev_summed, n - 1)
                        v.tensor_scalar(equal[:, b, :], srcs_t[b][:, 0:P], src4[:, half, k:k + 1], None,
                                        ALU.is_equal).then_inc(q.equal_ready, 1)
                        dve.wait_ge(q.hid_ready, n + 1)
                        if not early:
                            dve.wait_ge(q.relu_ready, n - 1)
                        v.tensor_tensor(hidden[:, b, :, :].rearrange("p a d -> p (a d)"), hid[b][:, 0, 0:2 * D],
                                        s.b_edge[:, :], ALU.add).then_inc(q.hidden_ready, 1)
                        dve.wait_ge(q.equal_ready, n + 1)
                        if not (first and half == 0 and k == 0):
                            dve.wait_ge(q.counted, n)
                        if k == 0 and not (first and half == 0):
                            dve.wait_ge(q.ridx_step, 6 * i + 3 * half)
                        v.tensor_tensor_reduce(pairs_scratch[:, :], equal[:, b, :], s.lower[:, :], 1.0, 0.0,
                                               ALU.mult, ALU.add, repeats[:, k:k + 1]).then_inc(q.counted, 1)
                        if k == 0:
                            if not first:
                                dve.wait_ge(stored[half], 64 * i)
                            v.tensor_copy(sidx[:, half, :], s.scatter_rows[:, bass.ds(t0, 4)]
                                          ).then_inc(q.sidx_ready, 1)
                            v.tensor_copy(rows[:, half, :, D + 1], s.position[:, bass.ds(t0, 4)]
                                          ).then_inc(q.sidx_ready, 1)
                        dve.wait_ge(q.relu_ready, n + 1)
                        if not (first and half == 0 and k == 0):
                            dve.wait_ge(q.row_ready, n)
                        before = rows[:, half, k - 1, 0:D + 1] if k else rows[:, 1 - half, 3, 0:D + 1]
                        v.scalar_tensor_tensor(rows[:, half, k, 0:D + 1], before, s.same_in[:, bass.ds(n, 1)],
                                               relus[:, b, 0, 0:D + 1], ALU.mult, ALU.add).then_inc(q.row_ready, 1)
                    dve.wait_ge(q.counted, t0 + 4)
                    v.tensor_scalar(ridx_f[:, :], repeats[:, :], 0.0, s.dummy[:, 0:1], ALU.is_gt, ALU.mult
                                    ).then_inc(q.ridx_step, 1)
                    dve.wait_ge(q.ridx_step, 6 * i + 3 * half + 1)
                    v.tensor_tensor(ridx_f[:, :], ridx_f[:, :], src4[:, half, :], ALU.max).then_inc(q.ridx_step, 1)
                    dve.wait_ge(q.ridx_step, 6 * i + 3 * half + 2)
                    if not first:
                        dve.wait_ge(q.rev_stored, 16 * (t0 - 4))
                    v.tensor_copy(ridx[:, half, :], ridx_f[:, :]).then_inc(q.ridx_step, 1)

                feed(0, 0)
                feed(0, 1)
                half_block(0, 0, True, False)
                half_block(0, 1, True, False)
                with dve.Fori(1, ITERS - 1) as i:
                    half_block(i, 0, False, False)
                    half_block(i, 1, False, False)
                half_block(ITERS - 1, 0, False, True)
                half_block(ITERS - 1, 1, False, True)

        fixup(nc, s, "msg_fix", sums_in, rows[:, 1, 3, :], D + 1, dedup)


def fixup(nc, s, name, table, last, cols, sums):
    with nc.sbuf_tensor(f"{name}_first", [P, W], F32) as first, \
            nc.sbuf_tensor(f"{name}_last", [P, W], F32) as total:
        with phase(nc, name, "loaded", "summed", "added", "stored") as (block, q):
            @block.sync
            def _(sp):
                sp.dma_start(first[:, :], table[SIDE:SIDE + P, :]).then_inc(q.loaded, 16)

            @block.tensor
            def _(pe):
                nc.tensor.matmul(sums[0][:, 0:cols], s.mask_first[:, :], last[:, 0:cols], start=True, stop=True
                                 ).then_inc(q.summed, 1)
                nc.tensor.matmul(sums[1][:, 0:cols], s.mask_last[:, :], last[:, 0:cols], start=True, stop=True
                                 ).then_inc(q.summed, 1)

            @block.vector
            def _(dve):
                dve.wait_ge(q.summed, 2)
                dve.wait_ge(q.loaded, 16)
                nc.vector.tensor_tensor(first[:, 0:cols], first[:, 0:cols], sums[0][:, 0:cols], ALU.add
                                        ).then_inc(q.added, 1)
                nc.vector.tensor_copy(total[:, 0:cols], sums[1][:, 0:cols]).then_inc(q.added, 1)
                if cols < W:
                    nc.vector.tensor_copy(total[:, cols:W], last[:, cols:W]).then_inc(q.added, 1)

            @block.gpsimd
            def _(pool):
                pool.wait_ge(q.added, 2 + (cols < W))
                for j, rows in enumerate((first, total)):
                    pool.indirect_dma_start(table[:, :], bass.IndirectOffsetOnAxis(ap=s.fix_rows[:, j:j + 1], axis=0),
                                            rows[:, :], None, bounds_check=ROWS - 1, oob_is_err=False
                                            ).then_inc(q.stored, 16)
                pool.wait_ge(q.stored, 32)


def nodes_of(dram, start):
    return dram[bass.ds(start, BLOCK), :].rearrange("(p c) w -> p c w", c=4)


def over_blocks(eng, step):
    step(0, 0, True)
    step(1, 1, True)
    with eng.Fori(1, NBLOCKS // 2 - 1) as i:
        step(2 * i, 0, False)
        step(2 * i + 1, 1, False)
    step(NBLOCKS - 2, 0, False)
    step(NBLOCKS - 1, 1, False)


def is_block(j, n):
    return isinstance(j, int) and j == n


def start_of(j):
    return N - BLOCK if is_block(j, NBLOCKS - 1) else j * BLOCK


def loads_done(eng, sem, j, slot, n):
    eng.wait_ge(sem, 8 * n * (j - slot) + 16 * n)


def over_features(bias):
    return bias.rearrange("p (o d) -> p o d", o=1).to_broadcast([P, 4, D])


def head_rows(nc, s, steps, scores, rows, node_att, slot):
    v = nc.vector
    a = node_att[:, slot, :, :]
    r = rows[:, slot, :, :]
    steps.then(v.tensor_copy(r[:, :, D:D + HEADS], scores[:, :, 0:HEADS]))
    steps.then(v.tensor_copy(a[:, :, HEADS:2 * HEADS], scores[:, :, HEADS:2 * HEADS]))
    steps.wait()
    steps.then(v.tensor_tensor(a[:, :, 0:HEADS], r[:, :, D:D + HEADS], a[:, :, HEADS:2 * HEADS], ALU.add))
    steps.wait()
    steps.then(v.scalar_tensor_tensor(a[:, :, 0:HEADS], a[:, :, 0:HEADS], SLOPE, a[:, :, 0:HEADS], ALU.mult, ALU.max))


def deviation(nc, s, q, act, moments, rstd, j, slot, moment_steps):
    act.wait_ge(q.step, moment_steps * (j + 1))
    nc.scalar.activation(rstd[:, slot, :], moments[:, slot, :, 1], ACT.Sqrt, bias=s.eps[:, 0:1]
                         ).then_inc(q.rstd_ready, 1)


def row_moments(nc, steps, rows, stats, moments):
    for c in range(4):
        steps.then(nc.vector.bn_stats(stats[:, c, :], rows[:, c, :]))
    steps.wait()
    hold(steps.eng, steps.passed)
    for c in range(4):
        steps.then(nc.vector.bn_aggr(moments[:, c, :], stats[:, c, :]))


def normalise(nc, q, dve, rows, dst, moments, rstd, j, slot):
    v = nc.vector
    dve.wait_ge(q.rstd_ready, j + 1)
    v.reciprocal(rstd[:, slot, :], rstd[:, slot, :]).then_inc(q.inverted, 1)
    dve.wait_ge(q.inverted, j + 1)
    for c in range(4):
        v.tensor_scalar(dst[:, c, 0:D], rows[:, c, :], moments[:, slot, c, 0:1], rstd[:, slot, c:c + 1],
                        ALU.subtract, ALU.mult).then_inc(q.normed, 1)


MOMENT_STEPS = 4 + 4
HEAD_STEPS = 4


STORES = 1 + 4


def feed_places(nc, s, q, dve, places, j, slot):
    nc.vector.tensor_copy(places[:, slot, :], s.end_places[:, bass.ds(4 * j, 4)]).then_inc(q.placed, 1)


def store_rows(pool, q, stored, new, node_att, places, x_next, att_ends, j, slot):
    pool.wait_ge(q.tail_step, HEAD_STEPS * (j + 1))
    pool.wait_ge(q.placed, j + 1)
    if is_block(j, NBLOCKS - 1):
        pool.wait_ge(stored[0], 8 * STORES * NBLOCKS)
        pool.wait_ge(stored[1], 8 * STORES * (NBLOCKS - 2))
    pool.dma_start(nodes_of(x_next, start_of(j)), new[:, slot, :, :]).then_inc(stored[slot], 16)
    for c in range(4):
        pool.indirect_dma_start(att_ends[:, :], bass.IndirectOffsetOnAxis(ap=places[:, slot, c:c + 1], axis=0),
                                node_att[:, slot, c, :], None, bounds_check=SLOTS - 1, oob_is_err=False
                                ).then_inc(stored[slot], 16)


def turn_rows(nc, s, q, pe, bank, new, j, slot):
    pe.wait_ge(q.normed, 4 * (j + 1))
    if not is_block(j, 0):
        pe.wait_ge(q.tail_step, HEAD_STEPS * j)
    for c in range(4):
        mm = nc.tensor.transpose(bank[:, c * P:(c + 1) * P], new[:, slot, c, 0:D], s.ident[:, :])
    mm.then_inc(q.rows_turned, 1)


def score_rows(nc, s, q, pe, bank, new_t, layer, j):
    pe.wait_ge(q.rows_copied, j + 1)
    for c in range(4):
        mm = nc.tensor.matmul(bank[:, c * 8:c * 8 + 8], new_t[:, c * P:(c + 1) * P], s.w_att[:, layer, :],
                              start=True, stop=True)
    mm.then_inc(q.scored, 1)


def copy_rows(nc, q, act, bank, new_t, j):
    act.wait_ge(q.rows_turned, j + 1)
    if not is_block(j, 0):
        act.wait_ge(q.scored, j)
    nc.scalar.copy(new_t[:, :], bank[:, :]).then_inc(q.rows_copied, 1)


def update_nodes(nc, s, x, sums_in, sums_out, x_next, att_ends):
    with ExitStack() as ctx:
        def sb(name, shape, dt=F32):
            return ctx.enter_context(nc.sbuf_tensor(name, shape, dt))

        def pb(name, shape):
            return ctx.enter_context(nc.psum_tensor(name, shape, F32))

        xs = sb("xs", [P, 2, 4, D])
        ins = sb("ins", [P, 2, 4, W])
        outs = sb("outs", [P, 2, 4, W])
        degrees = sb("degrees", [P, 2, 4, 2])
        x_t = sb("xs_t", [P, 2, BLOCK])
        in_t = sb("ins_t", [P, BLOCK])
        out_t = sb("outs_t", [P, BLOCK])
        deg_t = sb("deg_t", [2, BLOCK])
        agg_t = sb("agg_t", [P, BLOCK])
        hid_t = sb("hid_t", [P, 2, BLOCK])
        base = sb("base_rows", [P, 2, 4, D])
        total = sb("total_rows", [P, 2, 4, D])
        new = sb("new_rows", [P, 2, 4, D + HEADS])
        new_t = sb("new_t", [P, BLOCK])
        node_att = sb("node_att", [P, 2, 4, 2 * HEADS])
        places = sb("places", [P, 2, 4], I32)
        stats = sb("stats", [P, 4, 6])
        moments = sb("moments", [P, 2, 4, 2])
        rstd = sb("rstd", [P, 2, 4])
        p_x = pb("p_x", [P, BLOCK])
        p_in = pb("p_in", [P, BLOCK])
        p_out = pb("p_out", [P, BLOCK])
        p_agg = pb("p_agg", [P, BLOCK])
        p_hid = [pb(f"p_hid{m}", [P, BLOCK]) for m in range(2)]
        p_new = pb("p_new", [P, 4, D])
        p_tail = pb("p_tail", [P, BLOCK])

        with phase(nc, "upd", "loaded_a", "loaded_b", "degrees_ready", "turned", "deg_turned", "copied",
                   "deg_copied", "doubled", "base_ready", "agg_ready", "agg_copied", "hid_ready", "hid_copied",
                   "new_ready", "step", "rstd_ready", "inverted", "normed", "rows_turned", "rows_copied", "scored",
                   "tail_step", "placed", "stored_a", "stored_b", "passed") as (block, q):
            loaded = [q.loaded_a, q.loaded_b]
            stored = [q.stored_a, q.stored_b]
            moment_steps = 1 + MOMENT_STEPS

            @block.sync
            def _(sp):
                def step(j, slot, first):
                    if not first:
                        sp.wait_ge(q.turned, 3 * (j - 1))
                        sp.wait_ge(q.base_ready, j - 1)
                        hold(sp, q.passed)
                        sp.wait_ge(q.degrees_ready, 3 * (j - 1))
                        hold(sp, q.passed)
                    for rows, table in ((xs, x), (ins, sums_in), (outs, sums_out)):
                        sp.dma_start(rows[:, slot, :, :], nodes_of(table, start_of(j))).then_inc(loaded[slot], 16)

                over_blocks(sp, step)

            @block.gpsimd
            def _(pool):
                def step(j, slot, first):
                    loads_done(pool, loaded[slot], j, slot, 3)
                    if not first:
                        pool.wait_ge(q.step, moment_steps * (j - 2) + 1)
                    nc.gpsimd.tensor_tensor(base[:, slot], xs[:, slot], xs[:, slot], ALU.add).then_inc(q.doubled, 1)
                    pool.wait_ge(q.doubled, j + 1)
                    nc.gpsimd.tensor_tensor(base[:, slot], base[:, slot], over_features(s.upd_b2[:, :]), ALU.add
                                            ).then_inc(q.base_ready, 1)
                    if not first:
                        store_rows(pool, q, stored, new, node_att, places, x_next, att_ends, j - 2, slot)

                over_blocks(pool, step)
                for j in (NBLOCKS - 2, NBLOCKS - 1):
                    store_rows(pool, q, stored, new, node_att, places, x_next, att_ends, j, j % 2)
                for slot in range(2):
                    pool.wait_ge(stored[slot], 8 * STORES * NBLOCKS)

            @block.tensor
            def _(pe):
                def messages(j, slot, very_first):
                    pe.wait_ge(q.degrees_ready, 3 * (j + 1))
                    pe.wait_ge(q.copied, 3 * j + 1)
                    for c in range(4):
                        mm = nc.tensor.transpose(p_x[0:2, c * P:(c + 1) * P], degrees[:, slot, c, :], s.ident[:, :])
                    mm.then_inc(q.deg_turned, 1)
                    pe.wait_ge(q.copied, 3 * j + 3)
                    if not very_first:
                        pe.wait_ge(q.agg_copied, j)
                    nc.tensor.matmul(p_agg[:, :], s.w_msg2[:, 0, :], in_t[:, :], start=True, stop=False)
                    nc.tensor.matmul(p_agg[:, :], s.w_msg2[:, 1, :], out_t[:, :], start=False, stop=False)
                    pe.wait_ge(q.deg_copied, j + 1)
                    nc.tensor.matmul(p_agg[:, :], s.b_msg2[:, :], deg_t[:, :], start=False, stop=True
                                     ).then_inc(q.agg_ready, 1)

                def hidden(j, slot, very_first):
                    pe.wait_ge(q.agg_copied, j + 1)
                    for m in range(2):
                        if not very_first:
                            pe.wait_ge(q.hid_copied, 2 * j + m - 1)
                        nc.tensor.matmul(p_hid[m][:, :], s.upd1[:, 0, m * P:(m + 1) * P], agg_t[:, :], start=True,
                                         stop=False)
                        nc.tensor.matmul(p_hid[m][:, :], s.upd1[:, 1, m * P:(m + 1) * P], x_t[:, slot, :],
                                         start=False, stop=True).then_inc(q.hid_ready, 1)

                def output(j, very_first):
                    pe.wait_ge(q.hid_copied, 2 * j + 2)
                    if not very_first:
                        pe.wait_ge(q.step, moment_steps * (j - 1) + 1)
                    for c in range(4):
                        for m in range(2):
                            mm = nc.tensor.matmul(p_new[:, c, :], hid_t[:, m, c * P:(c + 1) * P], s.upd2[:, m, :],
                                                  start=m == 0, stop=m == 1)
                    mm.then_inc(q.new_ready, 1)

                def turn_tail(j, slot):
                    turn_rows(nc, s, q, pe, p_tail, new, j, slot)

                def tail(j):
                    score_rows(nc, s, q, pe, p_tail, new_t, 0, j)

                def step(j, slot, first):
                    very_first = first and slot == 0
                    loads_done(pe, loaded[slot], j, slot, 3)
                    for m, (dst, src) in enumerate(((p_x, xs), (p_in, ins), (p_out, outs))):
                        if m == 0 and not very_first:
                            pe.wait_ge(q.deg_copied, j)
                        elif not very_first:
                            pe.wait_ge(q.copied, 3 * j)
                        for c in range(4):
                            mm = nc.tensor.transpose(dst[:, c * P:(c + 1) * P], src[:, slot, c, 0:D], s.ident[:, :])
                        mm.then_inc(q.turned, 1)
                    if not very_first:
                        hidden(j - 1, 1 - slot, is_block(j, 1))
                    if not first:
                        turn_tail(j - 2, slot)
                    messages(j, slot, very_first)
                    if not very_first:
                        output(j - 1, is_block(j, 1))
                    if not first:
                        tail(j - 2)

                over_blocks(pe, step)
                hidden(NBLOCKS - 1, 1, False)
                turn_tail(NBLOCKS - 2, 0)
                output(NBLOCKS - 1, False)
                tail(NBLOCKS - 2)
                turn_tail(NBLOCKS - 1, 1)
                tail(NBLOCKS - 1)

            @block.scalar
            def _(act):
                def hidden(j, very_first):
                    for m in range(2):
                        act.wait_ge(q.hid_ready, 2 * j + m + 1)
                        if m == 0 and not very_first:
                            act.wait_ge(q.new_ready, j)
                        nc.scalar.activation(hid_t[:, m, :], p_hid[m][:, :], ACT.Relu, bias=s.upd_b1[:, m:m + 1]
                                             ).then_inc(q.hid_copied, 1)

                def step(j, slot, first):
                    very_first = first and slot == 0
                    for m, (dst, src) in enumerate(((x_t[:, slot, :], p_x), (in_t[:, :], p_in),
                                                    (out_t[:, :], p_out))):
                        act.wait_ge(q.turned, 3 * j + m + 1)
                        if m == 0 and not first:
                            act.wait_ge(q.hid_ready, 2 * (j - 1))
                        if m == 1 and not very_first:
                            act.wait_ge(q.agg_ready, j)
                        nc.scalar.copy(dst, src[:, :]).then_inc(q.copied, 1)
                    if not first:
                        deviation(nc, s, q, act, moments, rstd, j - 2, slot, moment_steps)
                    if not very_first:
                        hidden(j - 1, is_block(j, 1))
                    if not first:
                        copy_rows(nc, q, act, p_tail, new_t, j - 2)
                    act.wait_ge(q.deg_turned, j + 1)
                    nc.scalar.copy(deg_t[:, :], p_x[0:2, :]).then_inc(q.deg_copied, 1)
                    act.wait_ge(q.agg_ready, j + 1)
                    if not very_first:
                        act.wait_ge(q.hid_ready, 2 * j)
                    nc.scalar.copy(agg_t[:, :], p_agg[:, :]).then_inc(q.agg_copied, 1)

                over_blocks(act, step)
                deviation(nc, s, q, act, moments, rstd, NBLOCKS - 2, 0, moment_steps)
                hidden(NBLOCKS - 1, False)
                copy_rows(nc, q, act, p_tail, new_t, NBLOCKS - 2)
                deviation(nc, s, q, act, moments, rstd, NBLOCKS - 1, 1, moment_steps)
                copy_rows(nc, q, act, p_tail, new_t, NBLOCKS - 1)

            @block.vector
            def _(dve):
                v = nc.vector

                def total_and_moments(j, slot, first):
                    dve.wait_ge(q.new_ready, j + 1)
                    dve.wait_ge(q.base_ready, j + 1)
                    if not first:
                        dve.wait_ge(q.normed, 4 * (j - 1))
                    steps = Steps(dve, q.step, moment_steps * j, q.passed)
                    steps.then(v.tensor_tensor(total[:, slot], base[:, slot], p_new[:, :, :], ALU.add))
                    steps.wait()
                    row_moments(nc, steps, total[:, slot], stats, moments[:, slot])

                def finish(j, slot, first):
                    if not first:
                        dve.wait_ge(stored[slot], 8 * STORES * (j - slot))
                    dve.wait_ge(q.degrees_ready, 3 * (j + 1))
                    feed_places(nc, s, q, dve, places, j, slot)
                    normalise(nc, q, dve, total[:, slot], new[:, slot], moments, rstd, j, slot)

                def tail(j, slot):
                    dve.wait_ge(q.scored, j + 1)
                    steps = Steps(dve, q.tail_step, HEAD_STEPS * j)
                    head_rows(nc, s, steps, p_tail[:, 0:32].rearrange("p (c k) -> p c k", c=4), new, node_att, slot)

                def step(j, slot, first):
                    very_first = first and slot == 0
                    loads_done(dve, loaded[slot], j, slot, 3)
                    if not first:
                        dve.wait_ge(q.deg_turned, j - 1)
                    v.tensor_copy(degrees[:, slot, :, 0:1], ins[:, slot, :, D:D + 1]).then_inc(q.degrees_ready, 1)
                    v.tensor_copy(degrees[:, slot, :, 1:2], outs[:, slot, :, D:D + 1]).then_inc(q.degrees_ready, 1)
                    v.tensor_scalar(s.end_places[:, bass.ds(4 * j, 4)], ins[:, slot, :, D + 1], SKIP, None, ALU.add
                                    ).then_inc(q.degrees_ready, 1)
                    if not first:
                        finish(j - 2, slot, is_block(j, 2) or is_block(j, 3))
                    if not very_first:
                        total_and_moments(j - 1, 1 - slot, is_block(j, 1))
                    if not first:
                        tail(j - 2, slot)

                over_blocks(dve, step)
                finish(NBLOCKS - 2, 0, False)
                tail(NBLOCKS - 2, 0)
                total_and_moments(NBLOCKS - 1, 1, False)
                finish(NBLOCKS - 1, 1, False)
                tail(NBLOCKS - 1, 1)


def score_edges(nc, s, layer, x_rows, turned_x):
    with ExitStack() as ctx:
        def sb(name, shape, dt=F32):
            return ctx.enter_context(nc.sbuf_tensor(f"{name}_{layer}", shape, dt))

        gidx = sb("gidx2", [P, 2, 4], I32)
        rows = sb("src_rows", [P, 2, 4, D + HEADS])
        x_t = sb("src_t", [P, 2, BLOCK])
        banks = [ctx.enter_context(nc.psum_tensor(f"src_bank{h}_{layer}", [P, BLOCK], F32)) for h in range(2)]
        with phase(nc, f"score{layer}", "gidx_ready", "gathered_a", "gathered_b", "turned", "copied", "stored_a", "stored_b", "passed",
                   "scored") as (block, q):
            gathered = [q.gathered_a, q.gathered_b]
            stored = [q.stored_a, q.stored_b]

            def over_halves(eng, step):
                step(0, 0, True)
                step(0, 1, True)
                with eng.Fori(1, ITERS) as i:
                    step(i, 0, False)
                    step(i, 1, False)

            @block.gpsimd
            def _(pool):
                def step(i, half, first):
                    pool.wait_ge(q.gidx_ready, 2 * i + half + 1)
                    if not first:
                        pool.wait_ge(q.turned, 2 * i + half - 1)
                        pool.wait_ge(q.scored, 2 * i + half - 1)
                    hold(pool, q.passed)
                    for k in range(4):
                        pool.indirect_dma_start(rows[:, half, k, :], None, x_rows[:, :], bass.IndirectOffsetOnAxis(
                            ap=gidx[:, half, k:k + 1], axis=0)).then_inc(gathered[half], 16)

                over_halves(pool, step)

            @block.tensor
            def _(pe):
                def step(i, half, first):
                    pe.wait_ge(gathered[half], 64 * i + 64)
                    if not first:
                        pe.wait_ge(q.copied, 2 * i + half - 1)
                    for k in range(4):
                        mm = nc.tensor.transpose(banks[half][:, k * P:(k + 1) * P], rows[:, half, k, 0:D],
                                                 s.ident[:, :])
                    mm.then_inc(q.turned, 1)

                over_halves(pe, step)

            @block.scalar
            def _(act):
                def step(i, half, first):
                    act.wait_ge(q.turned, 2 * i + half + 1)
                    if not first:
                        act.wait_ge(stored[half], 16 * i)
                    nc.scalar.copy(x_t[:, half, :], banks[half][:, :]).then_inc(q.copied, 1)

                over_halves(act, step)

            @block.sync
            def _(sp):
                def step(i, half, first):
                    sp.wait_ge(q.copied, 2 * i + half + 1)
                    hold(sp, q.passed)
                    sp.dma_start(turned_x[bass.ds((2 * i + half) * P, P), :], x_t[:, half, :]
                                 ).then_inc(stored[half], 16)

                over_halves(sp, step)
                for half in range(2):
                    sp.wait_ge(stored[half], 16 * ITERS)

            @block.vector
            def _(dve):
                v = nc.vector

                def feed(i, half, first):
                    v.tensor_copy(gidx[:, half, :], s.gather_rows[:, bass.ds(8 * i + 4 * half, 4), 0]
                                  ).then_inc(q.gidx_ready, 1)

                def step(i, half, last):
                    dve.wait_ge(gathered[half], 64 * i + 64)
                    if not last:
                        feed(i + 1, half, False)
                    t = bass.ds(8 * i + 4 * half, 4)
                    v.tensor_copy(s.edge_score[:, :, t].rearrange("p h k -> p k h"), rows[:, half, :, D:D + HEADS]
                                  ).then_inc(q.scored, 1)

                feed(0, 0, True)
                feed(0, 1, True)
                with dve.Fori(0, ITERS - 1) as i:
                    step(i, 0, False)
                    step(i, 1, False)
                step(ITERS - 1, 0, True)
                step(ITERS - 1, 1, True)


def add_destinations(nc, s, layer, att_ends):
    with ExitStack() as ctx:
        def sb(name, shape, dt=F32):
            return ctx.enter_context(nc.sbuf_tensor(f"{name}_{layer}", shape, dt))

        ends = sb("att_at_ends", [P, T, 2 * HEADS])
        spread = sb("att_spread", [P, 2 * HEADS, T])
        edge = sb("att_edge", [P, 2 * HEADS])
        incoming = sb("att_incoming", [P, 2 * HEADS])
        chunk_rows = sb("att_chunk_rows", [2 * HEADS, 2, P])
        shifted = sb("att_shifted", [2 * HEADS, P])
        row_bank = ctx.enter_context(nc.psum_tensor(f"att_row_bank_{layer}", [P, BLOCK], F32))
        col_bank = ctx.enter_context(nc.psum_tensor(f"att_col_bank_{layer}", [P, BLOCK], F32))
        with phase(nc, f"dest{layer}", "loaded", "step", "edge_ready", "shifted_ready", "turned") as (block, q):
            @block.sync
            def _(sp):
                sp.dma_start(ends[:, :, :], att_ends.rearrange("(p t) w -> p t w", t=T)).then_inc(q.loaded, 16)

            @block.tensor
            def _(pe):
                pe.wait_ge(q.edge_ready, 1)
                nc.tensor.transpose(row_bank[0:2 * HEADS, 0:P], edge[:, :], s.ident[:, :]).then_inc(q.turned, 1)
                pe.wait_ge(q.shifted_ready, 1)
                nc.tensor.transpose(col_bank[:, 0:2 * HEADS], shifted[:, :], s.ident[0:2 * HEADS, 0:2 * HEADS]
                                    ).then_inc(q.turned, 1)

            @block.vector
            def _(dve):
                v = nc.vector
                steps = Steps(dve, q.step)
                dve.wait_ge(q.loaded, 16)
                for h in range(2 * HEADS):
                    steps.then(v.tensor_tensor_scan(spread[:, h, ::-1], s.goes_on[:, ::-1], ends[:, ::-1, h], 0.0,
                                                    ALU.mult, ALU.add))
                steps.wait()
                v.tensor_copy(edge[:, :], spread[:, :, 0]).then_inc(q.edge_ready, 1)
                dve.wait_ge(q.turned, 1)
                steps.then(v.tensor_copy(chunk_rows[:, 0, :], row_bank[0:2 * HEADS, 0:P]))
                steps.then(v.memset(shifted[:, :], 0.0))
                steps.wait()
                steps.then(v.tensor_tensor_scan(chunk_rows[:, 1, ::-1], s.chunk_goes_on[:, ::-1],
                                                chunk_rows[:, 0, ::-1], 0.0, ALU.mult, ALU.add))
                steps.wait()
                v.tensor_copy(shifted[:, 0:P - 1], chunk_rows[:, 1, 1:P]).then_inc(q.shifted_ready, 1)
                dve.wait_ge(q.turned, 2)
                steps.then(v.tensor_copy(incoming[:, :], col_bank[:, 0:2 * HEADS]))
                steps.wait()
                for h in range(2 * HEADS):
                    steps.then(v.tensor_tensor_scan(spread[:, h, ::-1], s.goes_on[:, ::-1], ends[:, ::-1, h],
                                                    incoming[:, h:h + 1], ALU.mult, ALU.add))
                steps.wait()
                v.tensor_tensor(s.edge_score[:, :, :], s.edge_score[:, :, :], spread[:, HEADS:2 * HEADS, :], ALU.add)
                v.tensor_copy(s.self_score[:, :, :], spread[:, 0:HEADS, :])


def segment_total(nc, s, name, values, op, chunk, row_bank, col_bank):
    maximum = op == ALU.max
    join = ALU.add if maximum else ALU.mult
    inner = s.reset_in if maximum else s.same_in
    outer = s.reset if maximum else s.same
    chunk_step = s.chunk_reset if maximum else s.chunk_same
    start = -BIG if maximum else 0.0
    scan, ends, incoming, chunk_rows, shifted = chunk
    with phase(nc, name, "step", "turn", "turned") as (block, q):
        @block.vector
        def _(dve):
            v = nc.vector
            steps = Steps(dve, q.step)
            turns = [0]

            def across(edge, step_row, joined, op1, first, backwards):
                steps.then(v.tensor_copy(ends[:, :], edge))
                steps.wait()
                dve.sem_inc(q.turn, 1)
                turns[0] += 1
                dve.wait_ge(q.turned, turns[0])
                steps.then(v.tensor_copy(chunk_rows[:, 0, :], row_bank[0:HEADS, 0:P]))
                steps.then(v.memset(shifted[:, :], first))
                steps.wait()
                if backwards:
                    steps.then(v.tensor_tensor_scan(chunk_rows[:, 1, ::-1], step_row[:, ::-1],
                                                    chunk_rows[:, 0, ::-1], first, joined, op1))
                    steps.wait()
                    steps.then(v.tensor_copy(shifted[:, 0:P - 1], chunk_rows[:, 1, 1:P]))
                else:
                    steps.then(v.tensor_tensor_scan(chunk_rows[:, 1, :], step_row[:, :], chunk_rows[:, 0, :], first,
                                                    joined, op1))
                    steps.wait()
                    steps.then(v.tensor_copy(shifted[:, 1:P], chunk_rows[:, 1, 0:P - 1]))
                steps.wait()
                dve.sem_inc(q.turn, 1)
                turns[0] += 1
                dve.wait_ge(q.turned, turns[0])
                steps.then(v.tensor_copy(incoming[:, :], col_bank[:, 0:HEADS]))
                steps.wait()

            for h in range(HEADS):
                steps.then(v.tensor_tensor_scan(scan[:, h, :], inner[:, :], values[:, h, :], start, join, op))
            steps.wait()
            across(scan[:, :, T - 1], chunk_step, join, op, start, False)
            for h in range(HEADS):
                steps.then(v.tensor_tensor_scan(scan[:, h, :], outer[:, :], values[:, h, :], incoming[:, h:h + 1],
                                                join, op))
            steps.wait()
            for h in range(HEADS):
                steps.then(v.tensor_tensor(scan[:, h, :], scan[:, h, :], s.ends[:, :], ALU.mult))
            steps.wait()
            for h in range(HEADS):
                steps.then(v.tensor_tensor_scan(values[:, h, ::-1], s.goes_on[:, ::-1], scan[:, h, ::-1], 0.0,
                                                ALU.mult, ALU.add))
            steps.wait()
            across(values[:, :, 0], s.chunk_goes_on[0:HEADS, :], ALU.mult, ALU.add, 0.0, True)
            for h in range(HEADS):
                steps.then(v.tensor_tensor_scan(values[:, h, ::-1], s.goes_on[:, ::-1], scan[:, h, ::-1],
                                                incoming[:, h:h + 1], ALU.mult, ALU.add))

        @block.tensor
        def _(pe):
            for n in range(2):
                pe.wait_ge(q.turn, 2 * n + 1)
                nc.tensor.transpose(row_bank[0:HEADS, 0:P], ends[:, :], s.ident[:, :]).then_inc(q.turned, 1)
                pe.wait_ge(q.turn, 2 * n + 2)
                nc.tensor.transpose(col_bank[:, 0:HEADS], shifted[:, :], s.ident[0:HEADS, 0:HEADS]
                                    ).then_inc(q.turned, 1)


def attention_weights(nc, s, layer):
    with ExitStack() as ctx:
        def sb(name, shape, dt=F32):
            return ctx.enter_context(nc.sbuf_tensor(f"{name}_{layer}", shape, dt))

        top = sb("top", [P, HEADS, T])
        chunk = (sb("scan", [P, HEADS, T]), sb("chunk_ends", [P, HEADS]), sb("incoming", [P, HEADS]),
                 sb("chunk_rows", [HEADS, 2, P]), sb("shifted", [HEADS, P]))
        row_bank = ctx.enter_context(nc.psum_tensor(f"row_bank_{layer}", [P, BLOCK], F32))
        col_bank = ctx.enter_context(nc.psum_tensor(f"col_bank_{layer}", [P, BLOCK], F32))
        e, own = s.edge_score, s.self_score

        with phase(nc, f"leaky{layer}", "step") as (block, q):
            @block.vector
            def _(dve):
                v = nc.vector
                v.scalar_tensor_tensor(e[:, :, :], e[:, :, :], SLOPE, e[:, :, :], ALU.mult, ALU.max
                                       ).then_inc(q.step, 1)
                dve.wait_ge(q.step, 1)
                v.tensor_tensor(top[:, :, :], e[:, :, :], own[:, :, :], ALU.max)

        segment_total(nc, s, f"max{layer}", top, ALU.max, chunk, row_bank, col_bank)

        with phase(nc, f"exp{layer}", "shifted", "exped") as (block, q):
            @block.vector
            def _(dve):
                v = nc.vector
                v.tensor_tensor(e[:, :, :], e[:, :, :], top[:, :, :], ALU.subtract).then_inc(q.shifted, 1)
                v.tensor_tensor(own[:, :, :], own[:, :, :], top[:, :, :], ALU.subtract).then_inc(q.shifted, 1)
                dve.wait_ge(q.shifted, 2)
                dve.wait_ge(q.exped, 2)
                v.tensor_copy(top[:, :, :], e[:, :, :])

            @block.scalar
            def _(act):
                act.wait_ge(q.shifted, 2)
                nc.scalar.activation(e[:, :, :], e[:, :, :], ACT.Exp).then_inc(q.exped, 1)
                nc.scalar.activation(own[:, :, :], own[:, :, :], ACT.Exp).then_inc(q.exped, 1)

        segment_total(nc, s, f"sum{layer}", top, ALU.add, chunk, row_bank, col_bank)

        with phase(nc, f"norm{layer}", "step") as (block, q):
            @block.vector
            def _(dve):
                v = nc.vector
                steps = Steps(dve, q.step)
                steps.then(v.tensor_tensor(top[:, :, :], top[:, :, :], own[:, :, :], ALU.add))
                steps.wait()
                steps.then(v.reciprocal(top[:, :, :], top[:, :, :]))
                steps.wait()
                steps.then(v.scalar_tensor_tensor(s.weights[:, 0:HEADS, :], e[:, :, :], 1.0 / HEADS, top[:, :, :],
                                                  ALU.mult, ALU.mult))
                steps.then(v.scalar_tensor_tensor(s.self_weights[:, :, :].rearrange("p t h -> p h t"), own[:, :, :],
                                                  1.0 / HEADS, top[:, :, :], ALU.mult, ALU.mult))
                steps.then(v.tensor_copy(s.weights[:, HEADS, :], s.same_in[:, :]))


def weigh_edges(nc, s, layer, turned_x, sums):
    with ExitStack() as ctx:
        def sb(name, shape, dt=F32):
            return ctx.enter_context(nc.sbuf_tensor(f"{name}_{layer}", shape, dt))

        x_t = sb("edge_t", [P, 2, BLOCK])
        sidx = sb("sidx2", [P, 2, 4], I32)
        weights = sb("weights4", [P, 2, HEADS + 1, 4])
        part = sb("part", [P, 2, 4, 2, D])
        rows = sb("sum_rows", [P, 2, 4, W])
        banks = [ctx.enter_context(nc.psum_tensor(f"heads{b}_{layer}", [P, BLOCK], F32)) for b in range(8)]

        with phase(nc, f"weigh_init{layer}", "x") as (block, q):
            @block.vector
            def _(dve):
                nc.vector.memset(rows[:, :, :, :], 0.0).then_inc(q.x, 1)
                dve.wait_ge(q.x, 1)
                nc.vector.memset(rows[:, :, :, D + HEADS:D + HEADS + 1], 1.0)

        with phase(nc, f"weigh{layer}", "loaded_a", "loaded_b", "weights_fed", "sidx_fed", "headed", "first_head", "step",
                   "row_ready", "extras_ready", "stored_a", "stored_b", "stored_c", "stored_d", "passed") as (block, q):
            loaded = [q.loaded_a, q.loaded_b]
            stored = [q.stored_a, q.stored_b, q.stored_c, q.stored_d]

            def over_halves(eng, step):
                step(0, 0, True)
                step(0, 1, True)
                with eng.Fori(1, ITERS) as i:
                    step(i, 0, False)
                    step(i, 1, False)

            @block.sync
            def _(sp):
                def step(i, half, first):
                    if not first:
                        sp.wait_ge(q.headed, 4 * (2 * i + half - 1))
                        hold(sp, q.passed)
                    sp.dma_start(x_t[:, half, :], turned_x[bass.ds((2 * i + half) * P, P), :]
                                 ).then_inc(loaded[half], 16)

                over_halves(sp, step)

            @block.tensor
            def _(pe):
                def step(i, half, first):
                    pe.wait_ge(loaded[half], 16 * i + 16)
                    for k in range(4):
                        if not first:
                            pe.wait_ge(q.step, 6 * (4 * i + 2 * half + k // 2 - 4) + 5 + k % 2)
                        nc.tensor.matmul(banks[4 * half + k][:, :], x_t[:, half, k * P:(k + 1) * P], s.gat_w[:, layer, :],
                                         start=True, stop=True).then_inc(q.headed, 1)

                over_halves(pe, step)

            @block.scalar
            def _(act):
                def step(i, half, first):
                    act.wait_ge(q.weights_fed, 2 * i + half + 1)
                    t0 = 8 * i + 4 * half
                    for pair in range(2):
                        for k in (2 * pair, 2 * pair + 1):
                            act.wait_ge(q.headed, t0 + k + 1)
                            if not first:
                                act.wait_ge(q.step, 6 * (4 * i + 2 * half + pair - 4) + 1 + k % 2)
                            nc.scalar.activation(part[:, half, k, 0, :], banks[4 * half + k][:, 0:D], ACT.Copy,
                                                 scale=weights[:, half, 0, k:k + 1]).then_inc(q.first_head, 1)
                        if not first:
                            act.wait_ge(stored[2 * half + pair], 32 * i)
                        nc.scalar.copy(rows[:, half, 2 * pair:2 * pair + 2, D:D + HEADS],
                                       s.self_weights[:, bass.ds(t0 + 2 * pair, 2), :]).then_inc(q.extras_ready, 1)

                over_halves(act, step)

            @block.vector
            def _(dve):
                v = nc.vector

                def feed(i, half, first):
                    t0 = 8 * i + 4 * half
                    if not first:
                        dve.wait_ge(q.first_head, t0 - 4)
                        dve.wait_ge(q.row_ready, t0 - 4)
                    v.tensor_copy(weights[:, half, :, :], s.weights[:, :, bass.ds(t0, 4)]).then_inc(q.weights_fed, 1)

                def row(i, half, pair, k, first):
                    n = 8 * i + 4 * half + k
                    if k % 2 == 0:
                        if not first:
                            dve.wait_ge(stored[2 * half + pair], 32 * i)
                        v.tensor_copy(sidx[:, half, k:k + 2], s.scatter_rows[:, bass.ds(n, 2)]).then_inc(q.sidx_fed, 1)
                    dve.wait_ge(q.step, 6 * (4 * i + 2 * half + pair) + 5 + k % 2)
                    if not (first and half == 0 and k == 0):
                        dve.wait_ge(q.row_ready, n)
                    before = rows[:, half, k - 1, 0:D] if k else rows[:, 1 - half, 3, 0:D]
                    v.scalar_tensor_tensor(rows[:, half, k, 0:D], before, weights[:, half, HEADS, k:k + 1],
                                           part[:, half, k, 1, :], ALU.mult, ALU.add).then_inc(q.row_ready, 1)

                def step(i, half, first, last=False):
                    t0 = 8 * i + 4 * half
                    dve.wait_ge(q.weights_fed, 2 * i + half + 1)
                    for pair in range(2):
                        done = 6 * (4 * i + 2 * half + pair)
                        for h in range(1, HEADS):
                            for k in (2 * pair, 2 * pair + 1):
                                if h == 1:
                                    dve.wait_ge(q.first_head, t0 + k + 1)
                                    if not first:
                                        dve.wait_ge(q.row_ready, t0 + k - 7)
                                else:
                                    dve.wait_ge(q.step, done + 2 * (h - 2) + k % 2 + 1)
                                v.scalar_tensor_tensor(part[:, half, k, 1, :],
                                                       banks[4 * half + k][:, h * D:(h + 1) * D],
                                                       weights[:, half, h, k:k + 1],
                                                       part[:, half, k, 0 if h == 1 else 1, :], ALU.mult, ALU.add
                                                       ).then_inc(q.step, 1)
                            if h < 3 and pair == 1:
                                row(i, half, 0, h - 1, first)
                            elif h < 3 and half == 1:
                                row(i, 0, 1, h + 1, first)
                            elif h < 3 and not is_block(i, 0):
                                row(i - 1, 1, 1, h + 1, is_block(i, 1))
                        if pair == 0 and not last:
                            feed(i + half, 1 - half, first and half == 0)

                feed(0, 0, True)
                step(0, 0, True)
                step(0, 1, True)
                step(1, 0, False)
                step(1, 1, False)
                with dve.Fori(2, ITERS - 1) as i:
                    step(i, 0, False)
                    step(i, 1, False)
                step(ITERS - 1, 0, False)
                step(ITERS - 1, 1, False, last=True)
                row(ITERS - 1, 1, 1, 2, False)
                row(ITERS - 1, 1, 1, 3, False)

            @block.gpsimd
            def _(pool):
                def step(i, half, first):
                    for k in range(4):
                        slot = 2 * half + k // 2
                        if k % 2 == 0:
                            pool.wait_ge(q.extras_ready, 4 * i + slot + 1)
                            pool.wait_ge(q.sidx_fed, 4 * i + slot + 1)
                        pool.wait_ge(q.row_ready, 8 * i + 4 * half + k + 1)
                        hold(pool, q.passed)
                        pool.indirect_dma_start(sums[:, :], bass.IndirectOffsetOnAxis(ap=sidx[:, half, k:k + 1],
                                                                                      axis=0),
                                                rows[:, half, k, :], None, bounds_check=ROWS - 1, oob_is_err=False
                                                ).then_inc(stored[slot], 16)

                over_halves(pool, step)
                for slot in range(4):
                    pool.wait_ge(stored[slot], 32 * ITERS)

        fixup(nc, s, f"weigh_fix{layer}", sums, rows[:, 1, 3, :], D, banks)


def gat_nodes(nc, s, layer, x_rows, sums, x_next, att_ends, x_first, out):
    last = layer == LAYERS - 1
    with ExitStack() as ctx:
        def sb(name, shape, dt=F32):
            return ctx.enter_context(nc.sbuf_tensor(f"{name}_{layer}", shape, dt))

        def pb(name, shape):
            return ctx.enter_context(nc.psum_tensor(f"{name}_{layer}", shape, F32))

        xs = sb("gx", [P, 2, 4, D + HEADS])
        ss = sb("gs", [P, 2, 4, W])
        firsts = sb("gf", [P, 2, 4, D + HEADS])
        own = sb("own", [P, 2, 4, HEADS])
        y = sb("y", [P, 2, 4, D])
        x_t = sb("gx_t", [P, 2, BLOCK])
        normal = sb("gnormal", [P, 2, 4, D])
        y_t = sb("gy_t", [P, BLOCK])
        total = sb("gtotal", [P, 2, 4, D])
        new = sb("gnew", [P, 2, 4, D + HEADS])
        new_t = sb("gnew_t", [P, BLOCK])
        node_att = sb("gatt", [P, 2, 4, 2 * HEADS])
        places = sb("gplaces", [P, 2, 4], I32)
        stats = sb("gstats", [P, 4, 6])
        moments = sb("gmoments", [P, 2, 4, 2])
        rstd = sb("grstd", [P, 2, 4])
        p_x = pb("gp_x", [P, BLOCK])
        heads = [pb(f"gp_h{c}", [P, BLOCK]) for c in range(4)]
        p_y = pb("gp_y", [P, BLOCK])
        p_skip = pb("gp_skip", [P, 4, D])
        p_tail = pb("gp_tail", [P, BLOCK])
        own_steps = 2
        back_steps = 2 + MOMENT_STEPS if last else 1
        stores = 1 if last else STORES

        with phase(nc, f"gat{layer}", "loaded_a", "loaded_b", "sums_a", "sums_b", "turned", "copied", "own_step", "headed",
                   "summed", "y_turned", "y_copied", "skipped", "step", "rstd_ready", "inverted",
                   "normed", "rows_turned", "rows_copied", "scored", "tail_step", "placed", "first_a", "first_b", "stored_a", "stored_b",
                   "passed"
                   ) as (block, q):
            loaded = [q.loaded_a, q.loaded_b]
            sums_loaded = [q.sums_a, q.sums_b]
            stored = [q.stored_a, q.stored_b]
            first_loaded = [q.first_a, q.first_b]

            @block.sync
            def _(sp):
                def step(j, slot, first):
                    if not first:
                        sp.wait_ge(q.turned, j - 1)
                        hold(sp, q.passed)
                    sp.dma_start(xs[:, slot, :, :], nodes_of(x_rows, start_of(j))).then_inc(loaded[slot], 16)
                    if not first:
                        sp.wait_ge(q.summed, 16 * (j - 1))
                        hold(sp, q.passed)
                    sp.dma_start(ss[:, slot, :, :], nodes_of(sums, start_of(j))).then_inc(sums_loaded[slot], 16)
                    if last:
                        load_first(j, slot, first)

                def load_first(j, slot, first):
                    if not first:
                        sp.wait_ge(q.step, back_steps * (j - 1))
                        hold(sp, q.passed)
                    sp.dma_start(firsts[:, slot, :, :], nodes_of(x_first, start_of(j))
                                 ).then_inc(first_loaded[slot], 16)

                over_blocks(sp, step)

            @block.gpsimd
            def _(pool):
                def store(j, slot):
                    if not last:
                        store_rows(pool, q, stored, new, node_att, places, x_next, att_ends, j, slot)
                        return
                    pool.wait_ge(q.normed, 4 * (j + 1))
                    if is_block(j, NBLOCKS - 1):
                        pool.wait_ge(stored[0], 8 * NBLOCKS)
                        pool.wait_ge(stored[1], 8 * (NBLOCKS - 2))
                    pool.dma_start(nodes_of(out, start_of(j)), normal[:, slot]).then_inc(stored[slot], 16)

                def step(j, slot, first):
                    if not first:
                        store(j - 2, slot)

                over_blocks(pool, step)
                store(NBLOCKS - 2, 0)
                store(NBLOCKS - 1, 1)
                for slot in range(2):
                    pool.wait_ge(stored[slot], 8 * stores * NBLOCKS)

            @block.tensor
            def _(pe):
                def turn(j, slot):
                    loads_done(pe, loaded[slot], j, slot, 1)
                    if not is_block(j, 0):
                        pe.wait_ge(q.copied, j)
                    for c in range(4):
                        mm = nc.tensor.transpose(p_x[:, c * P:(c + 1) * P], xs[:, slot, c, 0:D], s.ident[:, :])
                    mm.then_inc(q.turned, 1)

                def turn_y(j, slot, very_first):
                    pe.wait_ge(q.summed, 16 * j + 16)
                    if not very_first:
                        pe.wait_ge(q.y_copied, j)
                    for c in range(4):
                        mm = nc.tensor.transpose(p_y[:, c * P:(c + 1) * P], y[:, slot, c, :], s.ident[:, :])
                    mm.then_inc(q.y_turned, 1)

                def skip(j, very_first):
                    pe.wait_ge(q.y_copied, j + 1)
                    if not very_first:
                        pe.wait_ge(q.step, back_steps * (j - 1) + 1)
                    for c in range(4):
                        mm = nc.tensor.matmul(p_skip[:, c, :], y_t[:, c * P:(c + 1) * P], s.skip_w[:, layer, :],
                                              start=True, stop=True)
                    mm.then_inc(q.skipped, 1)

                def turn_tail(j, slot):
                    if not last:
                        turn_rows(nc, s, q, pe, p_tail, new, j, slot)

                def tail(j):
                    if not last:
                        score_rows(nc, s, q, pe, p_tail, new_t, layer + 1, j)

                def step(j, slot, first):
                    very_first = first and slot == 0
                    pe.wait_ge(q.copied, j + 1)
                    for c in range(4):
                        if c == 2 and not very_first:
                            turn_y(j - 1, 1 - slot, is_block(j, 1))
                        if c == 3 and not first:
                            turn_tail(j - 2, slot)
                        if not very_first:
                            pe.wait_ge(q.summed, 16 * (j - 1) + 8 * (c // 2) + 7 + c % 2)
                        nc.tensor.matmul(heads[c][:, :], x_t[:, slot, c * P:(c + 1) * P], s.gat_w[:, layer, :],
                                         start=True, stop=True).then_inc(q.headed, 1)
                    if not is_block(j, NBLOCKS - 1):
                        turn(j + 1, 1 - slot)
                    if not first:
                        tail(j - 2)
                    if not very_first:
                        skip(j - 1, is_block(j, 1))

                turn(0, 0)
                over_blocks(pe, step)
                turn_y(NBLOCKS - 1, 1, False)
                turn_tail(NBLOCKS - 2, 0)
                tail(NBLOCKS - 2)
                skip(NBLOCKS - 1, False)
                turn_tail(NBLOCKS - 1, 1)
                tail(NBLOCKS - 1)

            @block.scalar
            def _(act):
                def copy_x(j, slot, first):
                    act.wait_ge(q.turned, j + 1)
                    if not first:
                        act.wait_ge(q.headed, 4 * (j - 1))
                    nc.scalar.copy(x_t[:, slot, :], p_x[:, :]).then_inc(q.copied, 1)

                def copy_y(j, very_first):
                    act.wait_ge(q.y_turned, j + 1)
                    if not very_first:
                        act.wait_ge(q.skipped, j)
                    nc.scalar.copy(y_t[:, :], p_y[:, :]).then_inc(q.y_copied, 1)

                def tail(j, slot):
                    if last:
                        deviation(nc, s, q, act, moments, rstd, j, slot, back_steps)
                    else:
                        copy_rows(nc, q, act, p_tail, new_t, j)

                def step(j, slot, first):
                    if last and not first:
                        tail(j - 2, slot)
                    if not (first and slot == 0):
                        copy_y(j - 1, is_block(j, 1))
                    if not last and not first:
                        tail(j - 2, slot)
                    if not is_block(j, NBLOCKS - 1):
                        copy_x(j + 1, 1 - slot, is_block(j, 0))

                copy_x(0, 0, True)
                over_blocks(act, step)
                if last:
                    tail(NBLOCKS - 2, 0)
                copy_y(NBLOCKS - 1, False)
                if not last:
                    tail(NBLOCKS - 2, 0)
                tail(NBLOCKS - 1, 1)

            @block.vector
            def _(dve):
                v = nc.vector

                def back(j, slot, first):
                    dve.wait_ge(q.skipped, j + 1)
                    if last and not first:
                        dve.wait_ge(q.normed, 4 * (j - 1))
                    steps = Steps(dve, q.step, back_steps * j, q.passed)
                    steps.then(v.tensor_tensor(total[:, slot], p_skip[:, :, :], over_features(s.skip_b[:, layer, :]),
                                               ALU.add))
                    steps.wait()
                    if last:
                        loads_done(dve, first_loaded[slot], j, slot, 1)
                        steps.then(v.tensor_tensor(total[:, slot], total[:, slot], firsts[:, slot, :, 0:D], ALU.add))
                        steps.wait()
                        row_moments(nc, steps, total[:, slot], stats, moments[:, slot])
                    else:
                        if not first:
                            dve.wait_ge(stored[slot], 8 * STORES * (j - slot))
                        feed_places(nc, s, q, dve, places, j, slot)
                        v.tensor_scalar(new[:, slot, :, 0:D], total[:, slot], 0.0, None, ALU.max
                                        ).then_inc(q.normed, 4)

                def tail(j, slot, first):
                    if last:
                        if not first:
                            dve.wait_ge(stored[slot], 8 * (j - slot))
                        normalise(nc, q, dve, total[:, slot], normal[:, slot], moments, rstd, j, slot)
                        return
                    dve.wait_ge(q.scored, j + 1)
                    steps = Steps(dve, q.tail_step, HEAD_STEPS * j)
                    head_rows(nc, s, steps, p_tail[:, 0:32].rearrange("p (c k) -> p c k", c=4), new, node_att, slot)

                def step(j, slot, first):
                    very_first = first and slot == 0
                    loads_done(dve, sums_loaded[slot], j, slot, 1)
                    if not first:
                        dve.wait_ge(q.summed, 16 * (j - 1))
                    flag = ss[:, slot, :, D + HEADS:D + HEADS + 1].to_broadcast([P, 4, HEADS])
                    v.tensor_scalar(own[:, slot], flag, -1.0 / HEADS, 1.0 / HEADS, ALU.mult, ALU.add
                                    ).then_inc(q.own_step, 1)
                    dve.wait_ge(q.own_step, own_steps * j + 1)
                    v.tensor_tensor(own[:, slot], own[:, slot], ss[:, slot, :, D:D + HEADS], ALU.add
                                    ).then_inc(q.own_step, 1)
                    dve.wait_ge(q.own_step, own_steps * j + 2)
                    if not first:
                        dve.wait_ge(q.y_turned, j - 1)
                    for pair in range(2):
                        done = 16 * j + 8 * pair
                        for h in range(HEADS):
                            for c in (2 * pair, 2 * pair + 1):
                                if h:
                                    dve.wait_ge(q.summed, done + 2 * (h - 1) + c % 2 + 1)
                                else:
                                    dve.wait_ge(q.headed, 4 * j + c + 1)
                                v.scalar_tensor_tensor(y[:, slot, c, :], heads[c][:, h * D:(h + 1) * D],
                                                       own[:, slot, c, h:h + 1],
                                                       y[:, slot, c, :] if h else ss[:, slot, c, 0:D],
                                                       ALU.mult, ALU.add
                                                       ).then_inc(q.summed, 1)
                    if not first:
                        tail(j - 2, slot, is_block(j, 2) or is_block(j, 3))
                    if not very_first:
                        back(j - 1, 1 - slot, is_block(j, 1) or is_block(j, 2))

                over_blocks(dve, step)
                tail(NBLOCKS - 2, 0, False)
                back(NBLOCKS - 1, 1, False)
                tail(NBLOCKS - 1, 1, False)


def build(nc, x, src, dst, w, out):
    def dram(name, shape, dt=F32):
        return nc.dram_tensor(name, shape, dt).ap()

    half_sorted = dram("half_sorted", (SLOTS, 2), I32)
    sorted_pairs = dram("sorted_pairs", (SLOTS, 2), I32)
    sums_in = dram("sums_in", (ROWS, W))
    sums_out = dram("sums_out", (ROWS, W))
    turned_x = dram("turned_x", (HALVES * P, BLOCK))
    x_rows = [dram(f"x_rows{l}", (N, D + HEADS)) for l in range(LAYERS)]
    att_ends = dram("att_ends", (SLOTS, 2 * HEADS))

    with ExitStack() as ctx:
        def sb(name, shape, dt=F32):
            return ctx.enter_context(nc.sbuf_tensor(name, shape, dt))

        s = Buffers()
        s.ident = sb("ident", [P, P])
        s.lower = sb("lower", [P, P])
        s.upper = sb("upper", [P, P])
        s.upper_in = sb("upper_in", [P, P])
        s.lower_in = sb("lower_in", [P, P])
        s.ones = sb("ones", [P, P])
        s.eps = sb("eps", [P, 1])
        s.iota256 = sb("iota256", [P, 256])
        s.dummy = sb("dummy_row", [P, 1])
        s.upper_b = sb("upper_b", [P, P], BF16)
        s.lower_in_b = sb("lower_in_b", [P, P], BF16)
        s.ones_b = sb("ones_b", [P, P], BF16)
        s.iota256_b = sb("iota256_b", [P, 256], BF16)
        s.disorder = sb("disorder", [1, 1], I32)
        s.pairs = sb("pairs", [P, T, 2], I32)
        s.source = sb("source", [P, T])
        s.gather_rows = sb("gather_rows", [P, T, 2], I32)
        s.scatter_rows = sb("scatter_rows", [P, T], I32)
        s.same = sb("same", [P, T])
        s.same_in = sb("same_in", [P, T])
        s.reset = sb("reset", [P, T])
        s.reset_in = sb("reset_in", [P, T])
        s.ends = sb("ends", [P, T])
        s.goes_on = sb("goes_on", [P, T])
        s.position = sb("position", [P, T])
        s.end_places = sb("end_places", [P, NBLOCKS * 4])
        s.fix_rows = sb("fix_rows", [P, 2], I32)
        s.mask_first = sb("mask_first", [P, P])
        s.mask_last = sb("mask_last", [P, P])
        s.chunk_same = sb("chunk_same", [HEADS, P])
        s.chunk_goes_on = sb("chunk_goes_on", [2 * HEADS, P])
        s.chunk_reset = sb("chunk_reset", [HEADS, P])
        s.w_edge = sb("w_edge", [P, 2, 2 * D])
        s.w_msg2 = sb("w_msg2", [P, 2, D])
        s.b_edge = sb("b_edge", [P, 2 * D])
        s.b_msg2 = sb("b_msg2", [2, D])
        s.upd1 = sb("upd1", [P, 2, U])
        s.upd2 = sb("upd2", [P, 2, D])
        s.upd_b1 = sb("upd_b1", [P, 2])
        s.upd_b2 = sb("upd_b2", [P, D])
        s.gat_w = sb("gat_w", [P, LAYERS, HEADS * D])
        s.skip_w = sb("skip_w", [P, LAYERS, D])
        s.skip_b = sb("skip_b", [P, LAYERS, D])
        s.w_att = sb("w_att", [P, LAYERS, 2 * HEADS])
        make_constants(nc, s)
        with zero_tables(nc, (sums_in, sums_out, att_ends)):
            load_weights(nc, s, w)
            with ExitStack() as sorting:
                def tmp(name, shape, dt=F32):
                    return sorting.enter_context(nc.sbuf_tensor(name, shape, dt))

                s.digit_i, s.digits = tmp("digit_i", [P, T], I32), tmp("digits", [P, T])
                s.totals, s.base = tmp("totals", [P, 256]), tmp("base", [P, 256])
                s.picked, s.rank_ring = tmp("picked", [P, 256]), tmp("rank_ring", [P, 8])
                s.ranks, s.place = tmp("ranks", [P, T]), tmp("place", [P, T], I32)
                s.place_hi, s.place_ring = tmp("place_hi", [P, T], I32), tmp("place_ring", [P, 2, 4], I32)
                s.pair_ring = tmp("pair_ring", [P, 2, 4, 2], I32)
                load_edges(nc, s, src, dst)
                disorder = find_disorder(nc, s, sorted_pairs)
                with nc.If(disorder > 0):
                    nc.all_engine_barrier()
                    sort_edges(nc, s, half_sorted, sorted_pairs)
            plan_segments(nc, s, sorted_pairs)
        message_edges(nc, s, x, sums_in, sums_out)
        update_nodes(nc, s, x, sums_in, sums_out, x_rows[0], att_ends)
        for layer in range(LAYERS):
            with nc.sbuf_tensor(f"edge_weights{layer}", [P, HEADS + 1, T], F32) as weights, \
                    nc.sbuf_tensor(f"self_weights{layer}", [P, T, HEADS], F32) as self_weights:
                s.weights, s.self_weights = weights, self_weights
                with nc.sbuf_tensor(f"edge_score{layer}", [P, HEADS, T], F32) as edge_score, \
                        nc.sbuf_tensor(f"self_score{layer}", [P, HEADS, T], F32) as self_score:
                    s.edge_score, s.self_score = edge_score, self_score
                    score_edges(nc, s, layer, x_rows[layer], turned_x)
                    add_destinations(nc, s, layer, att_ends)
                    attention_weights(nc, s, layer)
                weigh_edges(nc, s, layer, turned_x, sums_in)
            after = min(layer + 1, LAYERS - 1)
            gat_nodes(nc, s, layer, x_rows[layer], sums_in, x_rows[after], att_ends, x_rows[0], out)


_INS = ["x", "src", "dst", "L0_gnn_msg_W1", "L0_gnn_msg_b1", "L0_gnn_msg_W2", "L0_gnn_msg_b2", "L0_gnn_rev_W1",
        "L0_gnn_rev_b1", "L0_gnn_rev_W2", "L0_gnn_rev_b2", "L0_gnn_upd_W1", "L0_gnn_upd_b1", "L0_gnn_upd_W2",
        "L0_gnn_upd_b2", "L1_gnn_W", "L1_gnn_att_src", "L1_gnn_att_dst", "L1_gnn_bias", "L1_gnn_skip_W",
        "L1_gnn_skip_b"]


def program(nc, shapes):
    args = {name: nc.dram_tensor(f"in_{name}", shape, dt, kind="ExternalInput").ap()
            for name, (shape, dt) in shapes.items()}
    out = nc.dram_tensor("out", (N, D), F32, kind="ExternalOutput").ap()
    w = {name[7:]: ap for name, ap in args.items() if name.startswith("L0_gnn_")}
    w |= {"gat_W": args["L1_gnn_W"], "gat_bias": args["L1_gnn_bias"], "skip_W": args["L1_gnn_skip_W"],
          "skip_b": args["L1_gnn_skip_b"], "att_src": args["L1_gnn_att_src"], "att_dst": args["L1_gnn_att_dst"]}
    build(nc, args["x"], args["src"], args["dst"], w, out)


def kernel(**inputs):
    import numpy as np
    import concourse.bacc as bacc
    from concourse.bass_utils import run_bass_kernel_spmd

    nc = bacc.Bacc("TRN2", target_bir_lowering=False, num_devices=1)
    arrays = {name: np.ascontiguousarray(inputs[name]) for name in _INS}
    program(nc, {name: (a.shape, mybir.dt.from_np(a.dtype)) for name, a in arrays.items()})
    r = run_bass_kernel_spmd(nc, [{f"in_{name}": a for name, a in arrays.items()}], core_ids=[0])
    return r.results[0]["out"]
```
